# Optimizing a Trainium2 kernel written in Bass

```python
import numpy as np
import jax
import jax.numpy as jnp

def _softmax(x, axis=-1):
    return jax.nn.softmax(x, axis=axis)

def _gelu(x):
    return jax.nn.gelu(x, approximate=True)

def _silu(x):
    return jax.nn.silu(x)

def _sigmoid(x):
    return jax.nn.sigmoid(x)

def _layernorm(x, axis=-1, eps=1e-05):
    m = jnp.mean(x, axis=axis, keepdims=True)
    v = jnp.var(x, axis=axis, keepdims=True)
    return (x - m) / jnp.sqrt(v + eps)

def _scatter_add(tgt, idx, src, axis=0):
    return tgt.at[idx].add(src)

def _segment_sum(src, seg, n):
    return jax.ops.segment_sum(src, seg, n)
kernel_name = 'mk_lm_tower_d2_tok_ids256_r4_816751'

def setup_inputs(seed: int=0):
    np.random.seed(seed)
    _w = jnp.asarray

    def _rec_inputs():
        import jax
        import jax.numpy as jnp
        _rk = jax.random.key(seed)
        x = jax.random.randint(jax.random.fold_in(_rk, 1), (32, 128), 0, 250, jnp.int32)
        return x
    x = _rec_inputs()

    def _L0_tok_setup():
        import jax, jax.numpy as jnp
        import numpy as np
        B, T, H, VOCAB = (128, 128, 64, 250)
        EPS = 1e-12

        def _pos_graph(seq_inputs):
            si = seq_inputs[:, :, None]
            mask = si != 0
            equal = si == si.transpose(0, 2, 1)
            tril = jnp.tril(jnp.ones((si.shape[1], si.shape[1]), dtype=jnp.float32))
            rel = equal.astype(jnp.float32) * tril
            rel = rel * mask.astype(jnp.float32) * mask.transpose(0, 2, 1).astype(jnp.float32)
            norm = rel.sum(-2, keepdims=True)
            norm = jnp.where(norm == 0, 1.0, norm)
            return rel / norm

        def _get_pos_emb(seq_inputs, emb_table):
            seq_mask = seq_inputs != 0
            length = seq_mask.sum(1, keepdims=True)
            coo = jnp.arange(seq_inputs.shape[1])[None, :] * seq_mask
            pos_index = (length - coo) * seq_mask
            return emb_table[pos_index]
        key = jax.random.key(seed)
        k1, k2, k3, k4 = jax.random.split(key, 4)
        stdv = 1.0 / np.sqrt(H)
        seq_inputs = jax.random.randint(k1, (B, T), 0, VOCAB, dtype=jnp.int64 if jax.config.jax_enable_x64 else jnp.int32)
        emb_table = jax.random.normal(k2, (T + 1, H), dtype=jnp.float32)
        W_in = jax.random.uniform(k3, (H, H), minval=-stdv, maxval=stdv, dtype=jnp.float32)
        b_oah = jax.random.uniform(k4, (H,), minval=-stdv, maxval=stdv, dtype=jnp.float32)
        return {'seq_inputs': seq_inputs, 'emb_table': emb_table, 'W_in': W_in, 'b_oah': b_oah}
    _L0_tok_all = _L0_tok_setup()
    _L0_tok_in = {k: v for k, v in _L0_tok_all.items() if k in ('emb_table', 'W_in', 'b_oah')}
    del _L0_tok_all

    def _L0_attn_setup():
        import jax, jax.numpy as jnp
        import numpy as np
        PI = np.pi
        key = jax.random.key(seed)
        ks = jax.random.split(key, 24)
        B, L, D, P, H, MAXL = (1, 512, 64, 32, 4, 4096)
        Dh = D // 2
        n = lambda k, s, sc=0.02: (jax.random.normal(k, s) * sc).astype(jnp.float32)
        z = lambda s: jnp.zeros(s, jnp.float32)
        return {'x': n(ks[0], (B, L, D), 1.0), 'pos_phases': n(ks[1], (MAXL, P), PI), 'window_deltas': jnp.arange(-2, 3, dtype=jnp.float32), 'mc_w': n(ks[2], (D, D)), 'mc_b': z((D,)), 'hop_w1': n(ks[3], (D + P, D)), 'hop_b1': z((D,)), 'hop_w2': n(ks[4], (D, H * (P + 1))), 'hop_b2': z((H * (P + 1),)), 'cpe_w': n(ks[5], (D, P)), 'cpe_b': z((P,)), 've_w': n(ks[6], (D, D)), 've_b': z((D,)), 'kce_w': n(ks[7], (D, D)), 'kce_b': z((D,)), 'ksk_w1': n(ks[8], (2 * D, D)), 'ksk_b1': z((D,)), 'ksk_w2': n(ks[9], (D, P)), 'ksk_b2': z((P,)), 'sg_w1': n(ks[10], (D, Dh)), 'sg_b1': z((Dh,)), 'sg_w2': n(ks[11], (Dh, 1)), 'sg_b2': z((1,)), 'ln_g': jnp.ones((D,), jnp.float32), 'ln_b': z((D,)), 'out_w': n(ks[12], (D, D)), 'out_b': z((D,))}
    _L0_attn_all = _L0_attn_setup()
    _L0_attn_in = {k: v for k, v in _L0_attn_all.items() if k in ('pos_phases', 'window_deltas', 'mc_w', 'mc_b', 'hop_w1', 'hop_b1', 'hop_w2', 'hop_b2', 'cpe_w', 'cpe_b', 've_w', 've_b', 'kce_w', 'kce_b', 'ksk_w1', 'ksk_b1', 'ksk_w2', 'ksk_b2', 'sg_w1', 'sg_b1', 'sg_w2', 'sg_b2', 'ln_g', 'ln_b', 'out_w', 'out_b')}
    del _L0_attn_all

    def _L0_ffn_setup():
        import jax, jax.numpy as jnp
        import numpy as np
        D_IN, D_HID, D_OUT = (64, 128, 64)
        N_EXPERTS, TOP_K = (64, 2)
        B, S = (8, 1024)
        key = jax.random.key(seed)
        ks = jax.random.split(key, 8)
        scale_in = 1.0 / np.sqrt(D_IN)
        scale_hid = 1.0 / np.sqrt(D_HID)
        return {'x': jax.random.normal(ks[0], (B, S, D_IN), dtype=jnp.float32), 'Wr': jax.random.uniform(ks[1], (D_IN, N_EXPERTS), jnp.float32, -scale_in, scale_in), 'br': jax.random.uniform(ks[2], (N_EXPERTS,), jnp.float32, -scale_in, scale_in), 'W1': jax.random.uniform(ks[3], (N_EXPERTS, D_IN, D_HID), jnp.float32, -scale_in, scale_in), 'b1': jax.random.uniform(ks[4], (N_EXPERTS, D_HID), jnp.float32, -scale_in, scale_in), 'W2': jax.random.uniform(ks[5], (N_EXPERTS, D_HID, D_OUT), jnp.float32, -scale_hid, scale_hid), 'b2': jax.random.uniform(ks[6], (N_EXPERTS, D_OUT), jnp.float32, -scale_hid, scale_hid)}
    _L0_ffn_all = _L0_ffn_setup()
    _L0_ffn_in = {k: v for k, v in _L0_ffn_all.items() if k in ('Wr', 'br', 'W1', 'b1', 'W2', 'b2')}
    del _L0_ffn_all

    def _L1_attn_setup():
        import jax, jax.numpy as jnp
        import numpy as np
        GROUPS = 4
        key = jax.random.key(seed)
        k1, k2, k3, k4 = jax.random.split(key, 4)
        B, S, D, H = (4, 1024, 64, 10)
        return {'x': jax.random.normal(k1, (B, S, D), dtype=jnp.float32), 'Wq': jax.random.normal(k2, (H, D, D), dtype=jnp.float32) * 0.02, 'Wk': jax.random.normal(k3, (H, D, D), dtype=jnp.float32) * 0.02, 'Wo': jax.random.normal(k4, (D, H * D), dtype=jnp.float32) * 0.02}
    _L1_attn_all = _L1_attn_setup()
    _L1_attn_in = {k: v for k, v in _L1_attn_all.items() if k in ('Wq', 'Wk', 'Wo')}
    del _L1_attn_all

    def _L1_ffn_setup():
        import jax, jax.numpy as jnp
        import numpy as np
        E = 8
        K = 2
        D = 64
        H = 128
        DOUT = 64
        EPS = 1e-05
        key = jax.random.key(seed)
        ks = jax.random.split(key, 9)
        s = 0.02
        return {'x': jax.random.normal(ks[0], (4, 2048, D), jnp.float32), 'gamma': 1.0 + 0.05 * jax.random.normal(ks[1], (D,), jnp.float32), 'beta': 0.05 * jax.random.normal(ks[2], (D,), jnp.float32), 'Wr': 0.01 * jax.random.normal(ks[3], (D, E), jnp.float32), 'br': jnp.zeros((E,), jnp.float32), 'W1': s * jax.random.normal(ks[4], (E, D, H), jnp.float32), 'b1': s * jax.random.normal(ks[5], (E, H), jnp.float32), 'W2': s * jax.random.normal(ks[6], (E, H, DOUT), jnp.float32), 'b2': s * jax.random.normal(ks[7], (E, DOUT), jnp.float32)}
    _L1_ffn_all = _L1_ffn_setup()
    _L1_ffn_in = {k: v for k, v in _L1_ffn_all.items() if k in ('gamma', 'beta', 'Wr', 'br', 'W1', 'b1', 'W2', 'b2')}
    del _L1_ffn_all
    return {'x': x, 'L0_tok_emb_table': _L0_tok_in['emb_table'], 'L0_tok_W_in': _L0_tok_in['W_in'], 'L0_tok_b_oah': _L0_tok_in['b_oah'], 'L0_attn_pos_phases': _L0_attn_in['pos_phases'], 'L0_attn_window_deltas': _L0_attn_in['window_deltas'], 'L0_attn_mc_w': _L0_attn_in['mc_w'], 'L0_attn_mc_b': _L0_attn_in['mc_b'], 'L0_attn_hop_w1': _L0_attn_in['hop_w1'], 'L0_attn_hop_b1': _L0_attn_in['hop_b1'], 'L0_attn_hop_w2': _L0_attn_in['hop_w2'], 'L0_attn_hop_b2': _L0_attn_in['hop_b2'], 'L0_attn_cpe_w': _L0_attn_in['cpe_w'], 'L0_attn_cpe_b': _L0_attn_in['cpe_b'], 'L0_attn_ve_w': _L0_attn_in['ve_w'], 'L0_attn_ve_b': _L0_attn_in['ve_b'], 'L0_attn_kce_w': _L0_attn_in['kce_w'], 'L0_attn_kce_b': _L0_attn_in['kce_b'], 'L0_attn_ksk_w1': _L0_attn_in['ksk_w1'], 'L0_attn_ksk_b1': _L0_attn_in['ksk_b1'], 'L0_attn_ksk_w2': _L0_attn_in['ksk_w2'], 'L0_attn_ksk_b2': _L0_attn_in['ksk_b2'], 'L0_attn_sg_w1': _L0_attn_in['sg_w1'], 'L0_attn_sg_b1': _L0_attn_in['sg_b1'], 'L0_attn_sg_w2': _L0_attn_in['sg_w2'], 'L0_attn_sg_b2': _L0_attn_in['sg_b2'], 'L0_attn_ln_g': _L0_attn_in['ln_g'], 'L0_attn_ln_b': _L0_attn_in['ln_b'], 'L0_attn_out_w': _L0_attn_in['out_w'], 'L0_attn_out_b': _L0_attn_in['out_b'], 'L0_ffn_Wr': _L0_ffn_in['Wr'], 'L0_ffn_br': _L0_ffn_in['br'], 'L0_ffn_W1': _L0_ffn_in['W1'], 'L0_ffn_b1': _L0_ffn_in['b1'], 'L0_ffn_W2': _L0_ffn_in['W2'], 'L0_ffn_b2': _L0_ffn_in['b2'], 'L1_attn_Wq': _L1_attn_in['Wq'], 'L1_attn_Wk': _L1_attn_in['Wk'], 'L1_attn_Wo': _L1_attn_in['Wo'], 'L1_ffn_gamma': _L1_ffn_in['gamma'], 'L1_ffn_beta': _L1_ffn_in['beta'], 'L1_ffn_Wr': _L1_ffn_in['Wr'], 'L1_ffn_br': _L1_ffn_in['br'], 'L1_ffn_W1': _L1_ffn_in['W1'], 'L1_ffn_b1': _L1_ffn_in['b1'], 'L1_ffn_W2': _L1_ffn_in['W2'], 'L1_ffn_b2': _L1_ffn_in['b2']}

def reference(x, L0_tok_emb_table, L0_tok_W_in, L0_tok_b_oah, L0_attn_pos_phases, L0_attn_window_deltas, L0_attn_mc_w, L0_attn_mc_b, L0_attn_hop_w1, L0_attn_hop_b1, L0_attn_hop_w2, L0_attn_hop_b2, L0_attn_cpe_w, L0_attn_cpe_b, L0_attn_ve_w, L0_attn_ve_b, L0_attn_kce_w, L0_attn_kce_b, L0_attn_ksk_w1, L0_attn_ksk_b1, L0_attn_ksk_w2, L0_attn_ksk_b2, L0_attn_sg_w1, L0_attn_sg_b1, L0_attn_sg_w2, L0_attn_sg_b2, L0_attn_ln_g, L0_attn_ln_b, L0_attn_out_w, L0_attn_out_b, L0_ffn_Wr, L0_ffn_br, L0_ffn_W1, L0_ffn_b1, L0_ffn_W2, L0_ffn_b2, L1_attn_Wq, L1_attn_Wk, L1_attn_Wo, L1_ffn_gamma, L1_ffn_beta, L1_ffn_Wr, L1_ffn_br, L1_ffn_W1, L1_ffn_b1, L1_ffn_W2, L1_ffn_b2):
    import jax
    import jax.numpy as jnp

    def _L0_tok_ref(seq_inputs, emb_table, W_in, b_oah):
        import jax, jax.numpy as jnp
        import numpy as np
        B, T, H, VOCAB = (128, 128, 64, 250)
        EPS = 1e-12

        def _pos_graph(seq_inputs):
            si = seq_inputs[:, :, None]
            mask = si != 0
            equal = si == si.transpose(0, 2, 1)
            tril = jnp.tril(jnp.ones((si.shape[1], si.shape[1]), dtype=jnp.float32))
            rel = equal.astype(jnp.float32) * tril
            rel = rel * mask.astype(jnp.float32) * mask.transpose(0, 2, 1).astype(jnp.float32)
            norm = rel.sum(-2, keepdims=True)
            norm = jnp.where(norm == 0, 1.0, norm)
            return rel / norm

        def _get_pos_emb(seq_inputs, emb_table):
            seq_mask = seq_inputs != 0
            length = seq_mask.sum(1, keepdims=True)
            coo = jnp.arange(seq_inputs.shape[1])[None, :] * seq_mask
            pos_index = (length - coo) * seq_mask
            return emb_table[pos_index]
        step = 1
        A_in = _pos_graph(seq_inputs)
        pe = _get_pos_emb(seq_inputs, emb_table)
        nrm = jnp.sqrt(jnp.sum(pe * pe, axis=1, keepdims=True))
        pe = pe / jnp.maximum(nrm, EPS)
        for _ in range(step):
            h_n = jnp.einsum('bth,oh->bto', pe, W_in)
            pe = jnp.einsum('bji,bjh->bih', A_in, h_n) + b_oah
        return pe

    def _L0_attn_ref(x, pos_phases, window_deltas, mc_w, mc_b, hop_w1, hop_b1, hop_w2, hop_b2, cpe_w, cpe_b, ve_w, ve_b, kce_w, kce_b, ksk_w1, ksk_b1, ksk_w2, ksk_b2, sg_w1, sg_b1, sg_w2, sg_b2, ln_g, ln_b, out_w, out_b):
        import jax, jax.numpy as jnp
        import numpy as np
        PI = np.pi
        B, L, D = x.shape
        P = cpe_w.shape[1]
        H = hop_b2.shape[0] // (P + 1)
        gelu = lambda t: jax.nn.gelu(t, approximate=False)
        sqrtP = jnp.sqrt(jnp.float32(P))
        pp = pos_phases[:L]
        pos_cos, pos_sin = (jnp.cos(pp), jnp.sin(pp))
        content = x @ mc_w + mc_b
        mem1_cos = jnp.cumsum(pos_cos[None, :, :, None] * content[:, :, None, :], axis=1)
        mem1_sin = jnp.cumsum(pos_sin[None, :, :, None] * content[:, :, None, :], axis=1)
        off_in = jnp.concatenate([x, jnp.broadcast_to(pp[None], (B, L, P))], axis=-1)
        ao = (gelu(off_in @ hop_w1 + hop_b1) @ hop_w2 + hop_b2).reshape(B, L, H, P + 1)
        center = jnp.tanh(ao[..., :P]) * PI
        width = jax.nn.sigmoid(ao[..., -1:]) * 2 + 0.1
        Wn = window_deltas.shape[0]
        deltas = window_deltas.reshape(1, 1, 1, Wn)
        weights = jnp.exp(-0.5 * deltas ** 2 / (width ** 2 + 1e-06))
        off_ph = center[:, :, :, None, :] + deltas[..., None] * 0.1
        oc, os_ = (jnp.cos(off_ph), jnp.sin(off_ph))
        pce = pos_cos.reshape(1, L, 1, 1, P)
        pse = pos_sin.reshape(1, L, 1, 1, P)
        qc = (pce * oc - pse * os_).reshape(B, L, H * Wn, P)
        qs = (pse * oc + pce * os_).reshape(B, L, H * Wn, P)
        retrieved = (jnp.einsum('blpd,blhp->blhd', mem1_cos, qc) + jnp.einsum('blpd,blhp->blhd', mem1_sin, qs)) / sqrtP
        retrieved = retrieved.reshape(B, L, H, Wn, D)
        ws = (retrieved * weights[..., None]).sum(axis=3)
        head_out = ws / (weights.sum(axis=3, keepdims=True) + 1e-06)
        mh_out = head_out.mean(axis=2)
        key_ph = jnp.tanh(x @ cpe_w + cpe_b) * PI
        key_cos, key_sin = (jnp.cos(key_ph), jnp.sin(key_ph))
        values = x @ ve_w + ve_b
        gate = jax.nn.sigmoid(gelu(x @ sg_w1 + sg_b1) @ sg_w2 + sg_b2)
        ctx = jnp.cumsum(x @ kce_w + kce_b, axis=1)
        pos = jnp.arange(1, L + 1, dtype=x.dtype).reshape(1, L, 1)
        storage_in = jnp.concatenate([x, ctx / pos], axis=-1)
        st_ph = jnp.tanh(gelu(storage_in @ ksk_w1 + ksk_b1) @ ksk_w2 + ksk_b2) * PI
        sc, ss = (jnp.cos(st_ph), jnp.sin(st_ph))
        gv = values[:, :, None, :] * gate[..., None]
        kv_cos = jnp.cumsum(sc[..., None] * gv, axis=1)
        kv_sin = jnp.cumsum(ss[..., None] * gv, axis=1)
        gate_cum = jnp.clip(jnp.cumsum(gate, axis=1), 1.0, None)
        kv_ret = (kv_cos * key_cos[..., None] + kv_sin * key_sin[..., None]).sum(axis=2)
        kv_ret = kv_ret / (jnp.sqrt(gate_cum) * sqrtP)
        combined = mh_out + kv_ret
        mu = combined.mean(-1, keepdims=True)
        var = combined.var(-1, keepdims=True)
        lnx = (combined - mu) / jnp.sqrt(var + 1e-05) * ln_g + ln_b
        return x + (lnx @ out_w + out_b)

    def _L0_ffn_ref(x, Wr, br, W1, b1, W2, b2):
        import jax, jax.numpy as jnp
        import numpy as np
        D_IN, D_HID, D_OUT = (64, 128, 64)
        N_EXPERTS, TOP_K = (64, 2)
        B, S = (8, 1024)
        Bx, Sx, D = x.shape
        xf = x.reshape(-1, D)
        T = xf.shape[0]
        E = Wr.shape[1]
        logits = xf @ Wr + br
        topk_logits, topk_idx = jax.lax.top_k(logits, TOP_K)
        gates = jax.nn.softmax(topk_logits, axis=1)
        combine = jnp.zeros((T, E), xf.dtype).at[jnp.arange(T)[:, None], topk_idx].add(gates)
        out = jnp.zeros((T, W2.shape[-1]), xf.dtype)
        for e in range(E):
            h = jax.nn.relu(xf @ W1[e] + b1[e])
            y = h @ W2[e] + b2[e]
            out = out + combine[:, e:e + 1] * y
        return out.reshape(Bx, Sx, -1)

    def _L1_attn_ref(x, Wq, Wk, Wo):
        import jax, jax.numpy as jnp
        import numpy as np
        GROUPS = 4
        H, D, _ = Wq.shape
        B, S, _ = x.shape
        G = GROUPS
        C = S // G
        Q = jnp.einsum('bsd,hde->hbse', x, Wq)
        K = jnp.einsum('bsd,hde->hbse', x, Wk)
        Qg = Q.reshape(H, B, G, C, D)
        KVg = jnp.roll(K.reshape(H, B, G, C, D), shift=-1, axis=2)
        S_ = jnp.einsum('hbgqd,hbgkd->hbgqk', Qg, KVg)
        P = jax.nn.softmax(S_, axis=-1)
        O = jnp.einsum('hbgqk,hbgkd->hbgqd', P, KVg)
        out = O.reshape(H, B, S, D).transpose(1, 2, 0, 3).reshape(B, S, H * D)
        return jnp.einsum('bsk,dk->bsd', out, Wo)

    def _L1_ffn_ref(x, gamma, beta, Wr, br, W1, b1, W2, b2):
        import jax, jax.numpy as jnp
        import numpy as np
        E = 8
        K = 2
        D = 64
        H = 128
        DOUT = 64
        EPS = 1e-05
        mu = jnp.mean(x, axis=-1, keepdims=True)
        var = jnp.mean(jnp.square(x - mu), axis=-1, keepdims=True)
        xn = (x - mu) * jax.lax.rsqrt(var + EPS) * gamma + beta
        logits = jnp.einsum('bsd,de->bse', xn, Wr) + br
        top_vals, top_idx = jax.lax.top_k(logits, K)
        w = jax.nn.softmax(top_vals, axis=-1)
        w_full = jnp.einsum('bsk,bske->bse', w, jax.nn.one_hot(top_idx, E, dtype=w.dtype))
        y = jnp.zeros(x.shape[:-1] + (DOUT,), x.dtype)
        for e in range(E):
            h = jax.nn.gelu(jnp.einsum('bsd,dh->bsh', xn, W1[e]) + b1[e], approximate=False)
            y_e = jnp.einsum('bsh,hd->bsd', h, W2[e]) + b2[e]
            y = y + y_e * w_full[..., e, None]
        return y
    h = _L0_tok_ref(x, L0_tok_emb_table, L0_tok_W_in, L0_tok_b_oah)
    h = h + _L0_attn_ref(_layernorm(h, axis=-1), L0_attn_pos_phases, L0_attn_window_deltas, L0_attn_mc_w, L0_attn_mc_b, L0_attn_hop_w1, L0_attn_hop_b1, L0_attn_hop_w2, L0_attn_hop_b2, L0_attn_cpe_w, L0_attn_cpe_b, L0_attn_ve_w, L0_attn_ve_b, L0_attn_kce_w, L0_attn_kce_b, L0_attn_ksk_w1, L0_attn_ksk_b1, L0_attn_ksk_w2, L0_attn_ksk_b2, L0_attn_sg_w1, L0_attn_sg_b1, L0_attn_sg_w2, L0_attn_sg_b2, L0_attn_ln_g, L0_attn_ln_b, L0_attn_out_w, L0_attn_out_b)
    h = h + _L0_ffn_ref(_layernorm(h, axis=-1), L0_ffn_Wr, L0_ffn_br, L0_ffn_W1, L0_ffn_b1, L0_ffn_W2, L0_ffn_b2)
    h = h + _L1_attn_ref(_layernorm(h, axis=-1), L1_attn_Wq, L1_attn_Wk, L1_attn_Wo)
    h = h + _L1_ffn_ref(_layernorm(h, axis=-1), L1_ffn_gamma, L1_ffn_beta, L1_ffn_Wr, L1_ffn_br, L1_ffn_W1, L1_ffn_b1, L1_ffn_W2, L1_ffn_b2)
    return h

_drawn_inputs = setup_inputs


def setup_inputs(seed=0):
    import zlib

    import numpy as np

    out = dict(_drawn_inputs(seed))
    spreads = {'L0_attn_mc_b': (0.0, 0.1),
     'L0_attn_hop_b1': (0.0, 0.8),
     'L0_attn_hop_b2': (0.0, 0.623),
     'L0_attn_cpe_b': (0.0, 0.8),
     'L0_attn_ve_b': (0.0, 0.1),
     'L0_attn_kce_b': (0.0, 0.8),
     'L0_attn_ksk_b1': (0.0, 0.8),
     'L0_attn_ksk_b2': (0.0, 0.8),
     'L0_attn_sg_b1': (0.0, 0.8),
     'L0_attn_ln_g': (1.0, 0.2),
     'L0_attn_ln_b': (0.0, 0.298),
     'L0_attn_out_b': (0.0, 0.1),
     'L1_ffn_br': (0.0, 0.718)}
    factors = {'L0_attn_window_deltas': 64.0,
     'L0_attn_hop_w1': 8.0,
     'L0_attn_hop_w2': 8.0,
     'L0_attn_cpe_w': 8.0,
     'L0_attn_kce_w': 8.0,
     'L0_attn_ksk_w1': 8.0,
     'L0_attn_ksk_w2': 8.0,
     'L0_attn_sg_w1': 8.0,
     'L0_attn_sg_w2': 8.0,
     'L0_ffn_b1': 3.287,
     'L1_attn_Wq': 8.0,
     'L1_ffn_gamma': 8.0,
     'L1_ffn_beta': 8.0,
     'L1_ffn_Wr': 4.661,
     'L1_ffn_W1': 5.477,
     'L1_ffn_b1': 8.0,
     'L1_ffn_W2': 5.122,
     'L1_ffn_b2': 14.151}
    for name, (base, spread) in spreads.items():
        noise = np.random.default_rng([zlib.crc32(name.encode()), seed]).standard_normal(out[name].shape)
        drawn = base * np.exp(spread * noise) if base else spread * noise
        out[name] = jnp.asarray(drawn.astype(out[name].dtype))
    for name, factor in factors.items():
        out[name] = (out[name] * factor).astype(out[name].dtype)
    return out
```

```python
import numpy as np
from contextlib import ExitStack

import concourse.bass as bass
from concourse import mybir

F32 = mybir.dt.float32
BF16 = mybir.dt.bfloat16
I32 = mybir.dt.int32
U32 = mybir.dt.uint32
ALU = mybir.AluOpType
ACT = mybir.ActivationFunctionType
AX = mybir.AxisListType

B, T, D = 32, 128, 64
CH = 4
NCH = B // CH
W = CH * T
NPOS = T + 1
P = 32
NH = 4
NW = 5
HP = P + 1
E0, E1, HID = 64, 8, 128
GH, GG, GC = 10, 4, 32
NPAR = GH // 2
EPS = 1e-5

AO, ST, GT, KY, CT, VL = 0, NH * HP, NH * HP + P, NH * HP + P + 1, NH * HP + 2 * P + 1, NH * HP + 2 * P + 1 + D
NPROJ = VL + D

PI_BELOW = float(np.nextafter(np.float32(np.pi), np.float32(0)))
HALF_PI = float(np.float32(np.pi / 2))
TWO_PI_PARTS = [6.28125, float(np.float32(2 * np.pi - 6.28125)),
                float(2 * np.pi - 6.28125 - float(np.float32(2 * np.pi - 6.28125)))]
ROUND = 12582912.0


class Store:
    pass


class Steps:

    def __init__(self, S, sem, per_turn=0):
        self.S, self.looped, self.sem, self.per_turn, self.n, self.marks = S, per_turn > 0, sem, per_turn, 0, {}

    def start(self, eng, turn=0):
        self.eng, self.base, self.n = eng, turn * self.per_turn, 0

    def done(self, ins):
        ins.then_inc(self.sem, 1)
        self.n += 1

    def wait(self):
        if self.looped:
            hold(self.S, self.eng, self.sem, self.base + self.n)
        else:
            self.eng.wait_ge(self.sem, self.n)

    def do(self, ins):
        self.done(ins)
        self.wait()

    def mark(self, name):
        self.marks[name] = self.n

    def end(self):
        assert self.n == self.per_turn, f"{self.n} steps a turn"

    def after(self, eng, name, turn=0):
        if self.looped:
            hold(self.S, eng, self.sem, turn * self.per_turn + self.marks[name])
        else:
            eng.wait_ge(self.sem, self.marks[name])


def hold(S, eng, sem, value):
    eng.wait_ge(sem, value)
    eng.sem_inc(S.waits[eng.engine], 1)


def bc(ap, shape):
    return ap.to_broadcast(shape)


def col(ap):
    return ap.rearrange("(p o) -> p o", o=1)


def setup_stage(nc, S, A):
    with ExitStack() as ctx:
        sb = lambda n, s, d=F32: ctx.enter_context(nc.sbuf_tensor(n, s, d))
        sem = lambda n: ctx.enter_context(nc.semaphore(n))
        x_row = sb("x_row", [B, T], I32)
        w_in = sb("w_in", [D, D])
        emb_last = sb("emb_last", [3, D])
        emb_rest = sb("emb_rest", [128, 2, D])
        last_part = sb("last_part", [3, 3, D], BF16)
        last_rest = sb("last_rest", [3, 2, D])
        emb_low = sb("emb_low", [128, D])
        kce_w = sb("kce_w", [D, D])
        kce_wT = sb("kce_wT", [D, D])
        ksk_low = sb("ksk_low", [D, D])
        kce_b = sb("kce_b", [D, 1])
        ksk_b1 = sb("ksk_b1", [128, 1])
        ln_g = sb("ln_g", [128, 1])
        ln_b = sb("ln_b", [D, 1])
        ln_bb = sb("ln_bb", [D, 128])
        out_w = sb("out_w", [128, D])
        out_b = sb("out_b", [128, D])
        wq = sb("wq", [D, GH, D])
        wk = sb("wk", [D, GH, D])
        wo = sb("wo", [D, GH, D])
        wqT = sb("wqT", [128, NPAR, D])
        wkT = sb("wkT", [128, NPAR, D])
        woT = sb("woT", [128, NPAR, D])
        pp = sb("pp", [T, P])
        ang = sb("ang", [T, P + NW])
        turns = sb("turns", [T, P + NW])
        absa = sb("absa", [T, P + NW])
        sincos = sb("sincos", [T, 2, P + NW])
        pdup = sb("pdup", [T, 2, 2, P])
        seq_len = sb("seq_len", [B, 1])
        mask_row = sb("mask_row", [B, T])
        idx_row = sb("idx_row", [B, T])
        neg_row = sb("neg_row", [B, T])
        idx_bf = sb("idx_bf", [B, T], BF16)
        rec_row = sb("rec_row", [128, 128])
        triS_f = sb("triS_f", [128, 128])
        xT_i = sb("xT_i", [T, B], I32)

        weights_in = sem("weights_in")
        weights_in2 = sem("weights_in_by_pool")
        early_in = sem("early_in")
        idx_out = sem("idx_out")
        idx_back = sem("idx_back")
        masks_made = sem("masks_made")
        dve_done = sem("setup_dve_done")
        act_done = sem("setup_act_done")
        pe_done = sem("setup_pe_done")
        pool_done = sem("setup_pool_done")
        zeroed = sem("rows_zeroed")

        early = [(x_row[:, :], A["x"]), (S.x_bc[:, :].rearrange("p (b t) -> p b t", b=B), A["x"].partition_broadcast(128)),
                 (S.emb[:, :], A["emb"][0:T, :]),
                 (emb_last[:, :], A["emb"][T, :].partition_broadcast(3)), (w_in[:, :], A["w_in"]),
                 (pp[:, :], A["phases"][0:T, :]), (ang[:, P:P + NW], A["deltas"].partition_broadcast(T)),
                 (ang[:, 0:P], A["phases"][0:T, :])]
        late = [(S.w1c[0:D, 0:D], A["hop_w1"][0:D, :]), (S.w1p[0:P, 0:D], A["hop_w1"][D:D + P, :]),
                (S.w1c[0:D, D:2 * D], A["ksk_w1"][0:D, :]), (ksk_low[:, :], A["ksk_w1"][D:2 * D, :]),
                (kce_w[:, :], A["kce_w"]), (kce_b[:, :], col(A["kce_b"])), (ksk_b1[D:128, :], col(A["ksk_b1"])),
                (S.b1c[0:D, :], col(A["hop_b1"])), (S.w2c[0:D, 0:ST], A["hop_w2"]), (S.w2c[D:128, ST:GT], A["ksk_w2"]),
                (S.sg_w1[0:D, :], A["sg_w1"]), (S.sg_b1[:, :], col(A["sg_b1"])), (S.sg_w2[:, :], A["sg_w2"]),
                (S.wx[0:D, 0:P], A["cpe_w"]), (S.wx[0:D, P:P + D], A["mc_w"]), (S.wx[0:D, P + D:P + 2 * D], A["ve_w"]),
                (S.proj_b[:, AO:ST], A["hop_b2"].partition_broadcast(128)), (S.proj_b[:, ST:GT], A["ksk_b2"].partition_broadcast(128)),
                (S.proj_b[:, GT:KY], A["sg_b2"].partition_broadcast(128)), (S.proj_b[:, KY:CT], A["cpe_b"].partition_broadcast(128)),
                (S.proj_b[:, CT:VL], A["mc_b"].partition_broadcast(128)), (S.proj_b[:, VL:NPROJ], A["ve_b"].partition_broadcast(128)),
                (ln_g[0:D, :], col(A["ln_g"])), (ln_g[D:128, :], col(A["ln_g"])), (ln_b[:, :], col(A["ln_b"])),
                (out_w[0:D, :], A["out_w"]), (out_w[D:128, :], A["out_w"]), (out_b[:, :], A["out_b"].partition_broadcast(128)),
                (S.b_oah[:, :], A["b_oah"].partition_broadcast(128)),
                (S.wr0[:, :], A["wr0"]), (S.br0[:, :], A["br0"].partition_broadcast(128)),
                (wq[:, :, :], A["wq"].rearrange("h d e -> d h e")), (wk[:, :, :], A["wk"].rearrange("h d e -> d h e")),
                (wo[:, :, :], A["wo"].rearrange("o (h e) -> o h e", e=D)),
                (S.gamma[:, :], col(A["gamma"])), (S.beta[:, :], col(A["beta"])), (S.wr1[:, :], A["wr1"]),
                (S.br1[:, :], A["br1"].partition_broadcast(128)),
                (S.w1_1[0:D, :, :], A["w1_1"].rearrange("e d h -> d e h")), (S.w2_1[:, :, :], A["w2_1"].rearrange("e h d -> h e d")),
                (S.b1_1[:, :], A["b1_1"].rearrange("e h -> h e")), (S.b2_1[:, :], A["b2_1"])]
        n_early, n_late, n_late2 = 16 * len(early), 16 * len(late[0::2]), 16 * len(late[1::2])

        block = ctx.enter_context(nc.Block())

        at = {}

        @block.vector
        def _(dve):
            st = Steps(S, dve_done)
            st.start(dve)
            V, do = nc.vector, st.do

            for t in (S.w1c[D:128, 0:D], S.w1p[0:P, D:128], S.w1p[P:2 * P, :], S.w1p[2 * P:128, :], S.sg_w1[D:128, :], S.wx[D:128, :], S.ppT[P:2 * P, :],
                      S.ppT[2 * P:128, :], S.w2c[0:D, ST:GT], S.w2c[D:128, 0:ST]):
                st.done(V.memset(t, 0.0))
            st.done(V.memset(S.qkT[D:128, :, :, :], 0.0))
            st.done(V.memset(S.w1_1[D:128, :, :], 0.0))
            st.done(V.memset(S.ones_bf[:, :], 1.0))
            st.done(V.memset(S.eps[:, :], EPS))
            st.done(V.memset(S.half_pi[:, :], HALF_PI))
            for r in range(2):
                st.done(V.memset(S.hn[:, r, :, D:D + 1], 1.0))
            dve.wait_ge(early_in, n_early)
            dve.wait_ge(masks_made, 3)
            do(V.tensor_scalar(mask_row[:, :], x_row[:, :], 0.0, None, ALU.not_equal))
            do(V.reduce_sum(seq_len[:, :], mask_row[:, :], AX.X))
            do(V.tensor_scalar(idx_row[:, :], S.iota_free[0:B, :], -1.0, seq_len[:, 0:1], ALU.mult, ALU.add))
            do(V.tensor_tensor(idx_row[:, :], idx_row[:, :], mask_row[:, :], ALU.mult))
            do(V.tensor_scalar(neg_row[:, :], idx_row[:, :], 0.0, float(NPOS), ALU.is_lt, ALU.mult))
            do(V.tensor_tensor(idx_bf[:, :], idx_row[:, :], neg_row[:, :], ALU.add))
            at['idx'] = st.n
            for k in range(4):
                st.done(V.transpose(xT_i[32 * k:32 * k + 32, :], x_row[:, 32 * k:32 * k + 32]))
            st.wait()
            st.done(V.tensor_copy(S.xT[:, :], xT_i[:, :]))
            do(V.tensor_scalar(S.maskT[:, :], xT_i[:, :], 0.0, None, ALU.not_equal))
            do(V.tensor_copy(S.emb3[:, 0, :], S.emb[:, :]))
            do(V.tensor_tensor(emb_rest[:, 0, :], S.emb[:, :], S.emb3[:, 0, :], ALU.subtract))
            do(V.tensor_copy(S.emb3[:, 1, :], emb_rest[:, 0, :]))
            do(V.tensor_tensor(emb_rest[:, 1, :], emb_rest[:, 0, :], S.emb3[:, 1, :], ALU.subtract))
            do(V.tensor_copy(S.emb3[:, 2, :], emb_rest[:, 1, :]))
            do(V.tensor_copy(last_part[:, 0, :], emb_last[:, :]))
            do(V.tensor_tensor(last_rest[:, 0, :], emb_last[:, :], last_part[:, 0, :], ALU.subtract))
            do(V.tensor_copy(last_part[:, 1, :], last_rest[:, 0, :]))
            do(V.tensor_tensor(last_rest[:, 1, :], last_rest[:, 0, :], last_part[:, 1, :], ALU.subtract))
            do(V.tensor_copy(last_part[:, 2, :], last_rest[:, 1, :]))
            do(V.tensor_scalar(emb_low[0:3, :], last_part[:, 0, :], S.ident[0:3, 0:1], None, ALU.mult))
            for k in (1, 2):
                do(V.scalar_tensor_tensor(emb_low[0:3, :], last_part[:, k, :], S.ident[0:3, k:k + 1],
                                          emb_low[0:3, :], ALU.mult, ALU.add))
            do(V.tensor_copy(S.emb_last3[:, :], emb_low[0:3, :]))
            do(V.tensor_copy(S.triS[:, :], triS_f[:, :]))
            do(V.tensor_scalar(rec_row[:, :], S.iota_free[:, :], 1.0, None, ALU.add))
            do(V.reciprocal(rec_row[:, :], rec_row[:, :]))
            do(V.tensor_tensor(S.cmean[:, :], rec_row[:, :], S.triC[:, :], ALU.mult))
            do(V.tensor_tensor(S.nhd2[:, :], ang[:, P:P + NW], ang[:, P:P + NW], ALU.mult))
            do(V.tensor_scalar(S.nhd2[:, :], S.nhd2[:, :], -0.5, None, ALU.mult))
            do(V.tensor_scalar(ang[:, P:P + NW], ang[:, P:P + NW], 0.1, None, ALU.mult))
            do(V.tensor_scalar(turns[:, :], ang[:, :], float(1 / (2 * np.pi)), ROUND, ALU.mult, ALU.add))
            do(V.tensor_scalar(turns[:, :], turns[:, :], -ROUND, None, ALU.add))
            for c in TWO_PI_PARTS:
                do(V.scalar_tensor_tensor(ang[:, :], turns[:, :], -c, ang[:, :], ALU.mult, ALU.add))
            do(V.tensor_scalar(ang[:, :], ang[:, :], PI_BELOW, -PI_BELOW, ALU.min, ALU.max))
            at['angle'] = st.n
            dve.wait_ge(act_done, 3)
            st.done(V.tensor_copy(S.pcs[:, :, :], sincos[:, :, 0:P]))
            st.done(V.tensor_copy(S.dcs[:, :, :], sincos[:, :, P:P + NW]))
            for k in range(2):
                st.done(V.tensor_copy(pdup[:, k, :, :], sincos[:, :, 0:P]))
            at['pdup'] = st.n
            dve.wait_ge(weights_in, n_late)
            dve.wait_ge(weights_in2, n_late2)
            st.done(V.tensor_scalar(S.out_w2[:, :], out_w[:, :], ln_g[:, 0:1], None, ALU.mult))
            st.done(V.tensor_copy(ln_bb[:, :], bc(ln_b[:, 0:1], [D, 128])))
            at['lnbb'] = st.n
            dve.wait_ge(pe_done, 1)
            st.done(V.tensor_copy(S.w_inT[:, :], S.ps[0][0:D, 0:D]))
            st.done(V.tensor_copy(kce_wT[:, :], S.ps[0][0:D, 128:128 + D]))
            st.done(V.tensor_copy(S.pcsT[:, :], S.ps[0][:, 256:384]))
            st.done(V.tensor_copy(S.ppT[0:P, :], S.ps[0][0:P, 384:512]))
            for n, dst in enumerate((wqT, wkT, woT)):
                st.done(V.tensor_copy(dst[:, :, :], S.ps[1 + n][:, 0:NPAR * D].rearrange("p (n d) -> p n d", d=D)))
            at['wT'] = st.n
            dve.wait_ge(pe_done, 2)
            st.done(V.tensor_copy(S.w1c[D:128, D:128], S.ps[0][D:128, 0:D]))
            st.done(V.tensor_tensor(S.b1c[D:128, :], S.ps[0][D:128, 64:65], ksk_b1[D:128, :], ALU.add))
            st.done(V.tensor_tensor(S.out_row[:, :], S.ps[7][:, 0:D], out_b[:, :], ALU.add))
            for par in range(2):
                st.done(V.tensor_copy(S.qkT[0:D, :, par, :], S.ps[1 + par][0:D, 0:NPAR * D].rearrange("p (n d) -> p n d", d=D)))
            for half in range(2):
                st.done(V.tensor_copy(S.wv[64 * half:64 * half + 64, :, :],
                                      S.ps[3 + half][64 * half:64 * half + 64, 0:NPAR * D].rearrange("p (n d) -> p n d", d=D)))

        @block.sync
        def _(sp):
            for dst, src in early:
                sp.dma_start(dst, src, allow_slow_non_contiguous=True).then_inc(early_in, 16)
            for dst, src in late[0::2]:
                sp.dma_start(dst, src, allow_slow_non_contiguous=True).then_inc(weights_in, 16)
            sp.wait_ge(dve_done, at['idx'])
            sp.dma_start(A["idx_scratch"], idx_bf[:, :]).then_inc(idx_out, 16)
            sp.wait_ge(idx_out, 16)
            sp.dma_start(S.idx_bc[:, :].rearrange("p (b t) -> p b t", b=B),
                         A["idx_scratch"].partition_broadcast(128)).then_inc(idx_back, 16)
            sp.wait_ge(idx_back, 16)
            sp.wait_ge(masks_made, 2)
            for r in range(0, S.slots, 128 * 32):
                sp.dma_start(A["slot_x"][r:r + 128 * 32, :].rearrange("(p n) d -> p n d", p=128),
                             S.zeros[:, :].rearrange("p (n d) -> p n d", d=D)).then_inc(zeroed, 16)
            sp.wait_ge(zeroed, 16 * (S.slots // 4096))

        @block.gpsimd
        def _(pool):
            nc.gpsimd.memset(S.ident[:, :], 0.0)
            nc.gpsimd.memset(S.triG[:, :], 1.0)
            nc.gpsimd.memset(S.triC[:, :], 1.0)
            nc.gpsimd.memset(triS_f[:, :], 1.0)
            nc.gpsimd.iota(S.iota_free[:, :], [[1, 128]], base=0, channel_multiplier=0, allow_small_or_imprecise_dtypes=True)
            nc.gpsimd.iota(S.iota_part[:, :], [[0, 1]], base=0, channel_multiplier=1,
                           allow_small_or_imprecise_dtypes=True).then_inc(masks_made, 1)
            nc.gpsimd.memset(S.zeros[:, :], 0.0).then_inc(masks_made, 1)
            pool.wait_ge(masks_made, 1)
            sel = nc.gpsimd.affine_select
            sel(out=S.ident[:, :], in_=S.ident[:, :], compare_op=ALU.not_equal, fill=1.0, base=0,
                pattern=[[-1, 128]], channel_multiplier=1)
            sel(out=S.triG[:, :], in_=S.triG[:, :], compare_op=ALU.is_ge, fill=0.0, base=0,
                pattern=[[-1, 128]], channel_multiplier=1)
            sel(out=S.triC[:, :], in_=S.triC[:, :], compare_op=ALU.is_ge, fill=0.0, base=0,
                pattern=[[1, 128]], channel_multiplier=-1)
            sel(out=triS_f[:, :], in_=triS_f[:, :], compare_op=ALU.is_gt, fill=0.0, base=0,
                pattern=[[1, 128]], channel_multiplier=-1).then_inc(masks_made, 1)
            for dst, src in late[1::2]:
                pool.dma_start(dst, src, allow_slow_non_contiguous=True).then_inc(weights_in2, 16)

        @block.scalar
        def _(act):
            act.wait_ge(dve_done, at['angle'])
            nc.scalar.activation(sincos[:, 1, :], ang[:, :], ACT.Sin).then_inc(act_done, 1)
            nc.scalar.activation(absa[:, :], ang[:, :], ACT.Abs).then_inc(act_done, 1)
            act.wait_ge(act_done, 2)
            nc.scalar.activation(sincos[:, 0, :], absa[:, :], ACT.Sin, bias=S.half_pi[:, 0:1], scale=-1.0).then_inc(act_done, 1)

        @block.tensor
        def _(pe):
            M = nc.tensor.matmul
            pe.wait_ge(weights_in, n_late)
            pe.wait_ge(weights_in2, n_late2)
            pe.wait_ge(masks_made, 3)
            pe.wait_ge(dve_done, at['lnbb'])
            idn = S.ident
            nc.tensor.transpose(S.ps[0][0:D, 0:D], w_in[:, :], idn[0:D, 0:D])
            nc.tensor.transpose(S.ps[0][0:D, 128:128 + D], kce_w[:, :], idn[0:D, 0:D])
            nc.tensor.transpose(S.ps[0][:, 256:384], pdup[:, :, :, :].rearrange("p a b c -> p (a b c)"), idn[:, :])
            nc.tensor.transpose(S.ps[0][0:P, 384:512], pp[:, :], idn[:, :])
            for n, src in enumerate((wq, wk, wo)):
                for k in range(NPAR):
                    last = nc.tensor.transpose(S.ps[1 + n][:, D * k:D * k + D],
                                               src[:, 2 * k:2 * k + 2, :].rearrange("p a b -> p (a b)"), idn[0:D, 0:D])
            last.then_inc(pe_done, 1)
            pe.wait_ge(dve_done, at['wT'])
            M(S.ps[0][D:128, 0:D], kce_wT[:, :], ksk_low[:, :], start=True, stop=True)
            M(S.ps[0][D:128, 64:65], ksk_low[:, :], kce_b[:, :], start=True, stop=True)
            M(S.ps[7][:, 0:D], ln_bb[:, :], out_w[0:D, :], start=True, stop=True)
            for par in range(2):
                rows = slice(64 * par, 64 * par + 64)
                for k in range(NPAR):
                    M(S.ps[1 + par][0:D, D * k:D * k + D], wkT[rows, k, :], wqT[rows, k, :], start=True, stop=True)
                    last = M(S.ps[3 + par][rows, D * k:D * k + D], wkT[rows, k, :], woT[rows, k, :], start=True, stop=True)
            last.then_inc(pe_done, 1)


def layer_norm_stats(nc, S, st, dve, i, rooted):
    V = nc.vector
    two = bass.ds(i * (2 * CH), 2 * CH)
    for k in range(2 * CH):
        st.done(V.bn_stats(S.stats[:, k, :], S.h[:, bass.ds(i * (2 * CH) + k, 1), :].rearrange("p a d -> p (a d)")))
    st.wait()
    for k in range(2 * CH):
        st.done(V.bn_aggr(S.mv[:, k, :], S.stats[:, k, :]))
    st.mark("variance")
    st.wait()
    hold(S, dve, rooted, i + 1)
    st.done(V.tensor_copy(S.mean[:, two], S.mv[:, :, 0]))
    st.done(V.tensor_copy(S.var[:, two], S.mv[:, :, 1]))
    st.do(V.reciprocal(S.rstd[:, two], S.dev[:, :]))


def token_stage(nc, S, A):
    with ExitStack() as ctx:
        sb = lambda n, s, d=F32: ctx.enter_context(nc.sbuf_tensor(n, s, d))
        sem = lambda n: ctx.enter_context(nc.semaphore(n))
        onehot = sb("onehot", [128, 2, W], BF16)
        onehot_last = sb("onehot_last", [3, 2, W], BF16)
        differ = sb("differ", [128, 2, CH, T], I32)
        graph = sb("graph", [128, 2, CH, T])
        pe_sb = sb("pe_sb", [D, 2, CH, T])
        pe_sq = sb("pe_sq", [D, 2, CH, T])
        pe_n = sb("pe_n", [D, 2, CH, T])
        ssq = sb("ssq", [D, 2, CH])
        nrm = sb("nrm", [D, 2, CH])
        wgt = sb("wgt", [128, 2, CH])

        embedded = sem("embedded")
        squared = sem("squared")
        rooted = sem("rooted")
        projected = sem("projected")
        h_copied = sem("hn_copied")
        rooted_h = sem("h_rooted")
        gathered = sem("gathered")
        st = Steps(S, sem("token_steps"), 41)

        block = ctx.enter_context(nc.Block())

        @block.vector
        def _(dve):
            V = nc.vector
            with dve.Fori(0, NCH // 2) as i:
                st.start(dve, i)
                for r in range(2):
                    tok = bass.ds(i * (2 * W) + r * W, W)
                    tiles = bass.ds(i * (2 * CH) + r * CH, CH)
                    st.done(V.tensor_scalar(onehot[:, r, :], S.idx_bc[:, tok], S.iota_part[:, 0:1], None, ALU.is_equal))
                    st.done(V.tensor_scalar(onehot_last[:, r, :], S.idx_bc[0:3, tok], float(T), None, ALU.is_equal))
                    st.mark(("one-hot", r))
                    st.done(V.tensor_tensor(differ[:, r, :, :], S.x_bc[:, tok].rearrange("p (b t) -> p b t", t=T),
                                            bc(S.xT[:, tiles].unsqueeze(2), [128, CH, T]), ALU.bitwise_xor))
                st.wait()
                for r in range(2):
                    st.done(V.scalar_tensor_tensor(graph[:, r, :, :], differ[:, r, :, :], 0.0,
                                                   bc(S.triG[:, :].unsqueeze(1), [128, CH, T]), ALU.is_equal, ALU.mult))
                for r in range(2):
                    hold(S, dve, squared, i * 4 + 2 * r + 2)
                    st.done(V.reduce_sum(ssq[:, r, :], pe_sq[:, r, :, :], AX.X))
                st.mark("summed")
                hold(S, dve, rooted, i + 1)
                st.do(V.tensor_scalar(nrm[:, :, :], nrm[:, :, :], 1e-12, None, ALU.max))
                st.do(V.reciprocal(nrm[:, :, :], nrm[:, :, :]))
                for r in range(2):
                    st.done(V.tensor_tensor(pe_n[:, r, :, :], pe_sb[:, r, :, :],
                                            bc(nrm[:, r, :].unsqueeze(2), [D, CH, T]), ALU.mult))
                    st.mark(("normed", r))
                for r in range(2):
                    tiles = bass.ds(i * (2 * CH) + r * CH, CH)
                    out = S.ps[4 + r][:, 0:CH * (D + 1)].rearrange("p (k d) -> p k d", d=D + 1)
                    hc = S.h[:, tiles, :]
                    hold(S, dve, gathered, i * 2 + r + 1)
                    st.do(V.reciprocal(wgt[:, r, :], out[:, :, D]))
                    st.do(V.tensor_tensor(wgt[:, r, :], wgt[:, r, :], S.maskT[:, tiles], ALU.mult))
                    st.do(V.tensor_tensor(hc, out[:, :, 0:D], bc(wgt[:, r, :].unsqueeze(2), [128, CH, D]), ALU.mult))
                    st.do(V.tensor_tensor(hc, hc, bc(S.b_oah[:, :].unsqueeze(1), [128, CH, D]), ALU.add))
                layer_norm_stats(nc, S, st, dve, i, rooted_h)
                st.end()

        @block.tensor
        def _(pe):
            M = nc.tensor.matmul
            with pe.Fori(0, NCH // 2) as i:
                for r in range(2):
                    st.after(pe, ("one-hot", r), i)
                    for k in range(3):
                        M(S.ps[r][0:D, :], S.emb3[:, k, :], onehot[:, r, :], start=(k == 0), stop=False)
                    M(S.ps[r][0:D, :], S.emb_last3[:, :], onehot_last[:, r, :], start=False, stop=True).then_inc(embedded, 1)
                for r in range(2):
                    st.after(pe, ("normed", r), i)
                    for k in range(CH):
                        last = M(S.ps[2 + r][:, D * k:D * k + D], pe_n[:, r, k, :], S.w_inT[:, :], start=True, stop=True)
                    last.then_inc(projected, 1)
                for r in range(2):
                    hold(S, pe, h_copied, i * 2 + r + 1)
                    for k in range(CH):
                        last = M(S.ps[4 + r][:, (D + 1) * k:(D + 1) * (k + 1)], graph[:, r, k, :], S.hn[:, r, k, :],
                                 start=True, stop=True)
                    last.then_inc(gathered, 1)

        @block.scalar
        def _(act):
            with act.Fori(0, NCH // 2) as i:
                for r in range(2):
                    hold(S, act, embedded, i * 2 + r + 1)
                    src = S.ps[r][0:D, :].rearrange("p (k t) -> p k t", t=T)
                    nc.scalar.activation(pe_sb[:, r, :, :], src, ACT.Copy).then_inc(squared, 1)
                    nc.scalar.activation(pe_sq[:, r, :, :], src, ACT.Square).then_inc(squared, 1)
                st.after(act, "summed", i)
                nc.scalar.activation(nrm[:, :, :], ssq[:, :, :], ACT.Sqrt).then_inc(rooted, 1)
                for r in range(2):
                    hold(S, act, projected, i * 2 + r + 1)
                    nc.scalar.activation(S.hn[:, r, :, 0:D], S.ps[2 + r][:, 0:CH * D].rearrange("p (k d) -> p k d", d=D),
                                         ACT.Copy).then_inc(h_copied, 1)
                st.after(act, "variance", i)
                nc.scalar.activation(S.dev[:, :], S.mv[:, :, 1], ACT.Sqrt, bias=S.eps[:, 0:1]).then_inc(rooted_h, 1)


def project_stage(nc, S, A):
    with ExitStack() as ctx:
        sb = lambda n, s, d=F32: ctx.enter_context(nc.sbuf_tensor(n, s, d))
        sem = lambda n: ctx.enter_context(nc.semaphore(n))
        xr = sb("xr", [128, 2, CH, D])
        xx = sb("xx", [128, 2, W])
        g1 = sb("g1", [128, 2, W])
        g2 = sb("g2", [D // 2, 2, W])

        turned = sem("x_turned")
        xx_copied = sem("xx_copied")
        hidden = sem("hidden")
        gelued = sem("gelued")
        out_ready = sem("proj_ready")
        added = sem("residual_added")
        st = Steps(S, sem("project_steps"), 6)

        block = ctx.enter_context(nc.Block())

        @block.vector
        def _(dve):
            V = nc.vector
            with dve.Fori(0, NCH // 2) as i:
                st.start(dve, i)
                for r in range(2):
                    tiles = bass.ds(i * (2 * CH) + r * CH, CH)
                    st.do(V.tensor_tensor(xr[:, r, :, :], S.h[:, tiles, :], bc(S.mean[:, tiles].unsqueeze(2), [128, CH, D]),
                                          ALU.subtract))
                    st.do(V.tensor_tensor(xr[:, r, :, :], xr[:, r, :, :], bc(S.rstd[:, tiles].unsqueeze(2), [128, CH, D]),
                                          ALU.mult))
                    st.mark(("x", r))
                for r in range(2):
                    tiles = bass.ds(i * (2 * CH) + r * CH, CH)
                    hold(S, dve, out_ready, i * 2 + r + 1)
                    st.done(V.tensor_tensor(S.proj[:, tiles, :], S.bank[:, 4:8, 0:NPROJ],
                                            bc(S.proj_b[:, :].unsqueeze(1), [128, CH, NPROJ]), ALU.add))
                    st.mark(("proj", r))
                hold(S, dve, added, i * 2 + 2)
                st.end()

        @block.gpsimd
        def _(pool):
            with pool.Fori(0, NCH // 2) as i:
                for r in range(2):
                    tiles = bass.ds(i * (2 * CH) + r * CH, CH)
                    st.after(pool, ("x", r), i)
                    nc.gpsimd.tensor_tensor(S.h[:, tiles, :], S.h[:, tiles, :], xr[:, r, :, :], ALU.add).then_inc(added, 1)

        @block.tensor
        def _(pe):
            M = nc.tensor.matmul
            with pe.Fori(0, NCH // 2) as i:
                for r in range(2):
                    st.after(pe, ("x", r), i)
                    for k in range(CH):
                        nc.tensor.transpose(S.ps[r][0:D, T * k:T * k + T], xr[:, r, k, :], S.ident[:, :])
                        last = M(S.ps[r][D:128, T * k:T * k + T], xr[:, r, k, :], S.cmean[:, :], start=True, stop=True)
                    last.then_inc(turned, 1)
                for r in range(2):
                    hold(S, pe, xx_copied, i * 2 + r + 1)
                    M(S.ps[2 + r][:, :], S.w1c[:, :], xx[:, r, :], start=True, stop=False)
                    M(S.ps[2 + r][:, :].rearrange("p (k t) -> p k t", t=T), S.w1p[:, :], bc(S.ppT[:, :].unsqueeze(1), [128, CH, T]),
                      start=False, stop=True)
                    M(S.ps[r][0:D // 2, :], S.sg_w1[:, :], xx[:, r, :], start=True, stop=True).then_inc(hidden, 1)
                for r in range(2):
                    hold(S, pe, gelued, i * 4 + 2 * r + 2)
                    if r == 1:
                        st.after(pe, ("proj", 0), i)
                    for k in range(CH):
                        t = slice(T * k, T * k + T)
                        M(S.ps[4 + k][:, 0:GT], g1[:, r, t], S.w2c[:, :], start=True, stop=True)
                        M(S.ps[4 + k][:, GT:KY], g2[:, r, t], S.sg_w2[:, :], start=True, stop=True)
                        last = M(S.ps[4 + k][:, KY:NPROJ], xx[:, r, t], S.wx[:, :], start=True, stop=True)
                    last.then_inc(out_ready, 1)

        @block.scalar
        def _(act):
            with act.Fori(0, NCH // 2) as i:
                for r in range(2):
                    hold(S, act, turned, i * 2 + r + 1)
                    nc.scalar.activation(xx[:, r, :], S.ps[r][:, :], ACT.Copy).then_inc(xx_copied, 1)
                for r in range(2):
                    hold(S, act, hidden, i * 2 + r + 1)
                    nc.scalar.activation(g1[:, r, :], S.ps[2 + r][:, :], ACT.Gelu, bias=S.b1c[:, 0:1]).then_inc(gelued, 1)
                    nc.scalar.activation(g2[:, r, :], S.ps[r][0:D // 2, :], ACT.Gelu, bias=S.sg_b1[:, 0:1]).then_inc(gelued, 1)


def phase_stage(nc, S, A):
    NA = (NH + 2) * P
    with ExitStack() as ctx:
        sb = lambda n, s, d=F32: ctx.enter_context(nc.sbuf_tensor(n, s, d))
        sem = lambda n: ctx.enter_context(nc.semaphore(n))
        cosn = sb("cosn", [128, B, NA])
        sinn = sb("sinn", [128, B, NA])
        width = sb("width", [128, B, NH])
        gate = sb("gate", [128, B])
        wexp = sb("wexp", [128, B * NH, NW])
        wprod = sb("wprod", [128, 2, B * NH, NW])
        wsum = sb("wsum", [128, B * NH])
        along = sb("along", [128, 2, B * NH])
        kscale = sb("kscale", [128, B])
        t_c = sb("t_c", [128, 2, 2 * CH, NH * P])
        t_s = sb("t_s", [128, 2, 2 * CH, NH * P])
        r_c = sb("r_c", [128, 2, 2 * CH, P])
        r_s = sb("r_s", [128, 2, 2 * CH, P])

        tanhs = sem("tanhs")
        exped = sem("exped")
        rooted = sem("gate_rooted")
        summed = sem("gates_summed")
        trig = sem("trig")
        sized = sem("sized")
        pre = Steps(S, sem("weights_steps"))
        gated = sem("gated")
        st = Steps(S, sem("phase_steps"), 13)
        ps = Steps(S, sem("phase_pool_steps"), 6)
        sines = sem("sines_summed")

        block = ctx.enter_context(nc.Block())

        def combine(eng, st, t, hop, t4, al, first, second, op):
            st.done(eng.tensor_tensor(t4(t, 0), hop(first[0]), al(first[1]), ALU.mult))
            st.do(eng.tensor_tensor(t4(t, 1), hop(second[0]), al(second[1]), ALU.mult))
            st.do(eng.tensor_tensor(t[:, 0, :, :], t[:, 0, :, :], t[:, 1, :, :], op))
            st.do(eng.tensor_tensor(t[:, 0, :, 0:2 * P], t[:, 0, :, 0:2 * P], t[:, 0, :, 2 * P:4 * P], ALU.add))
            return eng.tensor_tensor(t[:, 0, :, 0:P], t[:, 0, :, 0:P], t[:, 0, :, P:2 * P], ALU.add)

        @block.vector
        def _(dve):
            V = nc.vector
            pre.start(dve)
            do = pre.do
            dve.wait_ge(tanhs, 2)
            do(V.tensor_scalar(gate[:, :], gate[:, :], 0.5, 0.5, ALU.mult, ALU.add))
            pre.mark("gate")
            do(V.tensor_scalar(width[:, :, :], width[:, :, :], 1.1, None, ALU.add))
            do(V.tensor_tensor(width[:, :, :], width[:, :, :], width[:, :, :], ALU.mult))
            do(V.tensor_scalar(width[:, :, :], width[:, :, :], 1e-6, None, ALU.add))
            wv = width[:, :, :].rearrange("p b h -> p (b h)")
            do(V.reciprocal(wv, wv))
            do(V.tensor_tensor(wexp[:, :, :], bc(wv.unsqueeze(2), [128, B * NH, NW]),
                               bc(S.nhd2[:, :].unsqueeze(1), [128, B * NH, NW]), ALU.mult))
            pre.mark("exponents")
            dve.wait_ge(summed, 1)
            do(V.tensor_scalar(kscale[:, :], S.ps[0][:, 0:B], 1.0, None, ALU.max))
            pre.mark("gate sum")
            dve.wait_ge(exped, 1)
            do(V.reduce_sum(wsum[:, :], wexp[:, :, :], AX.X))
            do(V.tensor_scalar(wsum[:, :], wsum[:, :], 1e-6, None, ALU.add))
            do(V.reciprocal(wsum[:, :], wsum[:, :]))
            do(V.tensor_scalar(wsum[:, :], wsum[:, :], 1.0 / (NH * P ** 0.5), None, ALU.mult))
            for k in range(2):
                pre.done(V.tensor_tensor(wprod[:, k, :, :], wexp[:, :, :], bc(S.dcs[:, k, :].unsqueeze(1), [128, B * NH, NW]),
                                         ALU.mult))
            pre.wait()
            for k in range(2):
                pre.done(V.reduce_sum(along[:, k, :], wprod[:, k, :, :], AX.X))
            pre.wait()
            for k in range(2):
                pre.done(V.tensor_tensor(along[:, k, :], along[:, k, :], wsum[:, :], ALU.mult))
            dve.wait_ge(rooted, 1)
            do(V.reciprocal(kscale[:, :], kscale[:, :]))
            do(V.tensor_scalar(kscale[:, :], kscale[:, :], 1.0 / P ** 0.5, None, ALU.mult))
            pre.mark("weights")
            with dve.Fori(0, NCH // 2) as i:
                st.start(dve, i)
                two = bass.ds(i * (2 * CH), 2 * CH)
                hop = lambda t: t[:, two, 0:NH * P].rearrange("p b (h f) -> p b h f", f=P)
                t4 = lambda t, k: t[:, k, :, :].rearrange("p b (h f) -> p b h f", f=P)
                al = lambda k: bc(along[:, k, :].rearrange("p (b h) -> p b h", h=NH)[:, two, :].unsqueeze(3),
                                  [128, 2 * CH, NH, P])
                hold(S, dve, trig, i * 2 + 2)
                st.do(combine(nc.vector, st, t_c, hop, t4, al, (cosn, 0), (sinn, 1), ALU.subtract))
                hold(S, dve, sines, i + 1)
                pc = bc(S.pcs[:, 0, :].unsqueeze(1), [128, 2 * CH, P])
                pn = bc(S.pcs[:, 1, :].unsqueeze(1), [128, 2 * CH, P])
                st.done(V.tensor_tensor(r_c[:, 0, :, :], t_c[:, 0, :, 0:P], pc, ALU.mult))
                st.done(V.tensor_tensor(r_c[:, 1, :, :], t_s[:, 0, :, 0:P], pn, ALU.mult))
                st.done(V.tensor_tensor(r_s[:, 0, :, :], t_c[:, 0, :, 0:P], pn, ALU.mult))
                st.do(V.tensor_tensor(r_s[:, 1, :, :], t_s[:, 0, :, 0:P], pc, ALU.mult))
                st.mark("turned")
                st.done(V.tensor_tensor(S.q_pos[:, two, 0:P], r_c[:, 0, :, :], r_c[:, 1, :, :], ALU.subtract))
                st.done(V.tensor_tensor(S.q_pos[:, two, P:2 * P], r_s[:, 0, :, :], r_s[:, 1, :, :], ALU.add))
                ks = bc(kscale[:, two].unsqueeze(2), [128, 2 * CH, P])
                ky = slice((NH + 1) * P, (NH + 2) * P)
                st.done(V.tensor_tensor(S.q_kv[:, two, 0:P], cosn[:, two, ky], ks, ALU.mult))
                st.done(V.tensor_tensor(S.q_kv[:, two, P:2 * P], sinn[:, two, ky], ks, ALU.mult))
                st.wait()
                st.end()

        @block.gpsimd
        def _(pool):
            G = nc.gpsimd
            pre.after(pool, "gate")
            pool.wait_ge(tanhs, 3)
            G.tensor_tensor(S.gv[:, :, :], S.proj[:, :, VL:NPROJ], bc(gate[:, :].unsqueeze(2), [128, B, D]),
                            ALU.mult).then_inc(gated, 1)
            pre.after(pool, "weights")
            with pool.Fori(0, NCH // 2) as i:
                ps.start(pool, i)
                two = bass.ds(i * (2 * CH), 2 * CH)
                hop = lambda t: t[:, two, 0:NH * P].rearrange("p b (h f) -> p b h f", f=P)
                t4 = lambda t, k: t[:, k, :, :].rearrange("p b (h f) -> p b h f", f=P)
                al = lambda k: bc(along[:, k, :].rearrange("p (b h) -> p b h", h=NH)[:, two, :].unsqueeze(3),
                                  [128, 2 * CH, NH, P])
                hold(S, pool, trig, i * 2 + 2)
                combine(nc.gpsimd, ps, t_s, hop, t4, al, (cosn, 1), (sinn, 0), ALU.add).then_inc(sines, 1)
                so = slice(NH * P, (NH + 1) * P)
                ps.done(G.tensor_copy(S.k_kv[:, two, 0:P], cosn[:, two, so]))
                ps.done(G.tensor_copy(S.k_kv[:, two, P:2 * P], sinn[:, two, so]))
                st.after(pool, "turned", i)
                ps.end()

        @block.tensor
        def _(pe):
            pre.after(pe, "gate")
            nc.tensor.matmul(S.ps[0][:, 0:B], S.triC[:, :], gate[:, :], start=True, stop=True).then_inc(summed, 1)

        @block.scalar
        def _(act):
            N = nc.scalar.activation
            N(width[:, :, :], S.proj[:, :, AO:ST].rearrange("p b (h f) -> p b h f", f=HP)[:, :, :, P], ACT.Tanh,
              scale=0.5).then_inc(tanhs, 1)
            N(gate[:, :], S.proj[:, :, GT], ACT.Tanh, scale=0.5).then_inc(tanhs, 1)
            N(cosn[:, :, 0:NH * P].rearrange("p b (h f) -> p b h f", f=P),
              S.proj[:, :, AO:ST].rearrange("p b (h f) -> p b h f", f=HP)[:, :, :, 0:P], ACT.Tanh)
            N(cosn[:, :, NH * P:(NH + 1) * P], S.proj[:, :, ST:GT], ACT.Tanh)
            N(cosn[:, :, (NH + 1) * P:NA], S.proj[:, :, KY:CT], ACT.Tanh).then_inc(tanhs, 1)
            pre.after(act, "exponents")
            N(wexp[:, :, :], wexp[:, :, :], ACT.Exp).then_inc(exped, 1)
            pre.after(act, "gate sum")
            N(kscale[:, :], kscale[:, :], ACT.Sqrt).then_inc(rooted, 1)
            act.wait_ge(tanhs, 3)
            with act.Fori(0, NCH // 2) as i:
                two = bass.ds(i * (2 * CH), 2 * CH)
                N(sinn[:, two, :], cosn[:, two, :], ACT.Sin, scale=PI_BELOW).then_inc(trig, 1)
                N(cosn[:, two, :], cosn[:, two, :], ACT.Abs).then_inc(sized, 1)
                hold(S, act, sized, i + 1)
                N(cosn[:, two, :], cosn[:, two, :], ACT.Sin, scale=-PI_BELOW, bias=S.half_pi[:, 0:1]).then_inc(trig, 1)


def memory_stage(nc, S, A):
    NPRS = CH // 2
    with ExitStack() as ctx:
        sb = lambda n, s, d=F32: ctx.enter_context(nc.sbuf_tensor(n, s, d))
        sem = lambda n: ctx.enter_context(nc.semaphore(n))
        rows = sb("qk_rows", [128, 2, 3, CH * D])
        qkT = sb("qk_turned", [128, 2, 3, NPRS, T])
        masked = sb("masked", [128, 2, 2, 2 * NPRS, T])
        comb = sb("comb", [128, 2, CH, D])
        combT = sb("combT", [128, 2, NPRS, T])
        stats = sb("comb_stats", [128, 2 * CH, 6])
        mv = sb("comb_mv", [128, 2, CH, 2])
        dev = sb("comb_dev", [128, 2, CH])

        copied = sem("rows_copied")
        turned = sem("qk_turned")
        evacuated = sem("qkT_copied")
        scored = sem("scored")
        retrieved = sem("retrieved")
        rooted = sem("comb_rooted")
        comb_turned = sem("comb_turned")
        combT_copied = sem("combT_copied")
        out_ready = sem("out_ready")
        biased = sem("h_biased")
        rooted_h = sem("h_rooted")
        st = Steps(S, sem("memory_steps"), 4 + 8 + 8 + 1 + 4 + 4 + 19)

        block = ctx.enter_context(nc.Block())

        @block.vector
        def _(dve):
            V = nc.vector
            with dve.Fori(0, NCH // 2) as i:
                st.start(dve, i)
                for r in range(2):
                    hold(S, dve, scored, i * 2 + r + 1)
                    for a in range(2):
                        st.done(V.tensor_tensor(masked[:, r, a, :, :], S.ps[4 + 2 * r + a][:, :].rearrange("p (n t) -> p n t", t=T),
                                                bc(S.triC[:, :].unsqueeze(1), [128, 2 * NPRS, T]), ALU.mult))
                    st.mark(("masked", r))
                for r in range(2):
                    hold(S, dve, retrieved, i * 2 + r + 1)
                    for t in range(CH):
                        st.done(V.bn_stats(stats[:, CH * r + t, :], S.ps[r][:, D * t:D * t + D]))
                st.wait()
                for r in range(2):
                    for t in range(CH):
                        st.done(V.bn_aggr(mv[:, r, t, :], stats[:, CH * r + t, :]))
                st.mark("comb variance")
                hold(S, dve, rooted, i + 1)
                st.do(V.reciprocal(dev[:, :, :], dev[:, :, :]))
                for r in range(2):
                    st.do(V.tensor_tensor(comb[:, r, :, :], S.ps[r][:, 0:CH * D].rearrange("p (k d) -> p k d", d=D),
                                          bc(mv[:, r, :, 0].unsqueeze(2), [128, CH, D]), ALU.subtract))
                    st.do(V.tensor_tensor(comb[:, r, :, :], comb[:, r, :, :], bc(dev[:, r, :].unsqueeze(2), [128, CH, D]),
                                          ALU.mult))
                    st.mark(("comb", r))
                hold(S, dve, biased, i + 1)
                hv = S.h[:, :, :].rearrange("p (n j a) d -> p n a j d", j=NPRS, a=2)
                for r in range(2):
                    hold(S, dve, out_ready, i * 2 + r + 1)
                    for a in range(2):
                        hh = hv[:, bass.ds(i * 2 + r, 1), a, :, :].rearrange("p n j d -> p (n j) d")
                        st.done(V.tensor_tensor(hh, hh, S.ps[4 + 2 * r + a][:, 0:NPRS * D].rearrange("p (j d) -> p j d", d=D),
                                                ALU.add))
                st.wait()
                layer_norm_stats(nc, S, st, dve, i, rooted_h)
                st.end()

        @block.gpsimd
        def _(pool):
            with pool.Fori(0, NCH // 2) as i:
                for r in range(2):
                    tiles = bass.ds(i * (2 * CH) + r * CH, CH)
                    for k, src in enumerate((S.q_pos, S.q_kv, S.k_kv)):
                        nc.gpsimd.tensor_copy(rows[:, r, k, :].rearrange("p (b d) -> p b d", d=D),
                                              src[:, tiles, :]).then_inc(copied, 1)
                two = bass.ds(i * (2 * CH), 2 * CH)
                nc.gpsimd.tensor_tensor(S.h[:, two, :], S.h[:, two, :], bc(S.out_row[:, :].unsqueeze(1), [128, 2 * CH, D]),
                                        ALU.add).then_inc(biased, 1)
                hold(S, pool, turned, i * 2 + 2)

        @block.tensor
        def _(pe):
            M = nc.tensor.matmul
            with pe.Fori(0, NCH // 2) as i:
                for r in range(2):
                    hold(S, pe, copied, i * 6 + 3 * r + 3)
                    for k in range(3):
                        for j in range(NPRS):
                            at = (2 * k + j) * T
                            last = nc.tensor.transpose(S.ps[r if k < 2 else 2 + r][:, at % 512:at % 512 + T],
                                                       rows[:, r, k, 128 * j:128 * j + 128], S.ident[:, :])
                    last.then_inc(turned, 1)
                for r in range(2):
                    hold(S, pe, evacuated, i * 4 + 2 * r + 2)
                    for a in range(2):
                        half = slice(64 * a, 64 * a + 64)
                        M(S.ps[4 + 2 * r + a][:, 0:2 * T], S.pcsT[half, :],
                          qkT[half, r, 0, :, :].rearrange("p j t -> p (j t)"), start=True, stop=True)
                        for j in range(NPRS):
                            last = M(S.ps[4 + 2 * r + a][:, (2 + j) * T:(3 + j) * T], qkT[half, r, 2, j, :],
                                     qkT[half, r, 1, j, :], start=True, stop=True)
                    last.then_inc(scored, 1)
                for r in range(2):
                    st.after(pe, ("masked", r), i)
                    for t in range(CH):
                        j, a = t // 2, t % 2
                        tile = bass.ds(i * (2 * CH) + r * CH + t, 1)
                        M(S.ps[r][:, D * t:D * t + D], masked[:, r, a, j, :],
                          S.proj[:, tile, CT:VL].rearrange("p a d -> p (a d)"), start=True, stop=False)
                        last = M(S.ps[r][:, D * t:D * t + D], masked[:, r, a, 2 + j, :],
                                 S.gv[:, tile, :].rearrange("p a d -> p (a d)"), start=False, stop=True)
                    last.then_inc(retrieved, 1)
                for r in range(2):
                    st.after(pe, ("comb", r), i)
                    for j in range(NPRS):
                        last = nc.tensor.transpose(S.ps[2 + r][:, T * j:T * j + T],
                                                   comb[:, r, 2 * j:2 * j + 2, :].rearrange("p b d -> p (b d)"), S.ident[:, :])
                    last.then_inc(comb_turned, 1)
                for r in range(2):
                    hold(S, pe, combT_copied, i * 2 + r + 1)
                    for a in range(2):
                        half = slice(64 * a, 64 * a + 64)
                        for j in range(NPRS):
                            last = M(S.ps[4 + 2 * r + a][:, D * j:D * j + D], combT[half, r, j, :], S.out_w2[half, :],
                                     start=True, stop=True)
                    last.then_inc(out_ready, 1)

        @block.scalar
        def _(act):
            N = nc.scalar.activation
            with act.Fori(0, NCH // 2) as i:
                for r in range(2):
                    hold(S, act, turned, i * 2 + r + 1)
                    N(qkT[:, r, 0:2, :, :].rearrange("p k j t -> p (k j t)"), S.ps[r][:, :], ACT.Copy).then_inc(evacuated, 1)
                    N(qkT[:, r, 2, :, :].rearrange("p j t -> p (j t)"), S.ps[2 + r][:, 0:2 * T], ACT.Copy).then_inc(evacuated, 1)
                st.after(act, "comb variance", i)
                N(dev[:, :, :], mv[:, :, :, 1], ACT.Sqrt, bias=S.eps[:, 0:1]).then_inc(rooted, 1)
                for r in range(2):
                    hold(S, act, comb_turned, i * 2 + r + 1)
                    N(combT[:, r, :, :].rearrange("p j t -> p (j t)"), S.ps[2 + r][:, 0:2 * T], ACT.Copy).then_inc(combT_copied, 1)
                st.after(act, "variance", i)
                N(S.dev[:, :], S.mv[:, :, 1], ACT.Sqrt, bias=S.eps[:, 0:1]).then_inc(rooted_h, 1)


def normalise(nc, S, st, dst, tiles):
    V = nc.vector
    st.do(V.tensor_tensor(dst, S.h[:, tiles, :], bc(S.mean[:, tiles].unsqueeze(2), [128, CH, D]), ALU.subtract))
    st.do(V.tensor_tensor(dst, dst, bc(S.rstd[:, tiles].unsqueeze(2), [128, CH, D]), ALU.mult))


def route_stage(nc, S, A):
    with ExitStack() as ctx:
        sb = lambda n, s, d=F32: ctx.enter_context(nc.sbuf_tensor(n, s, d))
        sem = lambda n: ctx.enter_context(nc.semaphore(n))
        xr = sb("xr0", [128, 2, CH, D])
        xT = sb("xT0", [D, 2, W])
        logits = sb("logits", [128, 2, CH, E0])
        top = sb("top", [128, 2, CH, 8])
        top_i = sb("top_i", [128, 2, CH, 8], U32)
        top_f = sb("top_f", [128, 2, CH, 2])
        hot = sb("hot", [128, 2, B, E0], BF16)
        both = sb("both", [128, B, E0], BF16)
        total = sb("total", [128, E0, B])
        before = sb("before", [128, E0, B])
        carry = sb("carry", [128, E0, B])
        slot_m = sb("slot_m", [128, B, E0])
        picked = sb("picked", [128, 2, B, E0])
        n_tiles = sb("n_tiles", [128, E0])
        ends = sb("ends", [128, E0])
        base = sb("base", [128, E0])
        slot_f = sb("slot_f", [128, 2, B])
        past = sb("past", [128, E0])
        first_slot = sb("first_slot", [128, 1])
        owner = sb("owner", [128, 1])
        comb = sb("comb0", [128, 2, CH, E0])
        comb2 = sb("comb20", [128, 2, CH, E0])
        combT = sb("combT0", [E0, 2, W])

        turned = sem("x_turned0")
        xT_copied = sem("xT_copied0")
        scored = sem("router_scored")
        kept = sem("x_kept")
        st = Steps(S, sem("route_steps"), 4 + 2 + 8 + 8 + 2 + 6 + 2)
        sl = Steps(S, sem("slot_steps"))
        counted = sem("counted")
        exped = sem("gate_exped")
        owner_turned = sem("owner_turned")
        scattered = [sem(f"scattered{k}") for k in range(2)]
        cb = Steps(S, sem("b2_steps"), 8)
        c_turned = sem("comb0_turned")
        c_copied = sem("comb0_copied")
        b2_ready = sem("b2_ready")

        block = ctx.enter_context(nc.Block())

        @block.sync
        def _(sp):
            sp.dma_start(S.w1_0[0:D, :, :], A["w1_0"].rearrange("e d h -> d e h")).then_inc(S.experts_in, 16)
            sp.dma_start(S.w1_0[D:D + 1, :, :].rearrange("p e h -> p (e h)"), A["b1_0"].rearrange("(o e) h -> o (e h)", o=1)
                         ).then_inc(S.experts_in, 16)
            sp.dma_start(S.w2_0[:, :, :], A["w2_0"].rearrange("e h d -> h e d")).then_inc(S.experts_in, 16)
            sp.dma_start(S.b2_0[:, :], A["b2_0"]).then_inc(S.experts_in, 16)

        @block.vector
        def _(dve):
            V = nc.vector
            with dve.Fori(0, NCH // 2) as i:
                st.start(dve, i)
                for r in range(2):
                    normalise(nc, S, st, xr[:, r, :, :], bass.ds(i * (2 * CH) + r * CH, CH))
                    st.mark(("x", r))
                for r in range(2):
                    hold(S, dve, scored, i * 2 + r + 1)
                    st.do(V.tensor_tensor(logits[:, r, :, :], S.ps[2 + r][:, 0:CH * E0].rearrange("p (k e) -> p k e", e=E0),
                                          bc(S.br0[:, :].unsqueeze(1), [128, CH, E0]), ALU.add))
                    for k in range(CH):
                        st.done(V.max(top[:, r, k, :], logits[:, r, k, :]))
                    st.wait()
                    for k in range(CH):
                        st.done(V.max_index(top_i[:, r, k, :], top[:, r, k, :], logits[:, r, k, :]))
                    st.wait()
                    st.do(V.tensor_copy(top_f[:, r, :, :], top_i[:, r, :, 0:2]))
                for r in range(2):
                    tiles = bass.ds(i * (2 * CH) + r * CH, CH)
                    for c in range(2):
                        st.done(V.tensor_tensor(hot[:, c, tiles, :], bc(S.iota_free[:, 0:E0].unsqueeze(1), [128, CH, E0]),
                                                bc(top_f[:, r, :, c:c + 1], [128, CH, E0]), ALU.is_equal))
                    st.done(V.tensor_tensor(S.gates[:, 1, tiles], top[:, r, :, 1], top[:, r, :, 0], ALU.subtract))
                st.wait()
                for r in range(2):
                    tiles = bass.ds(i * (2 * CH) + r * CH, CH)
                    st.done(V.tensor_tensor(both[:, tiles, :], hot[:, 0, tiles, :], hot[:, 1, tiles, :], ALU.add))
                hold(S, dve, kept, i * 2 + 2)
                st.wait()
                st.end()
            sl.start(dve)
            do = sl.do
            do(V.memset(carry[:, :, :], 1.0))
            do(V.memset(carry[:, :, 0:1], 0.0))
            sl.mark("routed")
            dve.wait_ge(exped, 1)
            do(V.tensor_scalar(S.gates[:, 0, :], S.gates[:, 1, :], 1.0, None, ALU.add))
            do(V.reciprocal(S.gates[:, 0, :], S.gates[:, 0, :]))
            do(V.tensor_tensor(S.gates[:, 1, :], S.gates[:, 1, :], S.gates[:, 0, :], ALU.mult))
            dve.wait_ge(counted, 2)
            do(V.tensor_copy(total[:, :, :].rearrange("p e (n b) -> p n b e", n=4),
                             S.bank[:, 4:8, :].rearrange("p n (b e) -> p n b e", e=E0)))
            do(V.tensor_tensor_scan(before[:, :, :].rearrange("p e b -> p (e b)"), carry[:, :, :].rearrange("p e b -> p (e b)"),
                                    total[:, :, :].rearrange("p e b -> p (e b)"), 0.0, ALU.mult, ALU.add))
            do(V.tensor_scalar(n_tiles[:, :], before[:, :, B - 1], 1.0 / 128, 63.5 / 128, ALU.mult, ALU.add))
            do(V.tensor_scalar(n_tiles[:, :], n_tiles[:, :], ROUND, None, ALU.add))
            do(V.tensor_scalar(n_tiles[:, :], n_tiles[:, :], -ROUND, 128.0, ALU.add, ALU.mult))
            do(V.tensor_tensor_scan(ends[:, :], bc(carry[:, 0, 1:2], [128, E0]),
                                    n_tiles[:, :], 0.0, ALU.mult, ALU.add))
            do(V.tensor_tensor(base[:, :], ends[:, :], n_tiles[:, :], ALU.subtract))
            do(V.tensor_tensor(before[:, :, :], before[:, :, :], total[:, :, :], ALU.subtract))
            do(V.tensor_tensor(before[:, :, :], before[:, :, :], bc(base[:, :].unsqueeze(2), [128, E0, B]), ALU.add))
            do(V.tensor_tensor(slot_m[:, :, :].rearrange("p (n b) e -> p n b e", n=4),
                               S.bank[:, 0:4, :].rearrange("p n (b e) -> p n b e", e=E0),
                               before[:, :, :].rearrange("p e (n b) -> p n b e", n=4), ALU.add))
            for c in range(2):
                sl.done(V.tensor_tensor(picked[:, c, :, :], hot[:, c, :, :], slot_m[:, :, :], ALU.mult))
            sl.wait()
            for c in range(2):
                sl.done(V.reduce_sum(slot_f[:, c, :], picked[:, c, :, :], AX.X))
            sl.wait()
            do(V.tensor_copy(S.slot_u[:, :, :], slot_f[:, :, :]))
            sl.mark("slots")
            do(V.tensor_scalar(first_slot[:, :], S.iota_part[:, :], 128.0, None, ALU.mult))
            do(V.tensor_scalar(past[:, :], ends[:, :], first_slot[:, 0:1], None, ALU.is_le))
            do(V.reduce_sum(owner[:, :], past[:, :], AX.X))
            do(V.tensor_scalar(owner[:, :], owner[:, :], float(E0 - 1), None, ALU.min))
            sl.mark("owner")
            dve.wait_ge(owner_turned, 1)
            do(V.tensor_copy(S.owner_row[:, :], S.ps[0][0:1, 0:128]))
            sl.mark("owner row")
            with dve.Fori(0, NCH // 2) as i:
                cb.start(dve, i)
                for r in range(2):
                    tiles = bass.ds(i * (2 * CH) + r * CH, CH)
                    cb.done(V.tensor_tensor(comb[:, r, :, :], hot[:, 0, tiles, :],
                                            bc(S.gates[:, 0, tiles].unsqueeze(2), [128, CH, E0]), ALU.mult))
                    cb.do(V.tensor_tensor(comb2[:, r, :, :], hot[:, 1, tiles, :],
                                          bc(S.gates[:, 1, tiles].unsqueeze(2), [128, CH, E0]), ALU.mult))
                    cb.do(V.tensor_tensor(comb[:, r, :, :], comb[:, r, :, :], comb2[:, r, :, :], ALU.add))
                    cb.mark(("comb", r))
                for r in range(2):
                    tiles = bass.ds(i * (2 * CH) + r * CH, CH)
                    hold(S, dve, b2_ready, i * 2 + r + 1)
                    cb.do(V.tensor_tensor(S.h[:, tiles, :], S.h[:, tiles, :],
                                          S.ps[4 + r][:, 0:CH * D].rearrange("p (k d) -> p k d", d=D), ALU.add))
                cb.end()

        @block.gpsimd
        def _(pool):
            with pool.Fori(0, NCH // 2) as i:
                for r in range(2):
                    st.after(pool, ("x", r), i)
                    nc.gpsimd.tensor_copy(S.xn[:, bass.ds(i * (2 * CH) + r * CH, CH), :], xr[:, r, :, :]).then_inc(kept, 1)
            sl.after(pool, "slots")
            pool.wait_ge(kept, NCH)
            for b in range(B):
                for c in range(2):
                    nc.gpsimd.indirect_dma_start(A["slot_x"], bass.IndirectOffsetOnAxis(ap=S.slot_u[:, c, b:b + 1], axis=0),
                                                 S.xn[:, b, :], None).then_inc(scattered[c], 16)
            for c in range(2):
                pool.wait_ge(scattered[c], 16 * B)

        @block.tensor
        def _(pe):
            M = nc.tensor.matmul
            with pe.Fori(0, NCH // 2) as i:
                for r in range(2):
                    st.after(pe, ("x", r), i)
                    for k in range(CH):
                        last = nc.tensor.transpose(S.ps[r][0:D, T * k:T * k + T], xr[:, r, k, :], S.ident[:, :])
                    last.then_inc(turned, 1)
                for r in range(2):
                    hold(S, pe, xT_copied, i * 2 + r + 1)
                    for k in range(CH):
                        last = M(S.ps[2 + r][:, E0 * k:E0 * k + E0], xT[:, r, T * k:T * k + T], S.wr0[:, :], start=True, stop=True)
                    last.then_inc(scored, 1)
            sl.after(pe, "routed")
            for n in range(4):
                last = M(S.ps[n][:, :], S.triS[:, :], both[:, 8 * n:8 * n + 8, :].rearrange("p b e -> p (b e)"),
                         start=True, stop=True)
            last.then_inc(counted, 1)
            for n in range(4):
                last = M(S.ps[4 + n][:, :], S.ones_bf[:, :], both[:, 8 * n:8 * n + 8, :].rearrange("p b e -> p (b e)"),
                         start=True, stop=True)
            last.then_inc(counted, 1)
            sl.after(pe, "owner")
            nc.tensor.transpose(S.ps[0][0:1, 0:128], owner[:, :], S.ident[:, :]).then_inc(owner_turned, 1)
            sl.after(pe, "owner row")
            pe.wait_ge(S.experts_in, 64)
            with pe.Fori(0, NCH // 2) as i:
                for r in range(2):
                    cb.after(pe, ("comb", r), i)
                    for k in range(CH):
                        last = nc.tensor.transpose(S.ps[r][0:E0, T * k:T * k + T], comb[:, r, k, :], S.ident[:, :])
                    last.then_inc(c_turned, 1)
                for r in range(2):
                    hold(S, pe, c_copied, i * 2 + r + 1)
                    for k in range(CH):
                        last = M(S.ps[4 + r][:, D * k:D * k + D], combT[:, r, T * k:T * k + T], S.b2_0[:, :], start=True, stop=True)
                    last.then_inc(b2_ready, 1)

        @block.scalar
        def _(act):
            N = nc.scalar.activation
            with act.Fori(0, NCH // 2) as i:
                for r in range(2):
                    hold(S, act, turned, i * 2 + r + 1)
                    N(xT[:, r, :], S.ps[r][0:D, :], ACT.Copy).then_inc(xT_copied, 1)
            sl.after(act, "routed")
            N(S.gates[:, 1, :], S.gates[:, 1, :], ACT.Exp).then_inc(exped, 1)
            with act.Fori(0, NCH // 2) as i:
                for r in range(2):
                    hold(S, act, c_turned, i * 2 + r + 1)
                    N(combT[:, r, :], S.ps[r][0:E0, :], ACT.Copy).then_inc(c_copied, 1)


def experts_stage(nc, S, A):
    NG = S.slots // W
    with ExitStack() as ctx:
        sb = lambda n, s, d=F32: ctx.enter_context(nc.sbuf_tensor(n, s, d))
        sem = lambda n: ctx.enter_context(nc.semaphore(n))
        xs = sb("xs", [128, 2, CH, D])
        xsT = sb("xsT", [128, 2, W])
        w1e = sb("w1e", [128, 2, CH, HID])
        w2e = sb("w2e", [HID, 2, CH, D])
        hidT = sb("hidT", [HID, 2, CH, 128])
        ys = sb("ys", [128, 2, CH, D])

        loaded = [sem(f"slots_loaded{r}") for r in range(2)]
        stored = [sem(f"slots_stored{r}") for r in range(2)]
        turned = sem("slots_turned")
        padded = sem("padded")
        xsT_copied = sem("xsT_copied")
        w1_copied = sem("w1_copied")
        w2_copied = sem("w2_copied")
        h_ready = sem("h_ready")
        relued = sem("relued")
        y_ready = sem("y_ready")
        y_copied = sem("y_copied")

        rows_in = A["slot_x"].rearrange("(g k p) d -> g p k d", k=CH, p=128)
        rows_out = A["slot_y"].rearrange("(g k p) d -> g p k d", k=CH, p=128)
        owners = lambda eng, g, n: nc.values_load_multi_w_load_instructions(
            S.owner_row[0:1, bass.ds(g * CH, n)], engines=(eng.engine,), min_val=0, max_val=E0 - 1)[1]
        block = ctx.enter_context(nc.Block())

        @block.sync
        def _(sp):
            for r in range(2):
                sp.dma_start(xs[:, r, :, :], rows_in[r]).then_inc(loaded[r], 16)
            with sp.Fori(0, NG // 2 - 1) as i:
                for r in range(2):
                    hold(S, sp, turned, i * 2 + r + 1)
                    sp.dma_start(xs[:, r, :, :], rows_in[bass.ds(i * 2 + r + 2, 1)].rearrange("g p k d -> (g p) k d")
                                 ).then_inc(loaded[r], 16)

        @block.tensor
        def _(pe):
            M = nc.tensor.matmul

            def turn_rows(i):
                for r in range(2):
                    hold(S, pe, loaded[r], i * 16 + 16)
                    for k in range(CH):
                        last = nc.tensor.transpose(S.ps[r][0:D, T * k:T * k + T], xs[:, r, k, :], S.ident[:, :])
                    last.then_inc(turned, 1)

            def turn(i, more):
                for r in range(2):
                    hold(S, pe, xsT_copied, i * 2 + r + 1)
                    for k in range(CH):
                        if k == 0:
                            hold(S, pe, w1_copied, (i * 2 + r) * CH + CH)
                        last = M(S.ps[2 + r][:, T * k:T * k + T], w1e[:, r, k, :], xsT[:, r, T * k:T * k + T],
                                 start=True, stop=True)
                    last.then_inc(h_ready, 1)
                if more:
                    turn_rows(i + 1)
                for r in range(2):
                    hold(S, pe, relued, i * 2 + r + 1)
                    hold(S, pe, w2_copied, (i * 2 + r) * CH + CH)
                    hold(S, pe, y_copied, i * 2 + r + 1)
                    for k in range(CH):
                        last = M(S.ps[4 + r][:, D * k:D * k + D], hidT[:, r, k, :], w2e[:, r, k, :], start=True, stop=True)
                    last.then_inc(y_ready, 1)

            pe.wait_ge(padded, 3)
            turn_rows(0)
            with pe.Fori(0, NG // 2 - 1) as i:
                turn(i, True)
            turn(NG // 2 - 1, False)

        @block.scalar
        def _(act):
            N = nc.scalar.activation

            def copy_rows(i):
                for r in range(2):
                    hold(S, act, turned, i * 2 + r + 1)
                    N(xsT[0:D, r, :], S.ps[r][0:D, :], ACT.Copy).then_inc(xsT_copied, 1)

            def turn(i, more):
                if more:
                    copy_rows(i + 1)
                for r in range(2):
                    hold(S, act, y_ready, i * 2 + r + 1)
                    hold(S, act, stored[r], i * 16 + 16)
                    N(ys[:, r, :, :], S.ps[4 + r][:, 0:CH * D].rearrange("p (k d) -> p k d", d=D), ACT.Copy).then_inc(y_copied, 1)
                    hold(S, act, y_copied, i * 2 + r + 3)
                    act.dma_start(rows_out[bass.ds(i * 2 + r, 1)].rearrange("g p k d -> (g p) k d"), ys[:, r, :, :]
                                  ).then_inc(stored[r], 16)

            act.sem_inc(y_copied, 2)
            for r in range(2):
                act.sem_inc(stored[r], 16)
            copy_rows(0)
            with act.Fori(0, NG // 2 - 1) as i:
                turn(i, True)
            turn(NG // 2 - 1, False)
            for r in range(2):
                act.wait_ge(stored[r], 16 * (NG // 2) + 16)

        @block.vector
        def _(dve):
            V = nc.vector

            def copy_w2(experts, r):
                for k in range(CH):
                    V.tensor_copy(w2e[:, r, k, :], S.w2_0[:, bass.ds(experts[r * CH + k], 1), :].rearrange("p a d -> p (a d)")
                                  ).then_inc(w2_copied, 1)

            def turn(i, more):
                for r in range(2):
                    hold(S, dve, h_ready, i * 2 + r + 1)
                    V.tensor_scalar(hidT[:, r, :, :].rearrange("p k t -> p (k t)"), S.ps[2 + r][:, :], 0.0, None,
                                    ALU.max).then_inc(relued, 1)
                if more:
                    experts = owners(dve, i * 2 + 2, 2 * CH)
                    for r in range(2):
                        hold(S, dve, y_ready, i * 2 + r + 1)
                        copy_w2(experts, r)

            V.memset(w1e[D:128, :, :, :], 0.0).then_inc(padded, 1)
            V.memset(xsT[D:128, :, :], 0.0).then_inc(padded, 1)
            dve.wait_ge(padded, 2)
            V.memset(xsT[D:D + 1, :, :], 1.0).then_inc(padded, 1)
            dve.wait_ge(S.experts_in, 64)
            experts = owners(dve, 0, 2 * CH)
            for r in range(2):
                copy_w2(experts, r)
            with dve.Fori(0, NG // 2 - 1) as i:
                turn(i, True)
            turn(NG // 2 - 1, False)

        @block.gpsimd
        def _(pool):
            def copy_w1(experts, r):
                for k in range(CH):
                    nc.gpsimd.tensor_copy(w1e[0:D + 1, r, k, :], S.w1_0[:, bass.ds(experts[r * CH + k], 1), :].rearrange("p a h -> p (a h)")
                                          ).then_inc(w1_copied, 1)

            pool.wait_ge(padded, 3)
            pool.wait_ge(S.experts_in, 64)
            experts = owners(pool, 0, 2 * CH)
            for r in range(2):
                copy_w1(experts, r)
            with pool.Fori(0, NG // 2 - 1) as i:
                experts = owners(pool, i * 2 + 2, 2 * CH)
                for r in range(2):
                    hold(S, pool, h_ready, i * 2 + r + 1)
                    copy_w1(experts, r)


def combine_stage(nc, S, A):
    NB = 4
    with ExitStack() as ctx:
        sb = lambda n, s, d=F32: ctx.enter_context(nc.sbuf_tensor(n, s, d))
        sem = lambda n: ctx.enter_context(nc.semaphore(n))
        yg = sb("yg", [128, 2, B, D])
        gathered = [sem(f"gathered_{b}") for b in range(NCH // 2)]
        rooted_h = sem("h_rooted2")
        st = Steps(S, sem("combine_steps"))

        block = ctx.enter_context(nc.Block())

        @block.gpsimd
        def _(pool):
            for b in range(B):
                for c in range(2):
                    nc.gpsimd.indirect_dma_start(yg[:, c, b, :], None, A["slot_y"],
                                                 bass.IndirectOffsetOnAxis(ap=S.slot_u[:, c, b:b + 1], axis=0)
                                                 ).then_inc(gathered[b // (2 * CH)], 16)

        @block.vector
        def _(dve):
            V = nc.vector
            st.start(dve)
            for i in range(NCH // 2):
                two = slice(2 * CH * i, 2 * CH * (i + 1))
                dve.wait_ge(gathered[i], 16 * 2 * 2 * CH)
                for c in range(2):
                    st.done(V.tensor_tensor(yg[:, c, two, :], yg[:, c, two, :],
                                            bc(S.gates[:, c, two].unsqueeze(2), [128, 2 * CH, D]), ALU.mult))
                st.wait()
                for c in range(2):
                    st.do(V.tensor_tensor(S.h[:, two, :], S.h[:, two, :], yg[:, c, two, :], ALU.add))
                layer_norm_stats(nc, S, st, dve, i, rooted_h)
                st.marks[("variance", i)] = st.marks["variance"]

        @block.scalar
        def _(act):
            for i in range(NCH // 2):
                st.after(act, ("variance", i))
                nc.scalar.activation(S.dev[:, :], S.mv[:, :, 1], ACT.Sqrt, bias=S.eps[:, 0:1]).then_inc(rooted_h, 1)


def grouped_stage(nc, S, A):
    NU = 2
    UH = NU * NPAR
    NB = 2 * CH // NU
    with ExitStack() as ctx:
        sb = lambda n, s, d=F32: ctx.enter_context(nc.sbuf_tensor(n, s, d))
        sem = lambda n: ctx.enter_context(nc.semaphore(n))
        x3 = sb("x3", [128, 2, CH, 2, D])
        x3T = sb("x3T", [128, 2, 2, W])
        yk = sb("yk", [128, 2, NPAR, W])
        mx = sb("mx", [128, 2, 2, UH])
        ex = sb("ex", [128, 2, 2, UH, GC])
        sums = sb("sums", [128, 2, 2, UH])
        pT = sb("pT", [128, 2, 2, UH, GC])
        rs = sb("rs", [128, 2, UH, T])

        doubled = sem("x3_doubled")
        turned = sem("x3_turned")
        x3T_copied = sem("x3T_copied")
        y_ready = sem("yk_ready")
        y_even = sem("yk_even_copied")
        y_odd = sem("yk_odd_copied")
        scored = sem("group_scored")
        shifted = sem("shifted")
        exped = sem("group_exped")
        weighed = sem("weighed")
        mixed = sem("mixed")
        rs_act = sem("rs_copied_by_act")
        rs_dve = sem("rs_copied_by_dve")
        out_ready = sem("group_out_ready")
        rooted_h = sem("h_rooted3")
        st = Steps(S, sem("group_steps"), 4 + NB * 4 + 2 + 19)

        zeroed = sem("x3T_zeroed")

        def units():
            return [(n // (CH // NU), NU * (n % (CH // NU))) for n in range(NB)]

        block = ctx.enter_context(nc.Block())

        @block.vector
        def _(dve):
            V = nc.vector
            with dve.Fori(0, NCH // 2) as i:
                st.start(dve, i)
                for r in range(2):
                    tiles = bass.ds(i * (2 * CH) + r * CH, CH)
                    st.do(V.tensor_tensor(x3[:, r, :, 0, :], S.h[:, tiles, :], bc(S.mean[:, tiles].unsqueeze(2), [128, CH, D]),
                                          ALU.subtract))
                    st.do(V.tensor_tensor(x3[:, r, :, 0, :], x3[:, r, :, 0, :], bc(S.rstd[:, tiles].unsqueeze(2), [128, CH, D]),
                                          ALU.mult))
                    st.mark(("x", r))
                for n in range(1, 2 * NPAR, 2):
                    hold(S, dve, y_ready, i * (2 * NPAR) + n + 1)
                    V.tensor_copy(yk[:, n // NPAR, n % NPAR, :], S.ps[n % 2][:, :]).then_inc(y_odd, 1)

                def soften(n):
                    s = S.bank[:, 2:4, 0:UH * GC].rearrange("p a (u k) -> p a u k", k=GC)
                    hold(S, dve, scored, i * NB + n + 1)
                    st.do(V.reduce_max(mx[:, n % 2, :, :], s, AX.X))
                    V.tensor_tensor(ex[:, n % 2, :, :, :], s, bc(mx[:, n % 2, :, :].unsqueeze(3), [128, 2, UH, GC]),
                                    ALU.subtract).then_inc(shifted, 1)

                def weigh(n):
                    hold(S, dve, exped, i * NB + n + 1)
                    st.do(V.reduce_sum(sums[:, n % 2, :, :], ex[:, n % 2, :, :, :], AX.X))
                    st.do(V.reciprocal(sums[:, n % 2, :, :], sums[:, n % 2, :, :]))
                    st.do(V.tensor_tensor(ex[:, n % 2, :, :, :], ex[:, n % 2, :, :, :],
                                          bc(sums[:, n % 2, :, :].unsqueeze(3), [128, 2, UH, GC]), ALU.mult))
                    V.transpose(pT[:, n % 2, :, :, :].rearrange("p a u k -> p (a u k)"),
                                ex[:, n % 2, :, :, :].rearrange("p a u k -> p (a u k)")).then_inc(weighed, 1)

                def unload(n):
                    hold(S, dve, mixed, i * NB + n + 1)
                    V.tensor_copy(rs[:, n % 2, :, 2 * GC:4 * GC].rearrange("p u (g q) -> p g u q", q=GC),
                                  S.bank[:, 6:8, 0:UH * GC].rearrange("p g (u q) -> p g u q", q=GC)).then_inc(rs_dve, 1)

                soften(0)
                for n in range(NB):
                    weigh(n)
                    if n + 1 < NB:
                        soften(n + 1)
                    unload(n)
                for r in range(2):
                    tiles = bass.ds(i * (2 * CH) + r * CH, CH)
                    hold(S, dve, out_ready, i * 2 + r + 1)
                    st.done(V.tensor_tensor(S.h[:, tiles, :], S.h[:, tiles, :],
                                            S.ps[r][:, 0:CH * D].rearrange("p (k d) -> p k d", d=D), ALU.add))
                st.wait()
                layer_norm_stats(nc, S, st, dve, i, rooted_h)
                st.end()

        @block.gpsimd
        def _(pool):
            nc.gpsimd.memset(x3T[D:128, 0, :, :], 0.0).then_inc(zeroed, 1)
            pool.wait_ge(zeroed, 1)
            nc.gpsimd.memset(x3T[0:D, 1, :, :], 0.0).then_inc(zeroed, 1)
            pool.wait_ge(zeroed, 2)
            with pool.Fori(0, NCH // 2) as i:
                for r in range(2):
                    st.after(pool, ("x", r), i)
                    nc.gpsimd.tensor_copy(x3[:, r, :, 1, :], x3[:, r, :, 0, :]).then_inc(doubled, 1)

        @block.tensor
        def _(pe):
            M = nc.tensor.matmul
            with pe.Fori(0, NCH // 2) as i:
                pe.wait_ge(zeroed, 2)
                for r in range(2):
                    hold(S, pe, doubled, i * 2 + r + 1)
                    for k in range(CH):
                        last = nc.tensor.transpose(S.ps[r][:, T * k:T * k + T], x3[:, r, k, :, :].rearrange("p a d -> p (a d)"),
                                                   S.ident[:, :])
                    last.then_inc(turned, 1)
                for n in range(2 * NPAR):
                    r, k = n // NPAR, n % NPAR
                    if n < 2:
                        hold(S, pe, x3T_copied, i * 4 + 4)
                    elif n % 2:
                        hold(S, pe, y_odd, i * NPAR + n // 2)
                    else:
                        hold(S, pe, y_even, i * NPAR + n // 2)
                    M(S.ps[n % 2][:, :], S.qkT[:, k, :, :].rearrange("p a d -> p (a d)"), x3T[:, 0, r, :],
                      start=True, stop=True).then_inc(y_ready, 1)
                hold(S, pe, y_even, i * NPAR + NPAR)
                hold(S, pe, y_odd, i * NPAR + NPAR)

                def score(n):
                    r, first = units()[n]
                    if n:
                        hold(S, pe, shifted, i * NB + n)
                    for a in range(2):
                        for u in range(NU):
                            at = T * (first + u)
                            for g in range(GG):
                                v = (g + 1) % GG
                                last = M(S.ps[2 + a][GC * v:GC * v + GC, NPAR * GC * u:NPAR * GC * (u + 1)].rearrange(
                                            "p (h k) -> p h k", k=GC),
                                         x3T[:, a, r, at + GC * g:at + GC * g + GC],
                                         yk[:, r, :, at + GC * v:at + GC * v + GC], start=True, stop=True)
                    last.then_inc(scored, 1)

                def mix(n):
                    r, first = units()[n]
                    hold(S, pe, weighed, i * NB + n + 1)
                    if n:
                        hold(S, pe, rs_act, i * NB + n)
                        hold(S, pe, rs_dve, i * NB + n)
                    for u in range(NU):
                        for g in range(GG):
                            v = (g + 1) % GG
                            for a in range(2):
                                last = M(S.ps[4 + g][64 * a:64 * a + 64, NPAR * GC * u:NPAR * GC * (u + 1)],
                                         x3[GC * v:GC * v + GC, r, first + u, 0, :],
                                         pT[GC * v:GC * v + GC, n % 2, a, NPAR * u:NPAR * (u + 1), :].rearrange("p h q -> p (h q)"),
                                         start=True, stop=True)
                    last.then_inc(mixed, 1)

                def project(n):
                    r, first = units()[n]
                    hold(S, pe, rs_act, i * NB + n + 1)
                    hold(S, pe, rs_dve, i * NB + n + 1)
                    for u in range(NU):
                        for k in range(NPAR):
                            last = M(S.ps[r][:, D * (first + u):D * (first + u) + D], rs[:, n % 2, NPAR * u + k, :], S.wv[:, k, :],
                                     start=(k == 0), stop=(k == NPAR - 1))
                    if n % (NB // 2) == NB // 2 - 1:
                        last.then_inc(out_ready, 1)

                score(0)
                for n in range(NB):
                    if n + 1 < NB:
                        score(n + 1)
                    mix(n)
                    project(n)

        @block.scalar
        def _(act):
            N = nc.scalar.activation
            with act.Fori(0, NCH // 2) as i:
                for r in range(2):
                    hold(S, act, turned, i * 2 + r + 1)
                    for a in range(2):
                        half = slice(64 * a, 64 * a + 64)
                        N(x3T[half, a, r, :], S.ps[r][half, :], ACT.Copy).then_inc(x3T_copied, 1)
                for n in range(0, 2 * NPAR, 2):
                    hold(S, act, y_ready, i * (2 * NPAR) + n + 1)
                    N(yk[:, n // NPAR, n % NPAR, :], S.ps[n % 2][:, :], ACT.Copy).then_inc(y_even, 1)
                for n in range(NB):
                    hold(S, act, shifted, i * NB + n + 1)
                    e = ex[:, n % 2, :, :, :].rearrange("p a u k -> p (a u k)")
                    N(e, e, ACT.Exp).then_inc(exped, 1)
                    if n:
                        hold(S, act, mixed, i * NB + n)
                        N(rs[:, (n - 1) % 2, :, 0:2 * GC].rearrange("p u (g q) -> p g u q", q=GC),
                          S.bank[:, 4:6, 0:UH * GC].rearrange("p g (u q) -> p g u q", q=GC), ACT.Copy).then_inc(rs_act, 1)
                hold(S, act, mixed, i * NB + NB)
                N(rs[:, (NB - 1) % 2, :, 0:2 * GC].rearrange("p u (g q) -> p g u q", q=GC),
                  S.bank[:, 4:6, 0:UH * GC].rearrange("p g (u q) -> p g u q", q=GC), ACT.Copy).then_inc(rs_act, 1)
                st.after(act, "variance", i)
                N(S.dev[:, :], S.mv[:, :, 1], ACT.Sqrt, bias=S.eps[:, 0:1]).then_inc(rooted_h, 1)


def second_experts_stage(nc, S, A, out):
    with ExitStack() as ctx:
        sb = lambda n, s, d=F32: ctx.enter_context(nc.sbuf_tensor(n, s, d))
        sem = lambda n: ctx.enter_context(nc.semaphore(n))
        r2 = sb("r2", [128, B])
        xr = sb("x4", [128, 2, CH, D])
        xT = sb("x4T", [128, NCH, W])
        logits = sb("logits1", [128, 2, CH, E1])
        top = sb("top1", [128, 2, CH, 8])
        top_i = sb("top_i1", [128, 2, CH, 8], U32)
        top_f = sb("top_f1", [128, 2, CH, 2])
        xT_now = sb("x4T_now", [D, 2, W])
        hot = sb("hot1", [128, 2, B, E1])
        gates = sb("gates1", [128, 2, B])
        share = sb("share", [128, B, E1])
        share_now = sb("share_now", [128, 2, CH, E1])
        shareT = sb("shareT", [E1, 2, W])
        hid = sb("hid1", [HID, 4, W])
        acc = sb("acc", [128, 2, CH, D])
        res = sb("res", [128, 2, CH, D])

        scaled = sem("r2_rooted")
        turned = sem("x4_turned")
        x4_copied = sem("x4T_copied")
        scored = sem("router1_scored")
        exped = sem("gates1_exped")
        pre = Steps(S, sem("r2_steps"))
        st = Steps(S, sem("router1_steps"), 28)
        gs = Steps(S, sem("share_steps"))
        share_turned = sem("share_turned")
        shareT_copied = sem("shareT_copied")
        hidden = sem("hidden1")
        gelued = sem("gelued1")
        y_ready = sem("y1_ready")
        es = Steps(S, sem("expert1_steps"), 2 + 2 + 2 * E1 * CH + 2)
        sent_r = [sem(f"sent{r}") for r in range(2)]
        zeroed = sem("x4T_zeroed")
        hot_first = sem("hot_first")

        block = ctx.enter_context(nc.Block())

        @block.vector
        def _(dve):
            V = nc.vector
            pre.start(dve)
            pre.do(V.tensor_tensor(r2[:, :], S.rstd[:, :], S.rstd[:, :], ALU.mult))
            pre.do(V.tensor_tensor(r2[:, :], r2[:, :], S.var[:, :], ALU.mult))
            pre.mark("variance")
            dve.wait_ge(scaled, 1)
            pre.do(V.reciprocal(r2[:, :], r2[:, :]))
            pre.do(V.tensor_tensor(r2[:, :], r2[:, :], S.rstd[:, :], ALU.mult))
            with dve.Fori(0, NCH // 2) as i:
                st.start(dve, i)
                for r in range(2):
                    tiles = bass.ds(i * (2 * CH) + r * CH, CH)
                    st.do(V.tensor_tensor(xr[:, r, :, :], S.h[:, tiles, :], bc(S.mean[:, tiles].unsqueeze(2), [128, CH, D]),
                                          ALU.subtract))
                    st.do(V.tensor_tensor(xr[:, r, :, :], xr[:, r, :, :], bc(r2[:, tiles].unsqueeze(2), [128, CH, D]), ALU.mult))
                    st.mark(("x", r))
                for r in range(2):
                    tiles = bass.ds(i * (2 * CH) + r * CH, CH)
                    hold(S, dve, scored, i * 2 + r + 1)
                    st.do(V.tensor_tensor(logits[:, r, :, :], S.ps[2 + r][:, 0:CH * E1].rearrange("p (k e) -> p k e", e=E1),
                                          bc(S.br1[:, :].unsqueeze(1), [128, CH, E1]), ALU.add))
                    for k in range(CH):
                        st.done(V.max(top[:, r, k, :], logits[:, r, k, :]))
                    st.wait()
                    for k in range(CH):
                        st.done(V.max_index(top_i[:, r, k, :], top[:, r, k, :], logits[:, r, k, :]))
                    st.wait()
                    st.do(V.tensor_copy(top_f[:, r, :, :], top_i[:, r, :, 0:2]))
                    st.done(V.tensor_tensor(gates[:, 1, tiles], top[:, r, :, 1], top[:, r, :, 0], ALU.subtract))
                    for c in range(2):
                        ins = V.tensor_tensor(hot[:, c, tiles, :], bc(S.iota_free[:, 0:E1].unsqueeze(1), [128, CH, E1]),
                                              bc(top_f[:, r, :, c:c + 1], [128, CH, E1]), ALU.is_equal)
                        if c == 0:
                            ins.then_inc(hot_first, 1)
                        else:
                            st.do(ins)
                st.end()
            gs.start(dve)
            gs.mark("routed")
            dve.wait_ge(exped, 1)
            dve.wait_ge(hot_first, NCH)
            gs.do(V.tensor_scalar(gates[:, 0, :], gates[:, 1, :], 1.0, None, ALU.add))
            gs.do(V.reciprocal(gates[:, 0, :], gates[:, 0, :]))
            gs.do(V.tensor_tensor(gates[:, 1, :], gates[:, 1, :], gates[:, 0, :], ALU.mult))
            for c in range(2):
                gs.done(V.tensor_tensor(hot[:, c, :, :], hot[:, c, :, :], bc(gates[:, c, :].unsqueeze(2), [128, B, E1]), ALU.mult))
            gs.wait()
            gs.do(V.tensor_tensor(share[:, :, :], hot[:, 0, :, :], hot[:, 1, :, :], ALU.add))
            with dve.Fori(0, NCH // 2) as i:
                es.start(dve, i)
                for r in range(2):
                    tiles = bass.ds(i * (2 * CH) + r * CH, CH)
                    es.done(V.tensor_scalar(share_now[:, r, :, :], share[:, tiles, :], 1.0, None, ALU.mult))
                    es.mark(("share", r))
                for r in range(2):
                    tiles = bass.ds(i * (2 * CH) + r * CH, CH)
                    hold(S, dve, y_ready, i * (2 * E1 + 2) + r + 1)
                    es.done(V.tensor_tensor(acc[:, r, :, :], S.h[:, tiles, :],
                                            S.ps[2 + r][:, 0:CH * D].rearrange("p (k d) -> p k d", d=D), ALU.add))
                for n in range(2 * E1):
                    r, e = n // E1, n % E1
                    hold(S, dve, y_ready, i * (2 * E1 + 2) + n + 3)
                    es.wait()
                    for k in range(CH):
                        es.done(V.scalar_tensor_tensor(acc[:, r, k, :], S.ps[4 + n % 4][:, D * k:D * k + D],
                                                       share_now[:, r, k, e:e + 1], acc[:, r, k, :], ALU.mult, ALU.add))
                    es.mark(("added", n))
                    if e == E1 - 1:
                        es.wait()
                        hold(S, dve, sent_r[r], i * 16 + 16)
                        es.done(V.tensor_copy(res[:, r, :, :], acc[:, r, :, :]))
                        es.mark(("result", r))
                es.wait()
                es.end()

        @block.gpsimd
        def _(pool):
            nc.gpsimd.memset(xT[D:128, :, :], 0.0).then_inc(zeroed, 1)

        @block.tensor
        def _(pe):
            M = nc.tensor.matmul
            with pe.Fori(0, NCH // 2) as i:
                for r in range(2):
                    st.after(pe, ("x", r), i)
                    for k in range(CH):
                        last = nc.tensor.transpose(S.ps[r][0:D, T * k:T * k + T], xr[:, r, k, :], S.ident[:, :])
                    last.then_inc(turned, 1)
                for r in range(2):
                    hold(S, pe, x4_copied, i * 4 + 2 * r + 2)
                    for k in range(CH):
                        last = M(S.ps[2 + r][:, E1 * k:E1 * k + E1], xT_now[:, r, T * k:T * k + T], S.wr1[:, :], start=True, stop=True)
                    last.then_inc(scored, 1)
            pe.wait_ge(zeroed, 1)
            with pe.Fori(0, NCH // 2) as i:
                def up(n):
                    r, e = n // E1, n % E1
                    if n >= 2:
                        hold(S, pe, gelued, i * (2 * E1) + n - 1)
                    M(S.ps[n % 2][:, :], S.w1_1[:, e, :], xT[:, bass.ds(i * 2 + r, 1), :].rearrange("p a w -> p (a w)"),
                      start=True, stop=True).then_inc(hidden, 1)

                def down(n):
                    r, e = n // E1, n % E1
                    hold(S, pe, gelued, i * (2 * E1) + n + 1)
                    if n >= 4:
                        es.after(pe, ("added", n - 4), i)
                    for k in range(CH):
                        last = M(S.ps[4 + n % 4][:, D * k:D * k + D], hid[:, n % 4, T * k:T * k + T], S.w2_1[:, e, :],
                                 start=True, stop=True)
                    last.then_inc(y_ready, 1)

                up(0)
                up(1)
                for r in range(2):
                    es.after(pe, ("share", r), i)
                    for k in range(CH):
                        last = nc.tensor.transpose(S.ps[6 + r][0:E1, T * k:T * k + T], share_now[:, r, k, :], S.ident[:, :])
                    last.then_inc(share_turned, 1)
                for r in range(2):
                    hold(S, pe, shareT_copied, i * 2 + r + 1)
                    for k in range(CH):
                        last = M(S.ps[2 + r][:, D * k:D * k + D], shareT[:, r, T * k:T * k + T], S.b2_1[:, :], start=True, stop=True)
                    last.then_inc(y_ready, 1)
                for n in range(2 * E1):
                    if n + 2 < 2 * E1:
                        up(n + 2)
                    down(n)

        @block.scalar
        def _(act):
            N = nc.scalar.activation
            pre.after(act, "variance")
            N(r2[:, :], r2[:, :], ACT.Sqrt, bias=S.eps[:, 0:1]).then_inc(scaled, 1)
            with act.Fori(0, NCH // 2) as i:
                for r in range(2):
                    hold(S, act, turned, i * 2 + r + 1)
                    N(xT_now[:, r, :], S.ps[r][0:D, :], ACT.Identity, scale=S.gamma[:, 0:1], bias=S.beta[:, 0:1]).then_inc(x4_copied, 1)
                    N(xT[0:D, bass.ds(i * 2 + r, 1), :].rearrange("p a w -> p (a w)"), S.ps[r][0:D, :], ACT.Identity,
                      scale=S.gamma[:, 0:1], bias=S.beta[:, 0:1]).then_inc(x4_copied, 1)
            act.wait_ge(st.sem, st.per_turn * (NCH // 2))
            N(gates[:, 1, :], gates[:, 1, :], ACT.Exp).then_inc(exped, 1)
            with act.Fori(0, NCH // 2) as i:
                for n in range(2 * E1):
                    if n == 1:
                        for r in range(2):
                            hold(S, act, share_turned, i * 2 + r + 1)
                            N(shareT[:, r, :], S.ps[6 + r][0:E1, :], ACT.Copy).then_inc(shareT_copied, 1)
                    hold(S, act, hidden, i * (2 * E1) + n + 1)
                    if n >= 4:
                        hold(S, act, y_ready, i * (2 * E1 + 2) + n - 4 + 3)
                    N(hid[:, n % 4, :], S.ps[n % 2][:, :], ACT.Gelu, bias=S.b1_1[:, n % E1:n % E1 + 1]).then_inc(gelued, 1)

        @block.sync
        def _(sp):
            rows = out.rearrange("(c k) p d -> c p k d", k=CH)
            for r in range(2):
                sp.sem_inc(sent_r[r], 16)
            with sp.Fori(0, NCH // 2) as i:
                for r in range(2):
                    es.after(sp, ("result", r), i)
                    sp.dma_start(rows[bass.ds(i * 2 + r, 1)].rearrange("c p k d -> (c p) k d"), res[:, r, :, :]).then_inc(sent_r[r], 16)
            for r in range(2):
                sp.wait_ge(sent_r[r], 16 + 16 * (NCH // 2))


def build(nc, A, out):
    A["idx_scratch"] = nc.dram_tensor("idx_scratch", [B, T], BF16).ap()
    S = Store()
    S.slots = 2 * B * T + E0 * 128
    A["slot_y"] = nc.dram_tensor("slot_y", [S.slots, D], F32).ap()
    A["slot_x"] = nc.dram_tensor("slot_x", [S.slots, D], F32).ap()
    with ExitStack() as ctx:
        sb = lambda n, s, d=F32: ctx.enter_context(nc.sbuf_tensor(n, s, d))
        S.bank = ctx.enter_context(nc.psum_tensor("banks", [128, 8, 512], F32))
        S.ps = [S.bank[:, k, :] for k in range(8)]
        S.ident = sb("ident", [128, 128])
        S.triC = sb("triC", [128, 128])
        S.triS = sb("triS", [128, 128], BF16)
        S.cmean = sb("cmean", [128, 128])
        S.iota_free = sb("iota_free", [128, 128])
        S.iota_part = sb("iota_part", [128, 1])
        S.ones_bf = sb("ones_bf", [128, 128], BF16)
        S.eps = sb("eps", [128, 1])
        S.half_pi = sb("half_pi", [128, 1])
        S.xT = sb("xT", [T, B], I32)
        S.maskT = sb("maskT", [T, B])
        S.w1c = sb("w1c", [128, 128])
        S.w1p = sb("w1p", [128, 128])
        S.b1c = sb("b1c", [128, 1])
        S.w2c = sb("w2c", [128, GT])
        S.sg_w1 = sb("sg_w1", [128, D // 2])
        S.sg_b1 = sb("sg_b1", [D // 2, 1])
        S.sg_w2 = sb("sg_w2", [D // 2, 1])
        S.wx = sb("wx", [128, P + 2 * D])
        S.proj_b = sb("proj_b", [128, NPROJ])
        S.pcs = sb("pcs", [T, 2, P])
        S.pcsT = sb("pcsT", [128, T])
        S.ppT = sb("ppT", [128, T])
        S.dcs = sb("dcs", [T, 2, NW])
        S.nhd2 = sb("nhd2", [T, NW])
        S.out_w2 = sb("out_w2", [128, D])
        S.out_row = sb("out_row", [128, D])
        S.wr0 = sb("wr0", [D, E0])
        S.br0 = sb("br0", [128, E0])
        S.qkT = sb("qkT", [128, NPAR, 2, D])
        S.wv = sb("wv", [128, NPAR, D])
        S.gamma = sb("gamma", [D, 1])
        S.beta = sb("beta", [D, 1])
        S.wr1 = sb("wr1", [D, E1])
        S.br1 = sb("br1", [128, E1])
        S.w1_1 = sb("w1_1", [128, E1, HID])
        S.w2_1 = sb("w2_1", [HID, E1, D])
        S.b1_1 = sb("b1_1", [HID, E1])
        S.b2_1 = sb("b2_1", [E1, D])
        S.h = sb("h", [128, B, D])
        S.stats = sb("stats", [128, 2 * CH, 6])
        S.mv = sb("mv", [128, 2 * CH, 2])
        S.dev = sb("dev", [128, 2 * CH])
        S.mean = sb("mean", [128, B])
        S.var = sb("var", [128, B])
        S.rstd = sb("rstd", [128, B])
        S.waits = {e.engine: ctx.enter_context(nc.semaphore(f"waits_{n}")) for n, e in enumerate(
            (nc.tensor, nc.vector, nc.scalar, nc.gpsimd, nc.sync))}
        with ExitStack() as tok:
            tb = lambda n, s, d=F32: tok.enter_context(nc.sbuf_tensor(n, s, d))
            S.b_oah = tb("b_oah", [128, D])
            S.zeros = tb("zeros", [128, 32 * D])
            S.x_bc = tb("x_bc", [128, B * T], I32)
            S.idx_bc = tb("idx_bc", [128, B * T], BF16)
            S.triG = tb("triG", [128, 128])
            S.emb = tb("emb", [T, D])
            S.emb3 = tb("emb3", [T, 3, D], BF16)
            S.emb_last3 = tb("emb_last3", [3, D], BF16)
            S.w_inT = tb("w_inT", [D, D])
            S.hn = tb("hn", [128, 2, CH, D + 1])
            setup_stage(nc, S, A)
            token_stage(nc, S, A)
        with ExitStack() as mem:
            mb = lambda n, s, d=F32: mem.enter_context(nc.sbuf_tensor(n, s, d))
            S.proj = mb("proj", [128, B, NPROJ])
            project_stage(nc, S, A)
            S.q_pos = mb("q_pos", [128, B, 2 * P])
            S.q_kv = mb("q_kv", [128, B, 2 * P])
            S.k_kv = mb("k_kv", [128, B, 2 * P])
            S.gv = mb("gv", [128, B, D])
            phase_stage(nc, S, A)
            memory_stage(nc, S, A)
        with ExitStack() as moe:
            eb = lambda n, s, d=F32: moe.enter_context(nc.sbuf_tensor(n, s, d))
            S.xn = eb("xn", [128, B, D])
            S.gates = eb("gates", [128, 2, B])
            S.slot_u = eb("slot_u", [128, 2, B], U32)
            S.w1_0 = eb("w1_0", [D + 1, E0, HID])
            S.w2_0 = eb("w2_0", [HID, E0, D])
            S.b2_0 = eb("b2_0", [E0, D])
            S.experts_in = moe.enter_context(nc.semaphore("experts_in"))
            S.owner_row = eb("owner_row", [1, 128], I32)
            route_stage(nc, S, A)
            experts_stage(nc, S, A)
            combine_stage(nc, S, A)
        grouped_stage(nc, S, A)
        second_experts_stage(nc, S, A, out)


INPUTS = {
    "x": "x", "L0_tok_emb_table": "emb", "L0_tok_W_in": "w_in", "L0_tok_b_oah": "b_oah",
    "L0_attn_pos_phases": "phases", "L0_attn_window_deltas": "deltas", "L0_attn_mc_w": "mc_w", "L0_attn_mc_b": "mc_b",
    "L0_attn_hop_w1": "hop_w1", "L0_attn_hop_b1": "hop_b1", "L0_attn_hop_w2": "hop_w2", "L0_attn_hop_b2": "hop_b2",
    "L0_attn_cpe_w": "cpe_w", "L0_attn_cpe_b": "cpe_b", "L0_attn_ve_w": "ve_w", "L0_attn_ve_b": "ve_b",
    "L0_attn_kce_w": "kce_w", "L0_attn_kce_b": "kce_b", "L0_attn_ksk_w1": "ksk_w1", "L0_attn_ksk_b1": "ksk_b1",
    "L0_attn_ksk_w2": "ksk_w2", "L0_attn_ksk_b2": "ksk_b2", "L0_attn_sg_w1": "sg_w1", "L0_attn_sg_b1": "sg_b1",
    "L0_attn_sg_w2": "sg_w2", "L0_attn_sg_b2": "sg_b2", "L0_attn_ln_g": "ln_g", "L0_attn_ln_b": "ln_b",
    "L0_attn_out_w": "out_w", "L0_attn_out_b": "out_b", "L0_ffn_Wr": "wr0", "L0_ffn_br": "br0",
    "L0_ffn_W1": "w1_0", "L0_ffn_b1": "b1_0", "L0_ffn_W2": "w2_0", "L0_ffn_b2": "b2_0",
    "L1_attn_Wq": "wq", "L1_attn_Wk": "wk", "L1_attn_Wo": "wo", "L1_ffn_gamma": "gamma", "L1_ffn_beta": "beta",
    "L1_ffn_Wr": "wr1", "L1_ffn_br": "br1", "L1_ffn_W1": "w1_1", "L1_ffn_b1": "b1_1", "L1_ffn_W2": "w2_1",
    "L1_ffn_b2": "b2_1",
}


def kernel(**inputs):
    import concourse.bacc as _bacc
    from concourse.bass_utils import run_bass_kernel_spmd as _run

    nc = _bacc.Bacc("TRN2", target_bir_lowering=False, num_devices=1)
    arrays, aps = {}, {}
    for name, short in INPUTS.items():
        a = np.ascontiguousarray(inputs[name])
        arrays[f"in_{short}"] = a
        aps[short] = nc.dram_tensor(f"in_{short}", a.shape, mybir.dt.from_np(a.dtype), kind="ExternalInput").ap()
    out = nc.dram_tensor("out_h", (B, T, D), F32, kind="ExternalOutput").ap()
    build(nc, aps, out)
    r = _run(nc, [arrays], core_ids=[0])
    return r.results[0]["out_h"]
```

```python
import numpy as np
from contextlib import ExitStack

import concourse.bass as bass
from concourse import mybir

F32 = mybir.dt.float32
BF16 = mybir.dt.bfloat16
I32 = mybir.dt.int32
U32 = mybir.dt.uint32
ALU = mybir.AluOpType
ACT = mybir.ActivationFunctionType
AX = mybir.AxisListType

B, T, D = 32, 128, 64
CH = 4
NCH = B // CH
W = CH * T
NPOS = T + 1
P = 32
NH = 4
NW = 5
HP = P + 1
E0, E1, HID = 64, 8, 128
GH, GG, GC = 10, 4, 32
NPAR = GH // 2
EPS = 1e-5

AO, ST, GT, KY, CT, VL = 0, NH * HP, NH * HP + P, NH * HP + P + 1, NH * HP + 2 * P + 1, NH * HP + 2 * P + 1 + D
NPROJ = VL + D

PI_BELOW = float(np.nextafter(np.float32(np.pi), np.float32(0)))
HALF_PI = float(np.float32(np.pi / 2))
TWO_PI_PARTS = [6.28125, float(np.float32(2 * np.pi - 6.28125)),
                float(2 * np.pi - 6.28125 - float(np.float32(2 * np.pi - 6.28125)))]
ROUND = 12582912.0


class Store:
    pass


class Steps:

    def __init__(self, S, sem, per_turn=0):
        self.S, self.looped, self.sem, self.per_turn, self.n, self.marks = S, per_turn > 0, sem, per_turn, 0, {}

    def start(self, eng, turn=0):
        self.eng, self.base, self.n = eng, turn * self.per_turn, 0

    def done(self, ins):
        ins.then_inc(self.sem, 1)
        self.n += 1

    def wait(self):
        if self.looped:
            hold(self.S, self.eng, self.sem, self.base + self.n)
        else:
            self.eng.wait_ge(self.sem, self.n)

    def do(self, ins):
        self.done(ins)
        self.wait()

    def mark(self, name):
        self.marks[name] = self.n

    def end(self):
        assert self.n == self.per_turn, f"{self.n} steps a turn"

    def after(self, eng, name, turn=0):
        if self.looped:
            hold(self.S, eng, self.sem, turn * self.per_turn + self.marks[name])
        else:
            eng.wait_ge(self.sem, self.marks[name])


def hold(S, eng, sem, value):
    eng.wait_ge(sem, value)
    eng.sem_inc(S.waits[eng.engine], 1)


def bc(ap, shape):
    return ap.to_broadcast(shape)


def col(ap):
    return ap.rearrange("(p o) -> p o", o=1)


def setup_stage(nc, S, A):
    with ExitStack() as ctx:
        sb = lambda n, s, d=F32: ctx.enter_context(nc.sbuf_tensor(n, s, d))
        sem = lambda n: ctx.enter_context(nc.semaphore(n))
        x_row = sb("x_row", [B, T], I32)
        w_in = sb("w_in", [D, D])
        emb_last = sb("emb_last", [3, D])
        emb_rest = sb("emb_rest", [128, 2, D])
        last_part = sb("last_part", [3, 3, D], BF16)
        last_rest = sb("last_rest", [3, 2, D])
        emb_low = sb("emb_low", [128, D])
        kce_w = sb("kce_w", [D, D])
        kce_wT = sb("kce_wT", [D, D])
        ksk_low = sb("ksk_low", [D, D])
        kce_b = sb("kce_b", [D, 1])
        ksk_b1 = sb("ksk_b1", [128, 1])
        ln_g = sb("ln_g", [128, 1])
        ln_b = sb("ln_b", [D, 1])
        ln_bb = sb("ln_bb", [D, 128])
        out_w = sb("out_w", [128, D])
        out_b = sb("out_b", [128, D])
        wq = sb("wq", [D, GH, D])
        wk = sb("wk", [D, GH, D])
        wo = sb("wo", [D, GH, D])
        wqT = sb("wqT", [128, NPAR, D])
        wkT = sb("wkT", [128, NPAR, D])
        woT = sb("woT", [128, NPAR, D])
        pp = sb("pp", [T, P])
        ang = sb("ang", [T, P + NW])
        turns = sb("turns", [T, P + NW])
        absa = sb("absa", [T, P + NW])
        sincos = sb("sincos", [T, 2, P + NW])
        pdup = sb("pdup", [T, 2, 2, P])
        seq_len = sb("seq_len", [B, 1])
        mask_row = sb("mask_row", [B, T])
        idx_row = sb("idx_row", [B, T])
        neg_row = sb("neg_row", [B, T])
        idx_bf = sb("idx_bf", [B, T], BF16)
        rec_row = sb("rec_row", [128, 128])
        triS_f = sb("triS_f", [128, 128])
        xT_i = sb("xT_i", [T, B], I32)

        weights_in = sem("weights_in")
        weights_in2 = sem("weights_in_by_pool")
        early_in = sem("early_in")
        idx_out = sem("idx_out")
        idx_back = sem("idx_back")
        masks_made = sem("masks_made")
        dve_done = sem("setup_dve_done")
        act_done = sem("setup_act_done")
        pe_done = sem("setup_pe_done")
        pool_done = sem("setup_pool_done")
        zeroed = sem("rows_zeroed")

        early = [(x_row[:, :], A["x"]), (S.x_bc[:, :].rearrange("p (b t) -> p b t", b=B), A["x"].partition_broadcast(128)),
                 (S.emb[:, :], A["emb"][0:T, :]),
                 (emb_last[:, :], A["emb"][T, :].partition_broadcast(3)), (w_in[:, :], A["w_in"]),
                 (pp[:, :], A["phases"][0:T, :]), (ang[:, P:P + NW], A["deltas"].partition_broadcast(T)),
                 (ang[:, 0:P], A["phases"][0:T, :])]
        late = [(S.w1c[0:D, 0:D], A["hop_w1"][0:D, :]), (S.w1p[0:P, 0:D], A["hop_w1"][D:D + P, :]),
                (S.w1c[0:D, D:2 * D], A["ksk_w1"][0:D, :]), (ksk_low[:, :], A["ksk_w1"][D:2 * D, :]),
                (kce_w[:, :], A["kce_w"]), (kce_b[:, :], col(A["kce_b"])), (ksk_b1[D:128, :], col(A["ksk_b1"])),
                (S.b1c[0:D, :], col(A["hop_b1"])), (S.w2c[0:D, 0:ST], A["hop_w2"]), (S.w2c[D:128, ST:GT], A["ksk_w2"]),
                (S.sg_w1[0:D, :], A["sg_w1"]), (S.sg_b1[:, :], col(A["sg_b1"])), (S.sg_w2[:, :], A["sg_w2"]),
                (S.wx[0:D, 0:P], A["cpe_w"]), (S.wx[0:D, P:P + D], A["mc_w"]), (S.wx[0:D, P + D:P + 2 * D], A["ve_w"]),
                (S.proj_b[:, AO:ST], A["hop_b2"].partition_broadcast(128)), (S.proj_b[:, ST:GT], A["ksk_b2"].partition_broadcast(128)),
                (S.proj_b[:, GT:KY], A["sg_b2"].partition_broadcast(128)), (S.proj_b[:, KY:CT], A["cpe_b"].partition_broadcast(128)),
                (S.proj_b[:, CT:VL], A["mc_b"].partition_broadcast(128)), (S.proj_b[:, VL:NPROJ], A["ve_b"].partition_broadcast(128)),
                (ln_g[0:D, :], col(A["ln_g"])), (ln_g[D:128, :], col(A["ln_g"])), (ln_b[:, :], col(A["ln_b"])),
                (out_w[0:D, :], A["out_w"]), (out_w[D:128, :], A["out_w"]), (out_b[:, :], A["out_b"].partition_broadcast(128)),
                (S.b_oah[:, :], A["b_oah"].partition_broadcast(128)),
                (S.wr0[:, :], A["wr0"]), (S.br0[:, :], A["br0"].partition_broadcast(128)),
                (wq[:, :, :], A["wq"].rearrange("h d e -> d h e")), (wk[:, :, :], A["wk"].rearrange("h d e -> d h e")),
                (wo[:, :, :], A["wo"].rearrange("o (h e) -> o h e", e=D)),
                (S.gamma[:, :], col(A["gamma"])), (S.beta[:, :], col(A["beta"])), (S.wr1[:, :], A["wr1"]),
                (S.br1[:, :], A["br1"].partition_broadcast(128)),
                (S.w1_1[0:D, :, :], A["w1_1"].rearrange("e d h -> d e h")), (S.w2_1[:, :, :], A["w2_1"].rearrange("e h d -> h e d")),
                (S.b1_1[:, :], A["b1_1"].rearrange("e h -> h e")), (S.b2_1[:, :], A["b2_1"])]
        n_early, n_late, n_late2 = 16 * len(early), 16 * len(late[0::2]), 16 * len(late[1::2])

        block = ctx.enter_context(nc.Block())

        at = {}

        @block.vector
        def _(dve):
            st = Steps(S, dve_done)
            st.start(dve)
            V, do = nc.vector, st.do

            for t in (S.w1c[D:128, 0:D], S.w1p[0:P, D:128], S.w1p[P:2 * P, :], S.w1p[2 * P:128, :], S.sg_w1[D:128, :], S.wx[D:128, :], S.ppT[P:2 * P, :],
                      S.ppT[2 * P:128, :], S.w2c[0:D, ST:GT], S.w2c[D:128, 0:ST]):
                st.done(V.memset(t, 0.0))
            st.done(V.memset(S.qkT[D:128, :, :, :], 0.0))
            st.done(V.memset(S.w1_1[D:128, :, :], 0.0))
            st.done(V.memset(S.ones_bf[:, :], 1.0))
            st.done(V.memset(S.eps[:, :], EPS))
            st.done(V.memset(S.half_pi[:, :], HALF_PI))
            for r in range(2):
                st.done(V.memset(S.hn[:, r, :, D:D + 1], 1.0))
            dve.wait_ge(early_in, n_early)
            dve.wait_ge(masks_made, 3)
            do(V.tensor_scalar(mask_row[:, :], x_row[:, :], 0.0, None, ALU.not_equal))
            do(V.reduce_sum(seq_len[:, :], mask_row[:, :], AX.X))
            do(V.tensor_scalar(idx_row[:, :], S.iota_free[0:B, :], -1.0, seq_len[:, 0:1], ALU.mult, ALU.add))
            do(V.tensor_tensor(idx_row[:, :], idx_row[:, :], mask_row[:, :], ALU.mult))
            do(V.tensor_scalar(neg_row[:, :], idx_row[:, :], 0.0, float(NPOS), ALU.is_lt, ALU.mult))
            do(V.tensor_tensor(idx_bf[:, :], idx_row[:, :], neg_row[:, :], ALU.add))
            at['idx'] = st.n
            for k in range(4):
                st.done(V.transpose(xT_i[32 * k:32 * k + 32, :], x_row[:, 32 * k:32 * k + 32]))
            st.wait()
            st.done(V.tensor_copy(S.xT[:, :], xT_i[:, :]))
            do(V.tensor_scalar(S.maskT[:, :], xT_i[:, :], 0.0, None, ALU.not_equal))
            do(V.tensor_copy(S.emb3[:, 0, :], S.emb[:, :]))
            do(V.tensor_tensor(emb_rest[:, 0, :], S.emb[:, :], S.emb3[:, 0, :], ALU.subtract))
            do(V.tensor_copy(S.emb3[:, 1, :], emb_rest[:, 0, :]))
            do(V.tensor_tensor(emb_rest[:, 1, :], emb_rest[:, 0, :], S.emb3[:, 1, :], ALU.subtract))
            do(V.tensor_copy(S.emb3[:, 2, :], emb_rest[:, 1, :]))
            do(V.tensor_copy(last_part[:, 0, :], emb_last[:, :]))
            do(V.tensor_tensor(last_rest[:, 0, :], emb_last[:, :], last_part[:, 0, :], ALU.subtract))
            do(V.tensor_copy(last_part[:, 1, :], last_rest[:, 0, :]))
            do(V.tensor_tensor(last_rest[:, 1, :], last_rest[:, 0, :], last_part[:, 1, :], ALU.subtract))
            do(V.tensor_copy(last_part[:, 2, :], last_rest[:, 1, :]))
            do(V.tensor_scalar(emb_low[0:3, :], last_part[:, 0, :], S.ident[0:3, 0:1], None, ALU.mult))
            for k in (1, 2):
                do(V.scalar_tensor_tensor(emb_low[0:3, :], last_part[:, k, :], S.ident[0:3, k:k + 1],
                                          emb_low[0:3, :], ALU.mult, ALU.add))
            do(V.tensor_copy(S.emb_last3[:, :], emb_low[0:3, :]))
            do(V.tensor_copy(S.triS[:, :], triS_f[:, :]))
            do(V.tensor_scalar(rec_row[:, :], S.iota_free[:, :], 1.0, None, ALU.add))
            do(V.reciprocal(rec_row[:, :], rec_row[:, :]))
            do(V.tensor_tensor(S.cmean[:, :], rec_row[:, :], S.triC[:, :], ALU.mult))
            do(V.tensor_tensor(S.nhd2[:, :], ang[:, P:P + NW], ang[:, P:P + NW], ALU.mult))
            do(V.tensor_scalar(S.nhd2[:, :], S.nhd2[:, :], -0.5, None, ALU.mult))
            do(V.tensor_scalar(ang[:, P:P + NW], ang[:, P:P + NW], 0.1, None, ALU.mult))
            do(V.tensor_scalar(turns[:, :], ang[:, :], float(1 / (2 * np.pi)), ROUND, ALU.mult, ALU.add))
            do(V.tensor_scalar(turns[:, :], turns[:, :], -ROUND, None, ALU.add))
            for c in TWO_PI_PARTS:
                do(V.scalar_tensor_tensor(ang[:, :], turns[:, :], -c, ang[:, :], ALU.mult, ALU.add))
            do(V.tensor_scalar(ang[:, :], ang[:, :], PI_BELOW, -PI_BELOW, ALU.min, ALU.max))
            at['angle'] = st.n
            dve.wait_ge(act_done, 3)
            st.done(V.tensor_copy(S.pcs[:, :, :], sincos[:, :, 0:P]))
            st.done(V.tensor_copy(S.dcs[:, :, :], sincos[:, :, P:P + NW]))
            for k in range(2):
                st.done(V.tensor_copy(pdup[:, k, :, :], sincos[:, :, 0:P]))
            at['pdup'] = st.n
            dve.wait_ge(weights_in, n_late)
            dve.wait_ge(weights_in2, n_late2)
            st.done(V.tensor_scalar(S.out_w2[:, :], out_w[:, :], ln_g[:, 0:1], None, ALU.mult))
            st.done(V.tensor_copy(ln_bb[:, :], bc(ln_b[:, 0:1], [D, 128])))
            at['lnbb'] = st.n
            dve.wait_ge(pe_done, 1)
            st.done(V.tensor_copy(S.w_inT[:, :], S.ps[0][0:D, 0:D]))
            st.done(V.tensor_copy(kce_wT[:, :], S.ps[0][0:D, 128:128 + D]))
            st.done(V.tensor_copy(S.pcsT[:, :], S.ps[0][:, 256:384]))
            st.done(V.tensor_copy(S.ppT[0:P, :], S.ps[0][0:P, 384:512]))
            for n, dst in enumerate((wqT, wkT, woT)):
                st.done(V.tensor_copy(dst[:, :, :], S.ps[1 + n][:, 0:NPAR * D].rearrange("p (n d) -> p n d", d=D)))
            at['wT'] = st.n
            dve.wait_ge(pe_done, 2)
            st.done(V.tensor_copy(S.w1c[D:128, D:128], S.ps[0][D:128, 0:D]))
            st.done(V.tensor_tensor(S.b1c[D:128, :], S.ps[0][D:128, 64:65], ksk_b1[D:128, :], ALU.add))
            st.done(V.tensor_tensor(S.out_row[:, :], S.ps[7][:, 0:D], out_b[:, :], ALU.add))
            for par in range(2):
                st.done(V.tensor_copy(S.qkT[0:D, :, par, :], S.ps[1 + par][0:D, 0:NPAR * D].rearrange("p (n d) -> p n d", d=D)))
            for half in range(2):
                st.done(V.tensor_copy(S.wv[64 * half:64 * half + 64, :, :],
                                      S.ps[3 + half][64 * half:64 * half + 64, 0:NPAR * D].rearrange("p (n d) -> p n d", d=D)))

        @block.sync
        def _(sp):
            for dst, src in early:
                sp.dma_start(dst, src, allow_slow_non_contiguous=True).then_inc(early_in, 16)
            for dst, src in late[0::2]:
                sp.dma_start(dst, src, allow_slow_non_contiguous=True).then_inc(weights_in, 16)
            sp.wait_ge(dve_done, at['idx'])
            sp.dma_start(A["idx_scratch"], idx_bf[:, :]).then_inc(idx_out, 16)
            sp.wait_ge(idx_out, 16)
            sp.dma_start(S.idx_bc[:, :].rearrange("p (b t) -> p b t", b=B),
                         A["idx_scratch"].partition_broadcast(128)).then_inc(idx_back, 16)
            sp.wait_ge(idx_back, 16)
            sp.wait_ge(masks_made, 2)
            for r in range(0, S.slots, 128 * 32):
                sp.dma_start(A["slot_x"][r:r + 128 * 32, :].rearrange("(p n) d -> p n d", p=128),
                             S.zeros[:, :].rearrange("p (n d) -> p n d", d=D)).then_inc(zeroed, 16)
            sp.wait_ge(zeroed, 16 * (S.slots // 4096))

        @block.gpsimd
        def _(pool):
            nc.gpsimd.memset(S.ident[:, :], 0.0)
            nc.gpsimd.memset(S.triG[:, :], 1.0)
            nc.gpsimd.memset(S.triC[:, :], 1.0)
            nc.gpsimd.memset(triS_f[:, :], 1.0)
            nc.gpsimd.iota(S.iota_free[:, :], [[1, 128]], base=0, channel_multiplier=0, allow_small_or_imprecise_dtypes=True)
            nc.gpsimd.iota(S.iota_part[:, :], [[0, 1]], base=0, channel_multiplier=1,
                           allow_small_or_imprecise_dtypes=True).then_inc(masks_made, 1)
            nc.gpsimd.memset(S.zeros[:, :], 0.0).then_inc(masks_made, 1)
            pool.wait_ge(masks_made, 1)
            sel = nc.gpsimd.affine_select
            sel(out=S.ident[:, :], in_=S.ident[:, :], compare_op=ALU.not_equal, fill=1.0, base=0,
                pattern=[[-1, 128]], channel_multiplier=1)
            sel(out=S.triG[:, :], in_=S.triG[:, :], compare_op=ALU.is_ge, fill=0.0, base=0,
                pattern=[[-1, 128]], channel_multiplier=1)
            sel(out=S.triC[:, :], in_=S.triC[:, :], compare_op=ALU.is_ge, fill=0.0, base=0,
                pattern=[[1, 128]], channel_multiplier=-1)
            sel(out=triS_f[:, :], in_=triS_f[:, :], compare_op=ALU.is_gt, fill=0.0, base=0,
                pattern=[[1, 128]], channel_multiplier=-1).then_inc(masks_made, 1)
            for dst, src in late[1::2]:
                pool.dma_start(dst, src, allow_slow_non_contiguous=True).then_inc(weights_in2, 16)

        @block.scalar
        def _(act):
            act.wait_ge(dve_done, at['angle'])
            nc.scalar.activation(sincos[:, 1, :], ang[:, :], ACT.Sin).then_inc(act_done, 1)
            nc.scalar.activation(absa[:, :], ang[:, :], ACT.Abs).then_inc(act_done, 1)
            act.wait_ge(act_done, 2)
            nc.scalar.activation(sincos[:, 0, :], absa[:, :], ACT.Sin, bias=S.half_pi[:, 0:1], scale=-1.0).then_inc(act_done, 1)

        @block.tensor
        def _(pe):
            M = nc.tensor.matmul
            pe.wait_ge(weights_in, n_late)
            pe.wait_ge(weights_in2, n_late2)
            pe.wait_ge(masks_made, 3)
            pe.wait_ge(dve_done, at['lnbb'])
            idn = S.ident
            nc.tensor.transpose(S.ps[0][0:D, 0:D], w_in[:, :], idn[0:D, 0:D])
            nc.tensor.transpose(S.ps[0][0:D, 128:128 + D], kce_w[:, :], idn[0:D, 0:D])
            nc.tensor.transpose(S.ps[0][:, 256:384], pdup[:, :, :, :].rearrange("p a b c -> p (a b c)"), idn[:, :])
            nc.tensor.transpose(S.ps[0][0:P, 384:512], pp[:, :], idn[:, :])
            for n, src in enumerate((wq, wk, wo)):
                for k in range(NPAR):
                    last = nc.tensor.transpose(S.ps[1 + n][:, D * k:D * k + D],
                                               src[:, 2 * k:2 * k + 2, :].rearrange("p a b -> p (a b)"), idn[0:D, 0:D])
            last.then_inc(pe_done, 1)
            pe.wait_ge(dve_done, at['wT'])
            M(S.ps[0][D:128, 0:D], kce_wT[:, :], ksk_low[:, :], start=True, stop=True)
            M(S.ps[0][D:128, 64:65], ksk_low[:, :], kce_b[:, :], start=True, stop=True)
            M(S.ps[7][:, 0:D], ln_bb[:, :], out_w[0:D, :], start=True, stop=True)
            for par in range(2):
                rows = slice(64 * par, 64 * par + 64)
                for k in range(NPAR):
                    M(S.ps[1 + par][0:D, D * k:D * k + D], wkT[rows, k, :], wqT[rows, k, :], start=True, stop=True)
                    last = M(S.ps[3 + par][rows, D * k:D * k + D], wkT[rows, k, :], woT[rows, k, :], start=True, stop=True)
            last.then_inc(pe_done, 1)


def layer_norm_stats(nc, S, st, dve, i, rooted):
    V = nc.vector
    two = bass.ds(i * (2 * CH), 2 * CH)
    for k in range(2 * CH):
        st.done(V.bn_stats(S.stats[:, k, :], S.h[:, bass.ds(i * (2 * CH) + k, 1), :].rearrange("p a d -> p (a d)")))
    st.wait()
    for k in range(2 * CH):
        st.done(V.bn_aggr(S.mv[:, k, :], S.stats[:, k, :]))
    st.mark("variance")
    st.wait()
    hold(S, dve, rooted, i + 1)
    st.done(V.tensor_copy(S.mean[:, two], S.mv[:, :, 0]))
    st.do(V.reciprocal(S.rstd[:, two], S.dev[:, :]))


def token_stage(nc, S, A):
    with ExitStack() as ctx:
        sb = lambda n, s, d=F32: ctx.enter_context(nc.sbuf_tensor(n, s, d))
        sem = lambda n: ctx.enter_context(nc.semaphore(n))
        onehot = sb("onehot", [128, 2, W], BF16)
        onehot_last = sb("onehot_last", [3, 2, W], BF16)
        differ = sb("differ", [128, 2, CH, T], I32)
        graph = sb("graph", [128, 2, CH, T])
        pe_sb = sb("pe_sb", [D, 2, CH, T])
        pe_sq = sb("pe_sq", [D, 2, CH, T])
        pe_n = sb("pe_n", [D, 2, CH, T])
        ssq = sb("ssq", [D, 2, CH])
        nrm = sb("nrm", [D, 2, CH])
        wgt = sb("wgt", [128, 2, CH])

        embedded = sem("embedded")
        squared = sem("squared")
        rooted = sem("rooted")
        projected = sem("projected")
        h_copied = sem("hn_copied")
        rooted_h = sem("h_rooted")
        gathered = sem("gathered")
        st = Steps(S, sem("token_steps"), 40)

        block = ctx.enter_context(nc.Block())

        @block.vector
        def _(dve):
            V = nc.vector
            with dve.Fori(0, NCH // 2) as i:
                st.start(dve, i)
                for r in range(2):
                    tok = bass.ds(i * (2 * W) + r * W, W)
                    tiles = bass.ds(i * (2 * CH) + r * CH, CH)
                    st.done(V.tensor_scalar(onehot[:, r, :], S.idx_bc[:, tok], S.iota_part[:, 0:1], None, ALU.is_equal))
                    st.done(V.tensor_scalar(onehot_last[:, r, :], S.idx_bc[0:3, tok], float(T), None, ALU.is_equal))
                    st.mark(("one-hot", r))
                    st.done(V.tensor_tensor(differ[:, r, :, :], S.x_bc[:, tok].rearrange("p (b t) -> p b t", t=T),
                                            bc(S.xT[:, tiles].unsqueeze(2), [128, CH, T]), ALU.bitwise_xor))
                st.wait()
                for r in range(2):
                    st.done(V.scalar_tensor_tensor(graph[:, r, :, :], differ[:, r, :, :], 0.0,
                                                   bc(S.triG[:, :].unsqueeze(1), [128, CH, T]), ALU.is_equal, ALU.mult))
                for r in range(2):
                    hold(S, dve, squared, i * 4 + 2 * r + 2)
                    st.done(V.reduce_sum(ssq[:, r, :], pe_sq[:, r, :, :], AX.X))
                st.mark("summed")
                hold(S, dve, rooted, i + 1)
                st.do(V.tensor_scalar(nrm[:, :, :], nrm[:, :, :], 1e-12, None, ALU.max))
                st.do(V.reciprocal(nrm[:, :, :], nrm[:, :, :]))
                for r in range(2):
                    st.done(V.tensor_tensor(pe_n[:, r, :, :], pe_sb[:, r, :, :],
                                            bc(nrm[:, r, :].unsqueeze(2), [D, CH, T]), ALU.mult))
                    st.mark(("normed", r))
                for r in range(2):
                    tiles = bass.ds(i * (2 * CH) + r * CH, CH)
                    out = S.ps[4 + r][:, 0:CH * (D + 1)].rearrange("p (k d) -> p k d", d=D + 1)
                    hc = S.h[:, tiles, :]
                    hold(S, dve, gathered, i * 2 + r + 1)
                    st.do(V.reciprocal(wgt[:, r, :], out[:, :, D]))
                    st.do(V.tensor_tensor(wgt[:, r, :], wgt[:, r, :], S.maskT[:, tiles], ALU.mult))
                    st.do(V.tensor_tensor(hc, out[:, :, 0:D], bc(wgt[:, r, :].unsqueeze(2), [128, CH, D]), ALU.mult))
                    st.do(V.tensor_tensor(hc, hc, bc(S.b_oah[:, :].unsqueeze(1), [128, CH, D]), ALU.add))
                layer_norm_stats(nc, S, st, dve, i, rooted_h)
                st.end()

        @block.tensor
        def _(pe):
            M = nc.tensor.matmul
            with pe.Fori(0, NCH // 2) as i:
                for r in range(2):
                    st.after(pe, ("one-hot", r), i)
                    for k in range(3):
                        M(S.ps[r][0:D, :], S.emb3[:, k, :], onehot[:, r, :], start=(k == 0), stop=False)
                    M(S.ps[r][0:D, :], S.emb_last3[:, :], onehot_last[:, r, :], start=False, stop=True).then_inc(embedded, 1)
                for r in range(2):
                    st.after(pe, ("normed", r), i)
                    for k in range(CH):
                        last = M(S.ps[2 + r][:, D * k:D * k + D], pe_n[:, r, k, :], S.w_inT[:, :], start=True, stop=True)
                    last.then_inc(projected, 1)
                for r in range(2):
                    hold(S, pe, h_copied, i * 2 + r + 1)
                    for k in range(CH):
                        last = M(S.ps[4 + r][:, (D + 1) * k:(D + 1) * (k + 1)], graph[:, r, k, :], S.hn[:, r, k, :],
                                 start=True, stop=True)
                    last.then_inc(gathered, 1)

        @block.scalar
        def _(act):
            with act.Fori(0, NCH // 2) as i:
                for r in range(2):
                    hold(S, act, embedded, i * 2 + r + 1)
                    src = S.ps[r][0:D, :].rearrange("p (k t) -> p k t", t=T)
                    nc.scalar.activation(pe_sb[:, r, :, :], src, ACT.Copy).then_inc(squared, 1)
                    nc.scalar.activation(pe_sq[:, r, :, :], src, ACT.Square).then_inc(squared, 1)
                st.after(act, "summed", i)
                nc.scalar.activation(nrm[:, :, :], ssq[:, :, :], ACT.Sqrt).then_inc(rooted, 1)
                for r in range(2):
                    hold(S, act, projected, i * 2 + r + 1)
                    nc.scalar.activation(S.hn[:, r, :, 0:D], S.ps[2 + r][:, 0:CH * D].rearrange("p (k d) -> p k d", d=D),
                                         ACT.Copy).then_inc(h_copied, 1)
                st.after(act, "variance", i)
                nc.scalar.activation(S.dev[:, :], S.mv[:, :, 1], ACT.Sqrt, bias=S.eps[:, 0:1]).then_inc(rooted_h, 1)


def project_stage(nc, S, A):
    with ExitStack() as ctx:
        sb = lambda n, s, d=F32: ctx.enter_context(nc.sbuf_tensor(n, s, d))
        sem = lambda n: ctx.enter_context(nc.semaphore(n))
        xr = sb("xr", [128, 2, CH, D])
        xx = sb("xx", [128, 2, W])
        g1 = sb("g1", [128, 2, W])
        g2 = sb("g2", [D // 2, 2, W])

        turned = sem("x_turned")
        xx_copied = sem("xx_copied")
        hidden = sem("hidden")
        gelued = sem("gelued")
        out_ready = sem("proj_ready")
        added = sem("residual_added")
        st = Steps(S, sem("project_steps"), 6)

        block = ctx.enter_context(nc.Block())

        @block.vector
        def _(dve):
            V = nc.vector
            with dve.Fori(0, NCH // 2) as i:
                st.start(dve, i)
                for r in range(2):
                    tiles = bass.ds(i * (2 * CH) + r * CH, CH)
                    st.do(V.tensor_tensor(xr[:, r, :, :], S.h[:, tiles, :], bc(S.mean[:, tiles].unsqueeze(2), [128, CH, D]),
                                          ALU.subtract))
                    st.do(V.tensor_tensor(xr[:, r, :, :], xr[:, r, :, :], bc(S.rstd[:, tiles].unsqueeze(2), [128, CH, D]),
                                          ALU.mult))
                    st.mark(("x", r))
                for r in range(2):
                    tiles = bass.ds(i * (2 * CH) + r * CH, CH)
                    hold(S, dve, out_ready, i * 2 + r + 1)
                    st.done(V.tensor_tensor(S.proj[:, tiles, :], S.bank[:, 4:8, 0:NPROJ],
                                            bc(S.proj_b[:, :].unsqueeze(1), [128, CH, NPROJ]), ALU.add))
                    st.mark(("proj", r))
                hold(S, dve, added, i * 2 + 2)
                st.end()

        @block.gpsimd
        def _(pool):
            with pool.Fori(0, NCH // 2) as i:
                for r in range(2):
                    tiles = bass.ds(i * (2 * CH) + r * CH, CH)
                    st.after(pool, ("x", r), i)
                    nc.gpsimd.tensor_tensor(S.h[:, tiles, :], S.h[:, tiles, :], xr[:, r, :, :], ALU.add).then_inc(added, 1)

        @block.tensor
        def _(pe):
            M = nc.tensor.matmul
            with pe.Fori(0, NCH // 2) as i:
                for r in range(2):
                    st.after(pe, ("x", r), i)
                    for k in range(CH):
                        nc.tensor.transpose(S.ps[r][0:D, T * k:T * k + T], xr[:, r, k, :], S.ident[:, :])
                        last = M(S.ps[r][D:128, T * k:T * k + T], xr[:, r, k, :], S.cmean[:, :], start=True, stop=True)
                    last.then_inc(turned, 1)
                for r in range(2):
                    hold(S, pe, xx_copied, i * 2 + r + 1)
                    M(S.ps[2 + r][:, :], S.w1c[:, :], xx[:, r, :], start=True, stop=False)
                    M(S.ps[2 + r][:, :].rearrange("p (k t) -> p k t", t=T), S.w1p[:, :], bc(S.ppT[:, :].unsqueeze(1), [128, CH, T]),
                      start=False, stop=True)
                    M(S.ps[r][0:D // 2, :], S.sg_w1[:, :], xx[:, r, :], start=True, stop=True).then_inc(hidden, 1)
                for r in range(2):
                    hold(S, pe, gelued, i * 4 + 2 * r + 2)
                    if r == 1:
                        st.after(pe, ("proj", 0), i)
                    for k in range(CH):
                        t = slice(T * k, T * k + T)
                        M(S.ps[4 + k][:, 0:GT], g1[:, r, t], S.w2c[:, :], start=True, stop=True)
                        M(S.ps[4 + k][:, GT:KY], g2[:, r, t], S.sg_w2[:, :], start=True, stop=True)
                        last = M(S.ps[4 + k][:, KY:NPROJ], xx[:, r, t], S.wx[:, :], start=True, stop=True)
                    last.then_inc(out_ready, 1)

        @block.scalar
        def _(act):
            with act.Fori(0, NCH // 2) as i:
                for r in range(2):
                    hold(S, act, turned, i * 2 + r + 1)
                    nc.scalar.activation(xx[:, r, :], S.ps[r][:, :], ACT.Copy).then_inc(xx_copied, 1)
                for r in range(2):
                    hold(S, act, hidden, i * 2 + r + 1)
                    nc.scalar.activation(g1[:, r, :], S.ps[2 + r][:, :], ACT.Gelu, bias=S.b1c[:, 0:1]).then_inc(gelued, 1)
                    nc.scalar.activation(g2[:, r, :], S.ps[r][0:D // 2, :], ACT.Gelu, bias=S.sg_b1[:, 0:1]).then_inc(gelued, 1)


def phase_stage(nc, S, A):
    NA = (NH + 2) * P
    with ExitStack() as ctx:
        sb = lambda n, s, d=F32: ctx.enter_context(nc.sbuf_tensor(n, s, d))
        sem = lambda n: ctx.enter_context(nc.semaphore(n))
        cosn = sb("cosn", [128, B, NA])
        sinn = sb("sinn", [128, B, NA])
        width = sb("width", [128, B, NH])
        gate = sb("gate", [128, B])
        wexp = sb("wexp", [128, B * NH, NW])
        wprod = sb("wprod", [128, 2, B * NH, NW])
        wsum = sb("wsum", [128, B * NH])
        along = sb("along", [128, 2, B * NH])
        kscale = sb("kscale", [128, B])
        t_c = sb("t_c", [128, 2, 2 * CH, NH * P])
        t_s = sb("t_s", [128, 2, 2 * CH, NH * P])
        r_c = sb("r_c", [128, 2, 2 * CH, P])
        r_s = sb("r_s", [128, 2, 2 * CH, P])

        tanhs = sem("tanhs")
        exped = sem("exped")
        rooted = sem("gate_rooted")
        summed = sem("gates_summed")
        trig = sem("trig")
        sized = sem("sized")
        pre = Steps(S, sem("weights_steps"))
        gated = sem("gated")
        st = Steps(S, sem("phase_steps"), 13)
        ps = Steps(S, sem("phase_pool_steps"), 6)
        sines = sem("sines_summed")

        block = ctx.enter_context(nc.Block())

        def combine(eng, st, t, hop, t4, al, first, second, op):
            st.done(eng.tensor_tensor(t4(t, 0), hop(first[0]), al(first[1]), ALU.mult))
            st.do(eng.tensor_tensor(t4(t, 1), hop(second[0]), al(second[1]), ALU.mult))
            st.do(eng.tensor_tensor(t[:, 0, :, :], t[:, 0, :, :], t[:, 1, :, :], op))
            st.do(eng.tensor_tensor(t[:, 0, :, 0:2 * P], t[:, 0, :, 0:2 * P], t[:, 0, :, 2 * P:4 * P], ALU.add))
            return eng.tensor_tensor(t[:, 0, :, 0:P], t[:, 0, :, 0:P], t[:, 0, :, P:2 * P], ALU.add)

        @block.vector
        def _(dve):
            V = nc.vector
            pre.start(dve)
            do = pre.do
            dve.wait_ge(tanhs, 2)
            do(V.tensor_scalar(gate[:, :], gate[:, :], 0.5, 0.5, ALU.mult, ALU.add))
            pre.mark("gate")
            do(V.tensor_scalar(width[:, :, :], width[:, :, :], 1.1, None, ALU.add))
            do(V.tensor_tensor(width[:, :, :], width[:, :, :], width[:, :, :], ALU.mult))
            do(V.tensor_scalar(width[:, :, :], width[:, :, :], 1e-6, None, ALU.add))
            wv = width[:, :, :].rearrange("p b h -> p (b h)")
            do(V.reciprocal(wv, wv))
            do(V.tensor_tensor(wexp[:, :, :], bc(wv.unsqueeze(2), [128, B * NH, NW]),
                               bc(S.nhd2[:, :].unsqueeze(1), [128, B * NH, NW]), ALU.mult))
            pre.mark("exponents")
            dve.wait_ge(summed, 1)
            do(V.tensor_scalar(kscale[:, :], S.ps[0][:, 0:B], 1.0, None, ALU.max))
            pre.mark("gate sum")
            dve.wait_ge(exped, 1)
            do(V.reduce_sum(wsum[:, :], wexp[:, :, :], AX.X))
            do(V.tensor_scalar(wsum[:, :], wsum[:, :], 1e-6, None, ALU.add))
            do(V.reciprocal(wsum[:, :], wsum[:, :]))
            do(V.tensor_scalar(wsum[:, :], wsum[:, :], 1.0 / (NH * P ** 0.5), None, ALU.mult))
            for k in range(2):
                pre.done(V.tensor_tensor(wprod[:, k, :, :], wexp[:, :, :], bc(S.dcs[:, k, :].unsqueeze(1), [128, B * NH, NW]),
                                         ALU.mult))
            pre.wait()
            for k in range(2):
                pre.done(V.reduce_sum(along[:, k, :], wprod[:, k, :, :], AX.X))
            pre.wait()
            for k in range(2):
                pre.done(V.tensor_tensor(along[:, k, :], along[:, k, :], wsum[:, :], ALU.mult))
            dve.wait_ge(rooted, 1)
            do(V.reciprocal(kscale[:, :], kscale[:, :]))
            do(V.tensor_scalar(kscale[:, :], kscale[:, :], 1.0 / P ** 0.5, None, ALU.mult))
            pre.mark("weights")
            with dve.Fori(0, NCH // 2) as i:
                st.start(dve, i)
                two = bass.ds(i * (2 * CH), 2 * CH)
                hop = lambda t: t[:, two, 0:NH * P].rearrange("p b (h f) -> p b h f", f=P)
                t4 = lambda t, k: t[:, k, :, :].rearrange("p b (h f) -> p b h f", f=P)
                al = lambda k: bc(along[:, k, :].rearrange("p (b h) -> p b h", h=NH)[:, two, :].unsqueeze(3),
                                  [128, 2 * CH, NH, P])
                hold(S, dve, trig, i * 2 + 2)
                st.do(combine(nc.vector, st, t_c, hop, t4, al, (cosn, 0), (sinn, 1), ALU.subtract))
                hold(S, dve, sines, i + 1)
                pc = bc(S.pcs[:, 0, :].unsqueeze(1), [128, 2 * CH, P])
                pn = bc(S.pcs[:, 1, :].unsqueeze(1), [128, 2 * CH, P])
                st.done(V.tensor_tensor(r_c[:, 0, :, :], t_c[:, 0, :, 0:P], pc, ALU.mult))
                st.done(V.tensor_tensor(r_c[:, 1, :, :], t_s[:, 0, :, 0:P], pn, ALU.mult))
                st.done(V.tensor_tensor(r_s[:, 0, :, :], t_c[:, 0, :, 0:P], pn, ALU.mult))
                st.do(V.tensor_tensor(r_s[:, 1, :, :], t_s[:, 0, :, 0:P], pc, ALU.mult))
                st.mark("turned")
                st.done(V.tensor_tensor(S.q_pos[:, two, 0:P], r_c[:, 0, :, :], r_c[:, 1, :, :], ALU.subtract))
                st.done(V.tensor_tensor(S.q_pos[:, two, P:2 * P], r_s[:, 0, :, :], r_s[:, 1, :, :], ALU.add))
                ks = bc(kscale[:, two].unsqueeze(2), [128, 2 * CH, P])
                ky = slice((NH + 1) * P, (NH + 2) * P)
                st.done(V.tensor_tensor(S.q_kv[:, two, 0:P], cosn[:, two, ky], ks, ALU.mult))
                st.done(V.tensor_tensor(S.q_kv[:, two, P:2 * P], sinn[:, two, ky], ks, ALU.mult))
                st.wait()
                st.end()

        @block.gpsimd
        def _(pool):
            G = nc.gpsimd
            pre.after(pool, "gate")
            pool.wait_ge(tanhs, 3)
            G.tensor_tensor(S.gv[:, :, :], S.proj[:, :, VL:NPROJ], bc(gate[:, :].unsqueeze(2), [128, B, D]),
                            ALU.mult).then_inc(gated, 1)
            pre.after(pool, "weights")
            with pool.Fori(0, NCH // 2) as i:
                ps.start(pool, i)
                two = bass.ds(i * (2 * CH), 2 * CH)
                hop = lambda t: t[:, two, 0:NH * P].rearrange("p b (h f) -> p b h f", f=P)
                t4 = lambda t, k: t[:, k, :, :].rearrange("p b (h f) -> p b h f", f=P)
                al = lambda k: bc(along[:, k, :].rearrange("p (b h) -> p b h", h=NH)[:, two, :].unsqueeze(3),
                                  [128, 2 * CH, NH, P])
                hold(S, pool, trig, i * 2 + 2)
                combine(nc.gpsimd, ps, t_s, hop, t4, al, (cosn, 1), (sinn, 0), ALU.add).then_inc(sines, 1)
                so = slice(NH * P, (NH + 1) * P)
                ps.done(G.tensor_copy(S.k_kv[:, two, 0:P], cosn[:, two, so]))
                ps.done(G.tensor_copy(S.k_kv[:, two, P:2 * P], sinn[:, two, so]))
                st.after(pool, "turned", i)
                ps.end()

        @block.tensor
        def _(pe):
            pre.after(pe, "gate")
            nc.tensor.matmul(S.ps[0][:, 0:B], S.triC[:, :], gate[:, :], start=True, stop=True).then_inc(summed, 1)

        @block.scalar
        def _(act):
            N = nc.scalar.activation
            N(width[:, :, :], S.proj[:, :, AO:ST].rearrange("p b (h f) -> p b h f", f=HP)[:, :, :, P], ACT.Tanh,
              scale=0.5).then_inc(tanhs, 1)
            N(gate[:, :], S.proj[:, :, GT], ACT.Tanh, scale=0.5).then_inc(tanhs, 1)
            N(cosn[:, :, 0:NH * P].rearrange("p b (h f) -> p b h f", f=P),
              S.proj[:, :, AO:ST].rearrange("p b (h f) -> p b h f", f=HP)[:, :, :, 0:P], ACT.Tanh)
            N(cosn[:, :, NH * P:(NH + 1) * P], S.proj[:, :, ST:GT], ACT.Tanh)
            N(cosn[:, :, (NH + 1) * P:NA], S.proj[:, :, KY:CT], ACT.Tanh).then_inc(tanhs, 1)
            pre.after(act, "exponents")
            N(wexp[:, :, :], wexp[:, :, :], ACT.Exp).then_inc(exped, 1)
            pre.after(act, "gate sum")
            N(kscale[:, :], kscale[:, :], ACT.Sqrt).then_inc(rooted, 1)
            act.wait_ge(tanhs, 3)
            with act.Fori(0, NCH // 2) as i:
                two = bass.ds(i * (2 * CH), 2 * CH)
                N(sinn[:, two, :], cosn[:, two, :], ACT.Sin, scale=PI_BELOW).then_inc(trig, 1)
                N(cosn[:, two, :], cosn[:, two, :], ACT.Abs).then_inc(sized, 1)
                hold(S, act, sized, i + 1)
                N(cosn[:, two, :], cosn[:, two, :], ACT.Sin, scale=-PI_BELOW, bias=S.half_pi[:, 0:1]).then_inc(trig, 1)


def memory_stage(nc, S, A):
    NPRS = CH // 2
    with ExitStack() as ctx:
        sb = lambda n, s, d=F32: ctx.enter_context(nc.sbuf_tensor(n, s, d))
        sem = lambda n: ctx.enter_context(nc.semaphore(n))
        rows = sb("qk_rows", [128, 2, 3, CH * D])
        qkT = sb("qk_turned", [128, 2, 3, NPRS, T])
        masked = sb("masked", [128, 2, 2, 2 * NPRS, T])
        comb = sb("comb", [128, 2, CH, D])
        combT = sb("combT", [128, 2, NPRS, T])
        stats = sb("comb_stats", [128, 2 * CH, 6])
        mv = sb("comb_mv", [128, 2, CH, 2])
        dev = sb("comb_dev", [128, 2, CH])

        copied = sem("rows_copied")
        turned = sem("qk_turned")
        evacuated = sem("qkT_copied")
        scored = sem("scored")
        retrieved = sem("retrieved")
        rooted = sem("comb_rooted")
        comb_turned = sem("comb_turned")
        combT_copied = sem("combT_copied")
        out_ready = sem("out_ready")
        biased = sem("h_biased")
        rooted_h = sem("h_rooted")
        st = Steps(S, sem("memory_steps"), 4 + 8 + 8 + 1 + 4 + 4 + 18)

        block = ctx.enter_context(nc.Block())

        @block.vector
        def _(dve):
            V = nc.vector
            with dve.Fori(0, NCH // 2) as i:
                st.start(dve, i)
                for r in range(2):
                    hold(S, dve, scored, i * 2 + r + 1)
                    for a in range(2):
                        st.done(V.tensor_tensor(masked[:, r, a, :, :], S.ps[4 + 2 * r + a][:, :].rearrange("p (n t) -> p n t", t=T),
                                                bc(S.triC[:, :].unsqueeze(1), [128, 2 * NPRS, T]), ALU.mult))
                    st.mark(("masked", r))
                for r in range(2):
                    hold(S, dve, retrieved, i * 2 + r + 1)
                    for t in range(CH):
                        st.done(V.bn_stats(stats[:, CH * r + t, :], S.ps[r][:, D * t:D * t + D]))
                st.wait()
                for r in range(2):
                    for t in range(CH):
                        st.done(V.bn_aggr(mv[:, r, t, :], stats[:, CH * r + t, :]))
                st.mark("comb variance")
                hold(S, dve, rooted, i + 1)
                st.do(V.reciprocal(dev[:, :, :], dev[:, :, :]))
                for r in range(2):
                    st.do(V.tensor_tensor(comb[:, r, :, :], S.ps[r][:, 0:CH * D].rearrange("p (k d) -> p k d", d=D),
                                          bc(mv[:, r, :, 0].unsqueeze(2), [128, CH, D]), ALU.subtract))
                    st.do(V.tensor_tensor(comb[:, r, :, :], comb[:, r, :, :], bc(dev[:, r, :].unsqueeze(2), [128, CH, D]),
                                          ALU.mult))
                    st.mark(("comb", r))
                hold(S, dve, biased, i + 1)
                hv = S.h[:, :, :].rearrange("p (n j a) d -> p n a j d", j=NPRS, a=2)
                for r in range(2):
                    hold(S, dve, out_ready, i * 2 + r + 1)
                    for a in range(2):
                        hh = hv[:, bass.ds(i * 2 + r, 1), a, :, :].rearrange("p n j d -> p (n j) d")
                        st.done(V.tensor_tensor(hh, hh, S.ps[4 + 2 * r + a][:, 0:NPRS * D].rearrange("p (j d) -> p j d", d=D),
                                                ALU.add))
                st.wait()
                layer_norm_stats(nc, S, st, dve, i, rooted_h)
                st.end()

        @block.gpsimd
        def _(pool):
            with pool.Fori(0, NCH // 2) as i:
                for r in range(2):
                    tiles = bass.ds(i * (2 * CH) + r * CH, CH)
                    for k, src in enumerate((S.q_pos, S.q_kv, S.k_kv)):
                        nc.gpsimd.tensor_copy(rows[:, r, k, :].rearrange("p (b d) -> p b d", d=D),
                                              src[:, tiles, :]).then_inc(copied, 1)
                two = bass.ds(i * (2 * CH), 2 * CH)
                nc.gpsimd.tensor_tensor(S.h[:, two, :], S.h[:, two, :], bc(S.out_row[:, :].unsqueeze(1), [128, 2 * CH, D]),
                                        ALU.add).then_inc(biased, 1)
                hold(S, pool, turned, i * 2 + 2)

        @block.tensor
        def _(pe):
            M = nc.tensor.matmul
            with pe.Fori(0, NCH // 2) as i:
                for r in range(2):
                    hold(S, pe, copied, i * 6 + 3 * r + 3)
                    for k in range(3):
                        for j in range(NPRS):
                            at = (2 * k + j) * T
                            last = nc.tensor.transpose(S.ps[r if k < 2 else 2 + r][:, at % 512:at % 512 + T],
                                                       rows[:, r, k, 128 * j:128 * j + 128], S.ident[:, :])
                    last.then_inc(turned, 1)
                for r in range(2):
                    hold(S, pe, evacuated, i * 4 + 2 * r + 2)
                    for a in range(2):
                        half = slice(64 * a, 64 * a + 64)
                        M(S.ps[4 + 2 * r + a][:, 0:2 * T], S.pcsT[half, :],
                          qkT[half, r, 0, :, :].rearrange("p j t -> p (j t)"), start=True, stop=True)
                        for j in range(NPRS):
                            last = M(S.ps[4 + 2 * r + a][:, (2 + j) * T:(3 + j) * T], qkT[half, r, 2, j, :],
                                     qkT[half, r, 1, j, :], start=True, stop=True)
                    last.then_inc(scored, 1)
                for r in range(2):
                    st.after(pe, ("masked", r), i)
                    for t in range(CH):
                        j, a = t // 2, t % 2
                        tile = bass.ds(i * (2 * CH) + r * CH + t, 1)
                        M(S.ps[r][:, D * t:D * t + D], masked[:, r, a, j, :],
                          S.proj[:, tile, CT:VL].rearrange("p a d -> p (a d)"), start=True, stop=False)
                        last = M(S.ps[r][:, D * t:D * t + D], masked[:, r, a, 2 + j, :],
                                 S.gv[:, tile, :].rearrange("p a d -> p (a d)"), start=False, stop=True)
                    last.then_inc(retrieved, 1)
                for r in range(2):
                    st.after(pe, ("comb", r), i)
                    for j in range(NPRS):
                        last = nc.tensor.transpose(S.ps[2 + r][:, T * j:T * j + T],
                                                   comb[:, r, 2 * j:2 * j + 2, :].rearrange("p b d -> p (b d)"), S.ident[:, :])
                    last.then_inc(comb_turned, 1)
                for r in range(2):
                    hold(S, pe, combT_copied, i * 2 + r + 1)
                    for a in range(2):
                        half = slice(64 * a, 64 * a + 64)
                        for j in range(NPRS):
                            last = M(S.ps[4 + 2 * r + a][:, D * j:D * j + D], combT[half, r, j, :], S.out_w2[half, :],
                                     start=True, stop=True)
                    last.then_inc(out_ready, 1)

        @block.scalar
        def _(act):
            N = nc.scalar.activation
            with act.Fori(0, NCH // 2) as i:
                for r in range(2):
                    hold(S, act, turned, i * 2 + r + 1)
                    N(qkT[:, r, 0:2, :, :].rearrange("p k j t -> p (k j t)"), S.ps[r][:, :], ACT.Copy).then_inc(evacuated, 1)
                    N(qkT[:, r, 2, :, :].rearrange("p j t -> p (j t)"), S.ps[2 + r][:, 0:2 * T], ACT.Copy).then_inc(evacuated, 1)
                st.after(act, "comb variance", i)
                N(dev[:, :, :], mv[:, :, :, 1], ACT.Sqrt, bias=S.eps[:, 0:1]).then_inc(rooted, 1)
                for r in range(2):
                    hold(S, act, comb_turned, i * 2 + r + 1)
                    N(combT[:, r, :, :].rearrange("p j t -> p (j t)"), S.ps[2 + r][:, 0:2 * T], ACT.Copy).then_inc(combT_copied, 1)
                st.after(act, "variance", i)
                N(S.dev[:, :], S.mv[:, :, 1], ACT.Sqrt, bias=S.eps[:, 0:1]).then_inc(rooted_h, 1)


def normalise(nc, S, st, dst, tiles):
    V = nc.vector
    st.do(V.tensor_tensor(dst, S.h[:, tiles, :], bc(S.mean[:, tiles].unsqueeze(2), [128, CH, D]), ALU.subtract))
    st.do(V.tensor_tensor(dst, dst, bc(S.rstd[:, tiles].unsqueeze(2), [128, CH, D]), ALU.mult))


def route_stage(nc, S, A):
    with ExitStack() as ctx:
        sb = lambda n, s, d=F32: ctx.enter_context(nc.sbuf_tensor(n, s, d))
        sem = lambda n: ctx.enter_context(nc.semaphore(n))
        xr = sb("xr0", [128, 2, CH, D])
        xT = sb("xT0", [D, 2, W])
        logits = sb("logits", [128, 2, CH, E0])
        top = sb("top", [128, 2, CH, 8])
        top_i = sb("top_i", [128, 2, CH, 8], U32)
        top_f = sb("top_f", [128, 2, CH, 2])
        hot = sb("hot", [128, 2, B, E0], BF16)
        both = sb("both", [128, B, E0], BF16)
        total = sb("total", [128, E0, B])
        before = sb("before", [128, E0, B])
        carry = sb("carry", [128, E0, B])
        slot_m = sb("slot_m", [128, B, E0])
        picked = sb("picked", [128, 2, B, E0])
        n_tiles = sb("n_tiles", [128, E0])
        ends = sb("ends", [128, E0])
        base = sb("base", [128, E0])
        slot_f = sb("slot_f", [128, 2, B])
        past = sb("past", [128, E0])
        first_slot = sb("first_slot", [128, 1])
        owner = sb("owner", [128, 1])
        comb = sb("comb0", [128, 2, CH, E0])
        comb2 = sb("comb20", [128, 2, CH, E0])
        combT = sb("combT0", [E0, 2, W])

        turned = sem("x_turned0")
        xT_copied = sem("xT_copied0")
        scored = sem("router_scored")
        kept = sem("x_kept")
        st = Steps(S, sem("route_steps"), 4 + 2 + 8 + 8 + 2 + 6 + 2)
        sl = Steps(S, sem("slot_steps"))
        counted = sem("counted")
        exped = sem("gate_exped")
        owner_turned = sem("owner_turned")
        scattered = [sem(f"scattered{k}") for k in range(2)]
        cb = Steps(S, sem("b2_steps"), 8)
        c_turned = sem("comb0_turned")
        c_copied = sem("comb0_copied")
        b2_ready = sem("b2_ready")

        block = ctx.enter_context(nc.Block())

        @block.sync
        def _(sp):
            sp.dma_start(S.w1_0[0:D, :, :], A["w1_0"].rearrange("e d h -> d e h")).then_inc(S.experts_in, 16)
            sp.dma_start(S.w1_0[D:D + 1, :, :].rearrange("p e h -> p (e h)"), A["b1_0"].rearrange("(o e) h -> o (e h)", o=1)
                         ).then_inc(S.experts_in, 16)
            sp.dma_start(S.w2_0[:, :, :], A["w2_0"].rearrange("e h d -> h e d")).then_inc(S.experts_in, 16)
            sp.dma_start(S.b2_0[:, :], A["b2_0"]).then_inc(S.experts_in, 16)

        @block.vector
        def _(dve):
            V = nc.vector
            with dve.Fori(0, NCH // 2) as i:
                st.start(dve, i)
                for r in range(2):
                    normalise(nc, S, st, xr[:, r, :, :], bass.ds(i * (2 * CH) + r * CH, CH))
                    st.mark(("x", r))
                for r in range(2):
                    hold(S, dve, scored, i * 2 + r + 1)
                    st.do(V.tensor_tensor(logits[:, r, :, :], S.ps[2 + r][:, 0:CH * E0].rearrange("p (k e) -> p k e", e=E0),
                                          bc(S.br0[:, :].unsqueeze(1), [128, CH, E0]), ALU.add))
                    for k in range(CH):
                        st.done(V.max(top[:, r, k, :], logits[:, r, k, :]))
                    st.wait()
                    for k in range(CH):
                        st.done(V.max_index(top_i[:, r, k, :], top[:, r, k, :], logits[:, r, k, :]))
                    st.wait()
                    st.do(V.tensor_copy(top_f[:, r, :, :], top_i[:, r, :, 0:2]))
                for r in range(2):
                    tiles = bass.ds(i * (2 * CH) + r * CH, CH)
                    for c in range(2):
                        st.done(V.tensor_tensor(hot[:, c, tiles, :], bc(S.iota_free[:, 0:E0].unsqueeze(1), [128, CH, E0]),
                                                bc(top_f[:, r, :, c:c + 1], [128, CH, E0]), ALU.is_equal))
                    st.done(V.tensor_tensor(S.gates[:, 1, tiles], top[:, r, :, 1], top[:, r, :, 0], ALU.subtract))
                st.wait()
                for r in range(2):
                    tiles = bass.ds(i * (2 * CH) + r * CH, CH)
                    st.done(V.tensor_tensor(both[:, tiles, :], hot[:, 0, tiles, :], hot[:, 1, tiles, :], ALU.add))
                hold(S, dve, kept, i * 2 + 2)
                st.wait()
                st.end()
            sl.start(dve)
            do = sl.do
            do(V.memset(carry[:, :, :], 1.0))
            do(V.memset(carry[:, :, 0:1], 0.0))
            sl.mark("routed")
            dve.wait_ge(exped, 1)
            do(V.tensor_scalar(S.gates[:, 0, :], S.gates[:, 1, :], 1.0, None, ALU.add))
            do(V.reciprocal(S.gates[:, 0, :], S.gates[:, 0, :]))
            do(V.tensor_tensor(S.gates[:, 1, :], S.gates[:, 1, :], S.gates[:, 0, :], ALU.mult))
            dve.wait_ge(counted, 2)
            do(V.tensor_copy(total[:, :, :].rearrange("p e (n b) -> p n b e", n=4),
                             S.bank[:, 4:8, :].rearrange("p n (b e) -> p n b e", e=E0)))
            do(V.tensor_tensor_scan(before[:, :, :].rearrange("p e b -> p (e b)"), carry[:, :, :].rearrange("p e b -> p (e b)"),
                                    total[:, :, :].rearrange("p e b -> p (e b)"), 0.0, ALU.mult, ALU.add))
            do(V.tensor_scalar(n_tiles[:, :], before[:, :, B - 1], 1.0 / 128, 63.5 / 128, ALU.mult, ALU.add))
            do(V.tensor_scalar(n_tiles[:, :], n_tiles[:, :], ROUND, None, ALU.add))
            do(V.tensor_scalar(n_tiles[:, :], n_tiles[:, :], -ROUND, 128.0, ALU.add, ALU.mult))
            do(V.tensor_tensor_scan(ends[:, :], bc(carry[:, 0, 1:2], [128, E0]),
                                    n_tiles[:, :], 0.0, ALU.mult, ALU.add))
            do(V.tensor_tensor(base[:, :], ends[:, :], n_tiles[:, :], ALU.subtract))
            do(V.tensor_tensor(before[:, :, :], before[:, :, :], total[:, :, :], ALU.subtract))
            do(V.tensor_tensor(before[:, :, :], before[:, :, :], bc(base[:, :].unsqueeze(2), [128, E0, B]), ALU.add))
            do(V.tensor_tensor(slot_m[:, :, :].rearrange("p (n b) e -> p n b e", n=4),
                               S.bank[:, 0:4, :].rearrange("p n (b e) -> p n b e", e=E0),
                               before[:, :, :].rearrange("p e (n b) -> p n b e", n=4), ALU.add))
            for c in range(2):
                sl.done(V.tensor_tensor(picked[:, c, :, :], hot[:, c, :, :], slot_m[:, :, :], ALU.mult))
            sl.wait()
            for c in range(2):
                sl.done(V.reduce_sum(slot_f[:, c, :], picked[:, c, :, :], AX.X))
            sl.wait()
            do(V.tensor_copy(S.slot_u[:, :, :], slot_f[:, :, :]))
            sl.mark("slots")
            do(V.tensor_scalar(first_slot[:, :], S.iota_part[:, :], 128.0, None, ALU.mult))
            do(V.tensor_scalar(past[:, :], ends[:, :], first_slot[:, 0:1], None, ALU.is_le))
            do(V.reduce_sum(owner[:, :], past[:, :], AX.X))
            do(V.tensor_scalar(owner[:, :], owner[:, :], float(E0 - 1), None, ALU.min))
            sl.mark("owner")
            dve.wait_ge(owner_turned, 1)
            do(V.tensor_copy(S.owner_row[:, :], S.ps[0][0:1, 0:128]))
            sl.mark("owner row")
            with dve.Fori(0, NCH // 2) as i:
                cb.start(dve, i)
                for r in range(2):
                    tiles = bass.ds(i * (2 * CH) + r * CH, CH)
                    cb.done(V.tensor_tensor(comb[:, r, :, :], hot[:, 0, tiles, :],
                                            bc(S.gates[:, 0, tiles].unsqueeze(2), [128, CH, E0]), ALU.mult))
                    cb.do(V.tensor_tensor(comb2[:, r, :, :], hot[:, 1, tiles, :],
                                          bc(S.gates[:, 1, tiles].unsqueeze(2), [128, CH, E0]), ALU.mult))
                    cb.do(V.tensor_tensor(comb[:, r, :, :], comb[:, r, :, :], comb2[:, r, :, :], ALU.add))
                    cb.mark(("comb", r))
                for r in range(2):
                    tiles = bass.ds(i * (2 * CH) + r * CH, CH)
                    hold(S, dve, b2_ready, i * 2 + r + 1)
                    cb.do(V.tensor_tensor(S.h[:, tiles, :], S.h[:, tiles, :],
                                          S.ps[4 + r][:, 0:CH * D].rearrange("p (k d) -> p k d", d=D), ALU.add))
                cb.end()

        @block.gpsimd
        def _(pool):
            with pool.Fori(0, NCH // 2) as i:
                for r in range(2):
                    st.after(pool, ("x", r), i)
                    nc.gpsimd.tensor_copy(S.xn[:, bass.ds(i * (2 * CH) + r * CH, CH), :], xr[:, r, :, :]).then_inc(kept, 1)
            sl.after(pool, "slots")
            pool.wait_ge(kept, NCH)
            for b in range(B):
                for c in range(2):
                    nc.gpsimd.indirect_dma_start(A["slot_x"], bass.IndirectOffsetOnAxis(ap=S.slot_u[:, c, b:b + 1], axis=0),
                                                 S.xn[:, b, :], None).then_inc(scattered[c], 16)
            for c in range(2):
                pool.wait_ge(scattered[c], 16 * B)

        @block.tensor
        def _(pe):
            M = nc.tensor.matmul
            with pe.Fori(0, NCH // 2) as i:
                for r in range(2):
                    st.after(pe, ("x", r), i)
                    for k in range(CH):
                        last = nc.tensor.transpose(S.ps[r][0:D, T * k:T * k + T], xr[:, r, k, :], S.ident[:, :])
                    last.then_inc(turned, 1)
                for r in range(2):
                    hold(S, pe, xT_copied, i * 2 + r + 1)
                    for k in range(CH):
                        last = M(S.ps[2 + r][:, E0 * k:E0 * k + E0], xT[:, r, T * k:T * k + T], S.wr0[:, :], start=True, stop=True)
                    last.then_inc(scored, 1)
            sl.after(pe, "routed")
            for n in range(4):
                last = M(S.ps[n][:, :], S.triS[:, :], both[:, 8 * n:8 * n + 8, :].rearrange("p b e -> p (b e)"),
                         start=True, stop=True)
            last.then_inc(counted, 1)
            for n in range(4):
                last = M(S.ps[4 + n][:, :], S.ones_bf[:, :], both[:, 8 * n:8 * n + 8, :].rearrange("p b e -> p (b e)"),
                         start=True, stop=True)
            last.then_inc(counted, 1)
            sl.after(pe, "owner")
            nc.tensor.transpose(S.ps[0][0:1, 0:128], owner[:, :], S.ident[:, :]).then_inc(owner_turned, 1)
            sl.after(pe, "owner row")
            pe.wait_ge(S.experts_in, 64)
            with pe.Fori(0, NCH // 2) as i:
                for r in range(2):
                    cb.after(pe, ("comb", r), i)
                    for k in range(CH):
                        last = nc.tensor.transpose(S.ps[r][0:E0, T * k:T * k + T], comb[:, r, k, :], S.ident[:, :])
                    last.then_inc(c_turned, 1)
                for r in range(2):
                    hold(S, pe, c_copied, i * 2 + r + 1)
                    for k in range(CH):
                        last = M(S.ps[4 + r][:, D * k:D * k + D], combT[:, r, T * k:T * k + T], S.b2_0[:, :], start=True, stop=True)
                    last.then_inc(b2_ready, 1)

        @block.scalar
        def _(act):
            N = nc.scalar.activation
            with act.Fori(0, NCH // 2) as i:
                for r in range(2):
                    hold(S, act, turned, i * 2 + r + 1)
                    N(xT[:, r, :], S.ps[r][0:D, :], ACT.Copy).then_inc(xT_copied, 1)
            sl.after(act, "routed")
            N(S.gates[:, 1, :], S.gates[:, 1, :], ACT.Exp).then_inc(exped, 1)
            with act.Fori(0, NCH // 2) as i:
                for r in range(2):
                    hold(S, act, c_turned, i * 2 + r + 1)
                    N(combT[:, r, :], S.ps[r][0:E0, :], ACT.Copy).then_inc(c_copied, 1)


def experts_stage(nc, S, A):
    NG = S.slots // W
    with ExitStack() as ctx:
        sb = lambda n, s, d=F32: ctx.enter_context(nc.sbuf_tensor(n, s, d))
        sem = lambda n: ctx.enter_context(nc.semaphore(n))
        xs = sb("xs", [128, 2, CH, D])
        xsT = sb("xsT", [128, 2, W])
        w1e = sb("w1e", [128, 2, CH, HID])
        w2e = sb("w2e", [HID, 2, CH, D])
        hidT = sb("hidT", [HID, 2, CH, 128])
        ys = sb("ys", [128, 2, CH, D])

        loaded = [sem(f"slots_loaded{r}") for r in range(2)]
        stored = [sem(f"slots_stored{r}") for r in range(2)]
        turned = sem("slots_turned")
        padded = sem("padded")
        xsT_copied = sem("xsT_copied")
        w1_copied = sem("w1_copied")
        w2_copied = sem("w2_copied")
        h_ready = sem("h_ready")
        relued = sem("relued")
        y_ready = sem("y_ready")
        y_copied = sem("y_copied")

        rows_in = A["slot_x"].rearrange("(g k p) d -> g p k d", k=CH, p=128)
        rows_out = A["slot_y"].rearrange("(g k p) d -> g p k d", k=CH, p=128)
        owners = lambda eng, g, n: nc.values_load_multi_w_load_instructions(
            S.owner_row[0:1, bass.ds(g * CH, n)], engines=(eng.engine,), min_val=0, max_val=E0 - 1)[1]
        block = ctx.enter_context(nc.Block())

        @block.sync
        def _(sp):
            for r in range(2):
                sp.dma_start(xs[:, r, :, :], rows_in[r]).then_inc(loaded[r], 16)
            with sp.Fori(0, NG // 2 - 1) as i:
                for r in range(2):
                    hold(S, sp, turned, i * 2 + r + 1)
                    sp.dma_start(xs[:, r, :, :], rows_in[bass.ds(i * 2 + r + 2, 1)].rearrange("g p k d -> (g p) k d")
                                 ).then_inc(loaded[r], 16)

        @block.tensor
        def _(pe):
            M = nc.tensor.matmul

            def turn_rows(i):
                for r in range(2):
                    hold(S, pe, loaded[r], i * 16 + 16)
                    for k in range(CH):
                        last = nc.tensor.transpose(S.ps[r][0:D, T * k:T * k + T], xs[:, r, k, :], S.ident[:, :])
                    last.then_inc(turned, 1)

            def turn(i, more):
                for r in range(2):
                    hold(S, pe, xsT_copied, i * 2 + r + 1)
                    for k in range(CH):
                        if k == 0:
                            hold(S, pe, w1_copied, (i * 2 + r) * CH + CH)
                        last = M(S.ps[2 + r][:, T * k:T * k + T], w1e[:, r, k, :], xsT[:, r, T * k:T * k + T],
                                 start=True, stop=True)
                    last.then_inc(h_ready, 1)
                if more:
                    turn_rows(i + 1)
                for r in range(2):
                    hold(S, pe, relued, i * 2 + r + 1)
                    hold(S, pe, w2_copied, (i * 2 + r) * CH + CH)
                    hold(S, pe, y_copied, i * 2 + r + 1)
                    for k in range(CH):
                        last = M(S.ps[4 + r][:, D * k:D * k + D], hidT[:, r, k, :], w2e[:, r, k, :], start=True, stop=True)
                    last.then_inc(y_ready, 1)

            pe.wait_ge(padded, 3)
            turn_rows(0)
            with pe.Fori(0, NG // 2 - 1) as i:
                turn(i, True)
            turn(NG // 2 - 1, False)

        @block.scalar
        def _(act):
            N = nc.scalar.activation

            def copy_rows(i):
                for r in range(2):
                    hold(S, act, turned, i * 2 + r + 1)
                    N(xsT[0:D, r, :], S.ps[r][0:D, :], ACT.Copy).then_inc(xsT_copied, 1)

            def turn(i, more):
                if more:
                    copy_rows(i + 1)
                for r in range(2):
                    hold(S, act, y_ready, i * 2 + r + 1)
                    hold(S, act, stored[r], i * 16 + 16)
                    N(ys[:, r, :, :], S.ps[4 + r][:, 0:CH * D].rearrange("p (k d) -> p k d", d=D), ACT.Copy).then_inc(y_copied, 1)
                    hold(S, act, y_copied, i * 2 + r + 3)
                    act.dma_start(rows_out[bass.ds(i * 2 + r, 1)].rearrange("g p k d -> (g p) k d"), ys[:, r, :, :]
                                  ).then_inc(stored[r], 16)

            act.sem_inc(y_copied, 2)
            for r in range(2):
                act.sem_inc(stored[r], 16)
            copy_rows(0)
            with act.Fori(0, NG // 2 - 1) as i:
                turn(i, True)
            turn(NG // 2 - 1, False)
            for r in range(2):
                act.wait_ge(stored[r], 16 * (NG // 2) + 16)

        @block.vector
        def _(dve):
            V = nc.vector

            def copy_w2(experts, r):
                for k in range(CH):
                    V.tensor_copy(w2e[:, r, k, :], S.w2_0[:, bass.ds(experts[r * CH + k], 1), :].rearrange("p a d -> p (a d)")
                                  ).then_inc(w2_copied, 1)

            def turn(i, more):
                for r in range(2):
                    hold(S, dve, h_ready, i * 2 + r + 1)
                    V.tensor_scalar(hidT[:, r, :, :].rearrange("p k t -> p (k t)"), S.ps[2 + r][:, :], 0.0, None,
                                    ALU.max).then_inc(relued, 1)
                if more:
                    experts = owners(dve, i * 2 + 2, 2 * CH)
                    for r in range(2):
                        hold(S, dve, y_ready, i * 2 + r + 1)
                        copy_w2(experts, r)

            V.memset(w1e[D:128, :, :, :], 0.0).then_inc(padded, 1)
            V.memset(xsT[D:128, :, :], 0.0).then_inc(padded, 1)
            dve.wait_ge(padded, 2)
            V.memset(xsT[D:D + 1, :, :], 1.0).then_inc(padded, 1)
            dve.wait_ge(S.experts_in, 64)
            experts = owners(dve, 0, 2 * CH)
            for r in range(2):
                copy_w2(experts, r)
            with dve.Fori(0, NG // 2 - 1) as i:
                turn(i, True)
            turn(NG // 2 - 1, False)

        @block.gpsimd
        def _(pool):
            def copy_w1(experts, r):
                for k in range(CH):
                    nc.gpsimd.tensor_copy(w1e[0:D + 1, r, k, :], S.w1_0[:, bass.ds(experts[r * CH + k], 1), :].rearrange("p a h -> p (a h)")
                                          ).then_inc(w1_copied, 1)

            pool.wait_ge(padded, 3)
            pool.wait_ge(S.experts_in, 64)
            experts = owners(pool, 0, 2 * CH)
            for r in range(2):
                copy_w1(experts, r)
            with pool.Fori(0, NG // 2 - 1) as i:
                experts = owners(pool, i * 2 + 2, 2 * CH)
                for r in range(2):
                    hold(S, pool, h_ready, i * 2 + r + 1)
                    copy_w1(experts, r)


def grouped_stage(nc, S, A):
    NU = 2
    UH = NU * NPAR
    with ExitStack() as ctx:
        sb = lambda n, s, d=F32: ctx.enter_context(nc.sbuf_tensor(n, s, d))
        sem = lambda n: ctx.enter_context(nc.semaphore(n))
        yg = sb("yg", [128, 2, B, D])
        stats = sb("stats3", [128, CH, 6])
        mv = sb("mv3", [128, CH, 2])
        dev = sb("dev3", [128, CH])
        power = sb("power", [128, CH])
        stats_f = sb("stats4", [128, CH, 6])
        mv_f = sb("mv4", [128, CH, 2])
        xd = sb("xd", [128, 2, CH, 2, D])
        xv = sb("xv", [128, 2, CH, D])
        x3T = sb("x3T", [128, 2, 2, W])
        yk = sb("yk", [128, 2, NPAR, W])
        mx = sb("mx", [128, 2, 2, UH])
        ex = sb("ex", [128, 2, 2, UH, GC])
        sums = sb("sums", [128, 2, 2, UH])
        pT = sb("pT", [128, 2, 2, UH, GC])
        rs = sb("rs", [128, 2, UH, T])
        oT = sb("oT", [128, 2, T])

        zeroed = sem("x3T_zeroed")
        gathered = sem("gathered_y")
        ready = sem("chunk_gathered")
        rooted = sem("x3_rooted")
        doubled = sem("x3_doubled")
        kept = sem("x3_kept")
        turned = sem("x3_turned")
        x3T_copied = sem("x3T_copied")
        y_ready = sem("yk_ready")
        y_copied = sem("yk_copied")
        scored = sem("group_scored")
        shifted = sem("shifted")
        exped = sem("group_exped")
        weighed = sem("weighed")
        mixed = sem("mixed")
        rs_copied = sem("rs_copied")
        projected = sem("group_projected")
        o_copied = sem("oT_copied")
        final = sem("group_final")
        soft = Steps(S, sem("soften_steps"), 1)
        weigh_st = Steps(S, sem("weigh_steps"), 3)
        prep_st = Steps(S, sem("add_steps"), 13)
        x_st = Steps(S, sem("prepare_steps"), 2)
        fin_st = Steps(S, sem("finish_steps"), 11)

        block = ctx.enter_context(nc.Block())

        def all_chunks(eng, chunk):
            for c in range(2):
                chunk(c, c, c > 0, True, True)
            with eng.Fori(1, NCH // 2 - 1) as i:
                for r in range(2):
                    chunk(i * 2 + r, r, True, True, True)
            for r in range(2):
                chunk(NCH - 2 + r, r, True, r == 0, False)

        @block.vector
        def _(dve):
            V = nc.vector
            s = S.bank[:, 2:4, 0:UH * GC].rearrange("p a (u k) -> p a u k", k=GC)

            def soften(n, p):
                soft.start(dve, n)
                hold(S, dve, scored, n + 1)
                soft.do(V.reduce_max(mx[:, p, :, :], s, AX.X))
                V.tensor_tensor(ex[:, p, :, :, :], s, bc(mx[:, p, :, :].unsqueeze(3), [128, 2, UH, GC]),
                                ALU.subtract).then_inc(shifted, 1)
                soft.end()

            def weigh(n, p):
                weigh_st.start(dve, n)
                do = weigh_st.do
                hold(S, dve, exped, n + 1)
                do(V.reduce_sum(sums[:, p, :, :], ex[:, p, :, :, :], AX.X))
                do(V.reciprocal(sums[:, p, :, :], sums[:, p, :, :]))
                do(V.tensor_tensor(ex[:, p, :, :, :], ex[:, p, :, :, :],
                                   bc(sums[:, p, :, :].unsqueeze(3), [128, 2, UH, GC]), ALU.mult))
                V.transpose(pT[:, p, :, :, :].rearrange("p a u k -> p (a u k)"),
                            ex[:, p, :, :, :].rearrange("p a u k -> p (a u k)")).then_inc(weighed, 1)
                weigh_st.end()

            def add_experts(c):
                st = prep_st
                st.start(dve, c)
                tiles = bass.ds(c * CH, CH)
                hold(S, dve, ready, c + 1)
                for j in range(2):
                    st.done(V.tensor_tensor(yg[:, j, tiles, :], yg[:, j, tiles, :],
                                            bc(S.gates[:, j, tiles].unsqueeze(2), [128, CH, D]), ALU.mult))
                st.wait()
                for j in range(2):
                    st.do(V.tensor_tensor(S.h[:, tiles, :], S.h[:, tiles, :], yg[:, j, tiles, :], ALU.add))
                for k in range(CH):
                    st.done(V.bn_stats(stats[:, k, :], S.h[:, bass.ds(c * CH + k, 1), :].rearrange("p a d -> p (a d)")))
                st.wait()
                for k in range(CH):
                    st.done(V.bn_aggr(mv[:, k, :], stats[:, k, :]))
                st.wait()
                st.do(V.tensor_scalar(dev[:, :], mv[:, :, 1], EPS, None, ALU.add))
                st.mark("variance")
                st.end()

            def prepare(c, r, reused):
                st = x_st
                st.start(dve, c)
                tiles = bass.ds(c * CH, CH)
                hold(S, dve, rooted, c + 1)
                if reused:
                    hold(S, dve, turned, c - 1)
                    hold(S, dve, kept, c - 1)
                st.do(V.tensor_tensor(xd[:, r, :, 0, :], S.h[:, tiles, :], bc(mv[:, :, 0].unsqueeze(2), [128, CH, D]),
                                      ALU.subtract))
                st.do(V.tensor_tensor(xd[:, r, :, 0, :], xd[:, r, :, 0, :], bc(dev[:, :].unsqueeze(2), [128, CH, D]),
                                      ALU.mult))
                st.mark("x")
                st.end()

            def finish(c):
                st = fin_st
                st.start(dve, c)
                tiles = bass.ds(c * CH, CH)
                hold(S, dve, final, c + 1)
                st.do(V.tensor_tensor(S.h[:, tiles, :], S.h[:, tiles, :],
                                      S.ps[0][:, 0:CH * D].rearrange("p (k d) -> p k d", d=D), ALU.add))
                st.mark("added")
                for k in range(CH):
                    st.done(V.bn_stats(stats_f[:, k, :], S.h[:, bass.ds(c * CH + k, 1), :].rearrange("p a d -> p (a d)")))
                st.wait()
                for k in range(CH):
                    st.done(V.bn_aggr(mv_f[:, k, :], stats_f[:, k, :]))
                st.wait()
                st.done(V.tensor_copy(S.mean[:, tiles], mv_f[:, :, 0]))
                st.do(V.tensor_copy(S.var[:, tiles], mv_f[:, :, 1]))
                st.end()

            def chunk(c, r, before, after, after2):
                soften(c * 2 + 1, 1)
                weigh(c * 2 + 1, 1)
                if after2:
                    add_experts(c + 2)
                if after:
                    soften(c * 2 + 2, 0)
                if after2:
                    prepare(c + 2, r, True)
                if after:
                    weigh(c * 2 + 2, 0)
                if before:
                    finish(c - 1)

            for c in range(2):
                add_experts(c)
                prepare(c, c, False)
            soften(0, 0)
            weigh(0, 0)
            all_chunks(dve, chunk)
            finish(NCH - 1)

        @block.gpsimd
        def _(pool):
            nc.gpsimd.memset(x3T[D:128, 0, :, :], 0.0).then_inc(zeroed, 1)
            pool.wait_ge(zeroed, 1)
            nc.gpsimd.memset(x3T[0:D, 1, :, :], 0.0).then_inc(zeroed, 1)
            nc.gpsimd.memset(power[:, :], -0.5).then_inc(zeroed, 1)
            pool.wait_ge(zeroed, 3)

            def gather(c):
                for b in range(c * CH, (c + 1) * CH):
                    for j in range(2):
                        nc.gpsimd.indirect_dma_start(yg[:, j, b, :], None, A["slot_y"],
                                                     bass.IndirectOffsetOnAxis(ap=S.slot_u[:, j, b:b + 1], axis=0)
                                                     ).then_inc(gathered, 16)
                pool.wait_ge(gathered, 16 * 2 * CH * (c + 1))
                pool.sem_inc(ready, 1)

            def root(c):
                prep_st.after(pool, "variance", c)
                nc.gpsimd.tensor_tensor(dev[:, :], dev[:, :], power[:, :], ALU.pow).then_inc(rooted, 1)

            gather(0)
            root(0)
            gather(1)
            root(1)
            gather(2)
            for c in range(2, NCH):
                if c + 1 < NCH:
                    gather(c + 1)
                root(c)

        @block.tensor
        def _(pe):
            M = nc.tensor.matmul
            keys_copied = lambda c, n: hold(S, pe, y_copied, c * NPAR + n)

            def turn_x(c, r, finished):
                hold(S, pe, doubled, c + 1)
                if finished:
                    fin_st.after(pe, "added", c - 3)
                for k in range(CH):
                    last = nc.tensor.transpose(S.ps[0][:, T * k:T * k + T], xd[:, r, k, :, :].rearrange("p a d -> p (a d)"),
                                               S.ident[:, :])
                last.then_inc(turned, 1)

            def keys(c, r, k):
                if k == 0:
                    hold(S, pe, x3T_copied, c * 2 + 2)
                else:
                    keys_copied(c, k)
                M(S.ps[0][:, :], S.qkT[:, k, :, :].rearrange("p a d -> p (a d)"), x3T[:, 0, r, :],
                  start=True, stop=True).then_inc(y_ready, 1)

            def score(n, r, p, first=False):
                if not first:
                    hold(S, pe, shifted, n)
                for a in range(2):
                    for u in range(NU):
                        at = T * (NU * p + u)
                        for g in range(GG):
                            v = (g + 1) % GG
                            last = M(S.ps[2 + a][GC * v:GC * v + GC, NPAR * GC * u:NPAR * GC * (u + 1)].rearrange(
                                        "p (h k) -> p h k", k=GC),
                                     x3T[:, a, r, at + GC * g:at + GC * g + GC],
                                     yk[:, r, :, at + GC * v:at + GC * v + GC], start=True, stop=True)
                last.then_inc(scored, 1)

            def mix(n, c, r, p, part, parts, before):
                if part == 0:
                    hold(S, pe, weighed, n + 1)
                    hold(S, pe, kept, c + 1)
                    if before:
                        hold(S, pe, rs_copied, n)
                products = [(u, g, a) for u in range(NU) for g in range(GG) for a in range(2)]
                for u, g, a in products[len(products) * part // parts:len(products) * (part + 1) // parts]:
                    v = (g + 1) % GG
                    last = M(S.ps[4 + g][64 * a:64 * a + 64, NPAR * GC * u:NPAR * GC * (u + 1)],
                             xv[GC * v:GC * v + GC, r, NU * p + u, :],
                             pT[GC * v:GC * v + GC, p, a, NPAR * u:NPAR * (u + 1), :].rearrange("p h q -> p (h q)"),
                             start=True, stop=True)
                if part == parts - 1:
                    last.then_inc(mixed, 1)

            def project(n, p, reused):
                hold(S, pe, rs_copied, n + 1)
                if reused:
                    hold(S, pe, o_copied, n)
                for k in range(NPAR):
                    for u in range(NU):
                        last = M(S.ps[1][64 * u:64 * u + 64, T * p:T * p + T], S.wv[:, k, :], rs[:, p, NPAR * u + k, :],
                                 start=(k == 0), stop=(k == NPAR - 1))
                last.then_inc(projected, 1)

            def turn_out(c, after):
                hold(S, pe, o_copied, c * 2 + 2)
                if after:
                    keys_copied(c + 2, NPAR)
                else:
                    fin_st.after(pe, "added", c - 1)
                for p in range(2):
                    last = nc.tensor.transpose(S.ps[0][:, T * p:T * p + T], oT[:, p, :], S.ident[:, :])
                last.then_inc(final, 1)

            def chunk(c, r, before, after, after2):
                n = c * 2
                score(n + 1, r, 1)
                if after:
                    turn_x(c + 1, 1 - r, not isinstance(c, int) or c >= 2)
                if before:
                    project(n - 1, 1, True)
                for k in range(NPAR):
                    if after:
                        keys(c + 1, 1 - r, k)
                    mix(n, c, r, 0, k, NPAR, before)
                if after:
                    keys_copied(c + 1, NPAR)
                    score(n + 2, 1 - r, 0)
                if before:
                    turn_out(c - 1, after)
                project(n, 0, before)
                mix(n + 1, c, r, 1, 0, 1, True)

            pe.wait_ge(zeroed, 2)
            turn_x(0, 0, False)
            for k in range(NPAR):
                keys(0, 0, k)
            keys_copied(0, NPAR)
            score(0, 0, 0, True)
            all_chunks(pe, chunk)
            project(2 * NCH - 1, 1, True)
            turn_out(NCH - 1, False)

        @block.scalar
        def _(act):
            N = nc.scalar.activation

            def double(c, r):
                x_st.after(act, "x", c)
                N(xd[:, r, :, 1, :], xd[:, r, :, 0, :], ACT.Copy).then_inc(doubled, 1)

            def keep(c, r, before):
                if before:
                    hold(S, act, mixed, c * 2 - 2)
                N(xv[:, r, :, :], xd[:, r, :, 0, :], ACT.Copy).then_inc(kept, 1)

            def copy_x(c, r):
                hold(S, act, turned, c + 1)
                for a in range(2):
                    half = slice(64 * a, 64 * a + 64)
                    N(x3T[half, a, r, :], S.ps[0][half, :], ACT.Copy).then_inc(x3T_copied, 1)

            def copy_keys(c, r):
                for k in range(NPAR):
                    hold(S, act, y_ready, c * NPAR + k + 1)
                    N(yk[:, r, k, :], S.ps[0][:, :], ACT.Copy).then_inc(y_copied, 1)

            def exponential(n, p):
                hold(S, act, shifted, n + 1)
                e = ex[:, p, :, :, :].rearrange("p a u k -> p (a u k)")
                N(e, e, ACT.Exp).then_inc(exped, 1)

            def copy_mixed(n, p):
                hold(S, act, mixed, n + 1)
                N(rs[:, p, :, :].rearrange("p u (g q) -> p g u q", q=GC),
                  S.bank[:, 4:8, 0:UH * GC].rearrange("p g (u q) -> p g u q", q=GC), ACT.Copy).then_inc(rs_copied, 1)

            def copy_out(n, p):
                hold(S, act, projected, n + 1)
                N(oT[:, p, :], S.ps[1][:, T * p:T * p + T], ACT.Copy).then_inc(o_copied, 1)

            def chunk(c, r, before, after, after2):
                n = c * 2
                if after:
                    copy_x(c + 1, 1 - r)
                exponential(n + 1, 1)
                if before:
                    copy_out(n - 1, 1)
                if after:
                    copy_keys(c + 1, 1 - r)
                    keep(c + 1, 1 - r, before)
                copy_mixed(n, 0)
                if after:
                    exponential(n + 2, 0)
                copy_out(n, 0)
                copy_mixed(n + 1, 1)
                if after2:
                    double(c + 2, r)

            act.wait_ge(zeroed, 2)
            for c in range(2):
                double(c, c)
            keep(0, 0, False)
            copy_x(0, 0)
            copy_keys(0, 0)
            exponential(0, 0)
            all_chunks(act, chunk)
            copy_out(2 * NCH - 1, 1)


def second_experts_stage(nc, S, A, out):
    with ExitStack() as ctx:
        sb = lambda n, s, d=F32: ctx.enter_context(nc.sbuf_tensor(n, s, d))
        sem = lambda n: ctx.enter_context(nc.semaphore(n))
        r2 = sb("r2", [128, B])
        xr = sb("x4", [128, 2, CH, D])
        xT = sb("x4T", [128, NCH, W])
        logits = sb("logits1", [128, 2, CH, E1])
        top = sb("top1", [128, 2, CH, 8])
        top_i = sb("top_i1", [128, 2, CH, 8], U32)
        top_f = sb("top_f1", [128, 2, CH, 2])
        xT_now = sb("x4T_now", [D, 2, W])
        hot = sb("hot1", [128, 2, B, E1])
        gates = sb("gates1", [128, 2, B])
        share = sb("share", [128, B, E1])
        share_now = sb("share_now", [128, 2, CH, E1])
        shareT = sb("shareT", [E1, 2, W])
        hid = sb("hid1", [HID, 4, W])
        acc = sb("acc", [128, 2, CH, D])
        res = sb("res", [128, 2, CH, D])

        scaled = sem("r2_rooted")
        turned = sem("x4_turned")
        x4_copied = sem("x4T_copied")
        scored = sem("router1_scored")
        exped = sem("gates1_exped")
        pre = Steps(S, sem("r2_steps"))
        st = Steps(S, sem("router1_steps"), 28)
        gs = Steps(S, sem("share_steps"))
        share_turned = sem("share_turned")
        shareT_copied = sem("shareT_copied")
        hidden = sem("hidden1")
        gelued = sem("gelued1")
        y_ready = sem("y1_ready")
        es = Steps(S, sem("expert1_steps"), 2 + 2 + 2 * E1 * CH + 2)
        sent_r = [sem(f"sent{r}") for r in range(2)]
        zeroed = sem("x4T_zeroed")
        hot_first = sem("hot_first")

        block = ctx.enter_context(nc.Block())

        @block.vector
        def _(dve):
            V = nc.vector
            pre.start(dve)
            dve.wait_ge(scaled, 1)
            pre.do(V.reciprocal(S.rstd[:, :], S.rstd[:, :]))
            pre.do(V.tensor_tensor(r2[:, :], S.rstd[:, :], S.rstd[:, :], ALU.mult))
            pre.do(V.tensor_tensor(r2[:, :], r2[:, :], S.var[:, :], ALU.mult))
            pre.mark("variance")
            dve.wait_ge(scaled, 2)
            pre.do(V.reciprocal(r2[:, :], r2[:, :]))
            pre.do(V.tensor_tensor(r2[:, :], r2[:, :], S.rstd[:, :], ALU.mult))
            with dve.Fori(0, NCH // 2) as i:
                st.start(dve, i)
                for r in range(2):
                    tiles = bass.ds(i * (2 * CH) + r * CH, CH)
                    st.do(V.tensor_tensor(xr[:, r, :, :], S.h[:, tiles, :], bc(S.mean[:, tiles].unsqueeze(2), [128, CH, D]),
                                          ALU.subtract))
                    st.do(V.tensor_tensor(xr[:, r, :, :], xr[:, r, :, :], bc(r2[:, tiles].unsqueeze(2), [128, CH, D]), ALU.mult))
                    st.mark(("x", r))
                for r in range(2):
                    tiles = bass.ds(i * (2 * CH) + r * CH, CH)
                    hold(S, dve, scored, i * 2 + r + 1)
                    st.do(V.tensor_tensor(logits[:, r, :, :], S.ps[2 + r][:, 0:CH * E1].rearrange("p (k e) -> p k e", e=E1),
                                          bc(S.br1[:, :].unsqueeze(1), [128, CH, E1]), ALU.add))
                    for k in range(CH):
                        st.done(V.max(top[:, r, k, :], logits[:, r, k, :]))
                    st.wait()
                    for k in range(CH):
                        st.done(V.max_index(top_i[:, r, k, :], top[:, r, k, :], logits[:, r, k, :]))
                    st.wait()
                    st.do(V.tensor_copy(top_f[:, r, :, :], top_i[:, r, :, 0:2]))
                    st.done(V.tensor_tensor(gates[:, 1, tiles], top[:, r, :, 1], top[:, r, :, 0], ALU.subtract))
                    for c in range(2):
                        ins = V.tensor_tensor(hot[:, c, tiles, :], bc(S.iota_free[:, 0:E1].unsqueeze(1), [128, CH, E1]),
                                              bc(top_f[:, r, :, c:c + 1], [128, CH, E1]), ALU.is_equal)
                        if c == 0:
                            ins.then_inc(hot_first, 1)
                        else:
                            st.do(ins)
                st.end()
            gs.start(dve)
            gs.mark("routed")
            dve.wait_ge(exped, 1)
            dve.wait_ge(hot_first, NCH)
            gs.do(V.tensor_scalar(gates[:, 0, :], gates[:, 1, :], 1.0, None, ALU.add))
            gs.do(V.reciprocal(gates[:, 0, :], gates[:, 0, :]))
            gs.do(V.tensor_tensor(gates[:, 1, :], gates[:, 1, :], gates[:, 0, :], ALU.mult))
            for c in range(2):
                gs.done(V.tensor_tensor(hot[:, c, :, :], hot[:, c, :, :], bc(gates[:, c, :].unsqueeze(2), [128, B, E1]), ALU.mult))
            gs.wait()
            gs.do(V.tensor_tensor(share[:, :, :], hot[:, 0, :, :], hot[:, 1, :, :], ALU.add))
            with dve.Fori(0, NCH // 2) as i:
                es.start(dve, i)
                for r in range(2):
                    tiles = bass.ds(i * (2 * CH) + r * CH, CH)
                    es.done(V.tensor_scalar(share_now[:, r, :, :], share[:, tiles, :], 1.0, None, ALU.mult))
                    es.mark(("share", r))
                for r in range(2):
                    tiles = bass.ds(i * (2 * CH) + r * CH, CH)
                    hold(S, dve, y_ready, i * (2 * E1 + 2) + r + 1)
                    es.done(V.tensor_tensor(acc[:, r, :, :], S.h[:, tiles, :],
                                            S.ps[2 + r][:, 0:CH * D].rearrange("p (k d) -> p k d", d=D), ALU.add))
                for n in range(2 * E1):
                    r, e = n // E1, n % E1
                    hold(S, dve, y_ready, i * (2 * E1 + 2) + n + 3)
                    es.wait()
                    for k in range(CH):
                        es.done(V.scalar_tensor_tensor(acc[:, r, k, :], S.ps[4 + n % 4][:, D * k:D * k + D],
                                                       share_now[:, r, k, e:e + 1], acc[:, r, k, :], ALU.mult, ALU.add))
                    es.mark(("added", n))
                    if e == E1 - 1:
                        es.wait()
                        hold(S, dve, sent_r[r], i * 16 + 16)
                        es.done(V.tensor_copy(res[:, r, :, :], acc[:, r, :, :]))
                        es.mark(("result", r))
                es.wait()
                es.end()

        @block.gpsimd
        def _(pool):
            nc.gpsimd.memset(xT[D:128, :, :], 0.0).then_inc(zeroed, 1)

        @block.tensor
        def _(pe):
            M = nc.tensor.matmul
            with pe.Fori(0, NCH // 2) as i:
                for r in range(2):
                    st.after(pe, ("x", r), i)
                    for k in range(CH):
                        last = nc.tensor.transpose(S.ps[r][0:D, T * k:T * k + T], xr[:, r, k, :], S.ident[:, :])
                    last.then_inc(turned, 1)
                for r in range(2):
                    hold(S, pe, x4_copied, i * 4 + 2 * r + 2)
                    for k in range(CH):
                        last = M(S.ps[2 + r][:, E1 * k:E1 * k + E1], xT_now[:, r, T * k:T * k + T], S.wr1[:, :], start=True, stop=True)
                    last.then_inc(scored, 1)
            pe.wait_ge(zeroed, 1)
            with pe.Fori(0, NCH // 2) as i:
                def up(n):
                    r, e = n // E1, n % E1
                    if n >= 2:
                        hold(S, pe, gelued, i * (2 * E1) + n - 1)
                    M(S.ps[n % 2][:, :], S.w1_1[:, e, :], xT[:, bass.ds(i * 2 + r, 1), :].rearrange("p a w -> p (a w)"),
                      start=True, stop=True).then_inc(hidden, 1)

                def down(n):
                    r, e = n // E1, n % E1
                    hold(S, pe, gelued, i * (2 * E1) + n + 1)
                    if n >= 4:
                        es.after(pe, ("added", n - 4), i)
                    for k in range(CH):
                        last = M(S.ps[4 + n % 4][:, D * k:D * k + D], hid[:, n % 4, T * k:T * k + T], S.w2_1[:, e, :],
                                 start=True, stop=True)
                    last.then_inc(y_ready, 1)

                up(0)
                up(1)
                for r in range(2):
                    es.after(pe, ("share", r), i)
                    for k in range(CH):
                        last = nc.tensor.transpose(S.ps[6 + r][0:E1, T * k:T * k + T], share_now[:, r, k, :], S.ident[:, :])
                    last.then_inc(share_turned, 1)
                for r in range(2):
                    hold(S, pe, shareT_copied, i * 2 + r + 1)
                    for k in range(CH):
                        last = M(S.ps[2 + r][:, D * k:D * k + D], shareT[:, r, T * k:T * k + T], S.b2_1[:, :], start=True, stop=True)
                    last.then_inc(y_ready, 1)
                for n in range(2 * E1):
                    if n + 2 < 2 * E1:
                        up(n + 2)
                    down(n)

        @block.scalar
        def _(act):
            N = nc.scalar.activation
            N(S.rstd[:, :], S.var[:, :], ACT.Sqrt, bias=S.eps[:, 0:1]).then_inc(scaled, 1)
            pre.after(act, "variance")
            N(r2[:, :], r2[:, :], ACT.Sqrt, bias=S.eps[:, 0:1]).then_inc(scaled, 1)
            with act.Fori(0, NCH // 2) as i:
                for r in range(2):
                    hold(S, act, turned, i * 2 + r + 1)
                    N(xT_now[:, r, :], S.ps[r][0:D, :], ACT.Identity, scale=S.gamma[:, 0:1], bias=S.beta[:, 0:1]).then_inc(x4_copied, 1)
                    N(xT[0:D, bass.ds(i * 2 + r, 1), :].rearrange("p a w -> p (a w)"), S.ps[r][0:D, :], ACT.Identity,
                      scale=S.gamma[:, 0:1], bias=S.beta[:, 0:1]).then_inc(x4_copied, 1)
            act.wait_ge(st.sem, st.per_turn * (NCH // 2))
            N(gates[:, 1, :], gates[:, 1, :], ACT.Exp).then_inc(exped, 1)
            with act.Fori(0, NCH // 2) as i:
                for n in range(2 * E1):
                    if n == 1:
                        for r in range(2):
                            hold(S, act, share_turned, i * 2 + r + 1)
                            N(shareT[:, r, :], S.ps[6 + r][0:E1, :], ACT.Copy).then_inc(shareT_copied, 1)
                    hold(S, act, hidden, i * (2 * E1) + n + 1)
                    if n >= 4:
                        hold(S, act, y_ready, i * (2 * E1 + 2) + n - 4 + 3)
                    N(hid[:, n % 4, :], S.ps[n % 2][:, :], ACT.Gelu, bias=S.b1_1[:, n % E1:n % E1 + 1]).then_inc(gelued, 1)

        @block.sync
        def _(sp):
            rows = out.rearrange("(c k) p d -> c p k d", k=CH)
            for r in range(2):
                sp.sem_inc(sent_r[r], 16)
            with sp.Fori(0, NCH // 2) as i:
                for r in range(2):
                    es.after(sp, ("result", r), i)
                    sp.dma_start(rows[bass.ds(i * 2 + r, 1)].rearrange("c p k d -> (c p) k d"), res[:, r, :, :]).then_inc(sent_r[r], 16)
            for r in range(2):
                sp.wait_ge(sent_r[r], 16 + 16 * (NCH // 2))


def build(nc, A, out):
    A["idx_scratch"] = nc.dram_tensor("idx_scratch", [B, T], BF16).ap()
    S = Store()
    S.slots = 2 * B * T + E0 * 128
    A["slot_y"] = nc.dram_tensor("slot_y", [S.slots, D], F32).ap()
    A["slot_x"] = nc.dram_tensor("slot_x", [S.slots, D], F32).ap()
    with ExitStack() as ctx:
        sb = lambda n, s, d=F32: ctx.enter_context(nc.sbuf_tensor(n, s, d))
        S.bank = ctx.enter_context(nc.psum_tensor("banks", [128, 8, 512], F32))
        S.ps = [S.bank[:, k, :] for k in range(8)]
        S.ident = sb("ident", [128, 128])
        S.triC = sb("triC", [128, 128])
        S.triS = sb("triS", [128, 128], BF16)
        S.cmean = sb("cmean", [128, 128])
        S.iota_free = sb("iota_free", [128, 128])
        S.iota_part = sb("iota_part", [128, 1])
        S.ones_bf = sb("ones_bf", [128, 128], BF16)
        S.eps = sb("eps", [128, 1])
        S.half_pi = sb("half_pi", [128, 1])
        S.xT = sb("xT", [T, B], I32)
        S.maskT = sb("maskT", [T, B])
        S.w1c = sb("w1c", [128, 128])
        S.w1p = sb("w1p", [128, 128])
        S.b1c = sb("b1c", [128, 1])
        S.w2c = sb("w2c", [128, GT])
        S.sg_w1 = sb("sg_w1", [128, D // 2])
        S.sg_b1 = sb("sg_b1", [D // 2, 1])
        S.sg_w2 = sb("sg_w2", [D // 2, 1])
        S.wx = sb("wx", [128, P + 2 * D])
        S.proj_b = sb("proj_b", [128, NPROJ])
        S.pcs = sb("pcs", [T, 2, P])
        S.pcsT = sb("pcsT", [128, T])
        S.ppT = sb("ppT", [128, T])
        S.dcs = sb("dcs", [T, 2, NW])
        S.nhd2 = sb("nhd2", [T, NW])
        S.out_w2 = sb("out_w2", [128, D])
        S.out_row = sb("out_row", [128, D])
        S.wr0 = sb("wr0", [D, E0])
        S.br0 = sb("br0", [128, E0])
        S.qkT = sb("qkT", [128, NPAR, 2, D])
        S.wv = sb("wv", [128, NPAR, D])
        S.gamma = sb("gamma", [D, 1])
        S.beta = sb("beta", [D, 1])
        S.wr1 = sb("wr1", [D, E1])
        S.br1 = sb("br1", [128, E1])
        S.w1_1 = sb("w1_1", [128, E1, HID])
        S.w2_1 = sb("w2_1", [HID, E1, D])
        S.b1_1 = sb("b1_1", [HID, E1])
        S.b2_1 = sb("b2_1", [E1, D])
        S.h = sb("h", [128, B, D])
        S.stats = sb("stats", [128, 2 * CH, 6])
        S.mv = sb("mv", [128, 2 * CH, 2])
        S.dev = sb("dev", [128, 2 * CH])
        S.mean = sb("mean", [128, B])
        S.var = sb("var", [128, B])
        S.rstd = sb("rstd", [128, B])
        S.waits = {e.engine: ctx.enter_context(nc.semaphore(f"waits_{n}")) for n, e in enumerate(
            (nc.tensor, nc.vector, nc.scalar, nc.gpsimd, nc.sync))}
        with ExitStack() as tok:
            tb = lambda n, s, d=F32: tok.enter_context(nc.sbuf_tensor(n, s, d))
            S.b_oah = tb("b_oah", [128, D])
            S.zeros = tb("zeros", [128, 32 * D])
            S.x_bc = tb("x_bc", [128, B * T], I32)
            S.idx_bc = tb("idx_bc", [128, B * T], BF16)
            S.triG = tb("triG", [128, 128])
            S.emb = tb("emb", [T, D])
            S.emb3 = tb("emb3", [T, 3, D], BF16)
            S.emb_last3 = tb("emb_last3", [3, D], BF16)
            S.w_inT = tb("w_inT", [D, D])
            S.hn = tb("hn", [128, 2, CH, D + 1])
            setup_stage(nc, S, A)
            token_stage(nc, S, A)
        with ExitStack() as mem:
            mb = lambda n, s, d=F32: mem.enter_context(nc.sbuf_tensor(n, s, d))
            S.proj = mb("proj", [128, B, NPROJ])
            project_stage(nc, S, A)
            S.q_pos = mb("q_pos", [128, B, 2 * P])
            S.q_kv = mb("q_kv", [128, B, 2 * P])
            S.k_kv = mb("k_kv", [128, B, 2 * P])
            S.gv = mb("gv", [128, B, D])
            phase_stage(nc, S, A)
            memory_stage(nc, S, A)
        with ExitStack() as moe:
            eb = lambda n, s, d=F32: moe.enter_context(nc.sbuf_tensor(n, s, d))
            S.gates = eb("gates", [128, 2, B])
            S.slot_u = eb("slot_u", [128, 2, B], U32)
            with ExitStack() as experts:
                wb = lambda n, s, d=F32: experts.enter_context(nc.sbuf_tensor(n, s, d))
                S.xn = wb("xn", [128, B, D])
                S.w1_0 = wb("w1_0", [D + 1, E0, HID])
                S.w2_0 = wb("w2_0", [HID, E0, D])
                S.b2_0 = wb("b2_0", [E0, D])
                S.experts_in = experts.enter_context(nc.semaphore("experts_in"))
                S.owner_row = wb("owner_row", [1, 128], I32)
                route_stage(nc, S, A)
                experts_stage(nc, S, A)
            grouped_stage(nc, S, A)
        second_experts_stage(nc, S, A, out)


INPUTS = {
    "x": "x", "L0_tok_emb_table": "emb", "L0_tok_W_in": "w_in", "L0_tok_b_oah": "b_oah",
    "L0_attn_pos_phases": "phases", "L0_attn_window_deltas": "deltas", "L0_attn_mc_w": "mc_w", "L0_attn_mc_b": "mc_b",
    "L0_attn_hop_w1": "hop_w1", "L0_attn_hop_b1": "hop_b1", "L0_attn_hop_w2": "hop_w2", "L0_attn_hop_b2": "hop_b2",
    "L0_attn_cpe_w": "cpe_w", "L0_attn_cpe_b": "cpe_b", "L0_attn_ve_w": "ve_w", "L0_attn_ve_b": "ve_b",
    "L0_attn_kce_w": "kce_w", "L0_attn_kce_b": "kce_b", "L0_attn_ksk_w1": "ksk_w1", "L0_attn_ksk_b1": "ksk_b1",
    "L0_attn_ksk_w2": "ksk_w2", "L0_attn_ksk_b2": "ksk_b2", "L0_attn_sg_w1": "sg_w1", "L0_attn_sg_b1": "sg_b1",
    "L0_attn_sg_w2": "sg_w2", "L0_attn_sg_b2": "sg_b2", "L0_attn_ln_g": "ln_g", "L0_attn_ln_b": "ln_b",
    "L0_attn_out_w": "out_w", "L0_attn_out_b": "out_b", "L0_ffn_Wr": "wr0", "L0_ffn_br": "br0",
    "L0_ffn_W1": "w1_0", "L0_ffn_b1": "b1_0", "L0_ffn_W2": "w2_0", "L0_ffn_b2": "b2_0",
    "L1_attn_Wq": "wq", "L1_attn_Wk": "wk", "L1_attn_Wo": "wo", "L1_ffn_gamma": "gamma", "L1_ffn_beta": "beta",
    "L1_ffn_Wr": "wr1", "L1_ffn_br": "br1", "L1_ffn_W1": "w1_1", "L1_ffn_b1": "b1_1", "L1_ffn_W2": "w2_1",
    "L1_ffn_b2": "b2_1",
}


def kernel(**inputs):
    import concourse.bacc as _bacc
    from concourse.bass_utils import run_bass_kernel_spmd as _run

    nc = _bacc.Bacc("TRN2", target_bir_lowering=False, num_devices=1)
    arrays, aps = {}, {}
    for name, short in INPUTS.items():
        a = np.ascontiguousarray(inputs[name])
        arrays[f"in_{short}"] = a
        aps[short] = nc.dram_tensor(f"in_{short}", a.shape, mybir.dt.from_np(a.dtype), kind="ExternalInput").ap()
    out = nc.dram_tensor("out_h", (B, T, D), F32, kind="ExternalOutput").ap()
    build(nc, aps, out)
    r = _run(nc, [arrays], core_ids=[0])
    return r.results[0]["out_h"]
```

```python
import numpy as np
from contextlib import ExitStack

import concourse.bass as bass
from concourse import mybir

F32 = mybir.dt.float32
BF16 = mybir.dt.bfloat16
I32 = mybir.dt.int32
U32 = mybir.dt.uint32
ALU = mybir.AluOpType
ACT = mybir.ActivationFunctionType
AX = mybir.AxisListType

B, T, D = 32, 128, 64
CH = 4
NCH = B // CH
W = CH * T
NPOS = T + 1
P = 32
NH = 4
NW = 5
HP = P + 1
E0, E1, HID = 64, 8, 128
GH, GG, GC = 10, 4, 32
NPAR = GH // 2
EPS = 1e-5

AO, ST, GT, KY, CT, VL = 0, NH * HP, NH * HP + P, NH * HP + P + 1, NH * HP + 2 * P + 1, NH * HP + 2 * P + 1 + D
NPROJ = VL + D

PI_BELOW = float(np.nextafter(np.float32(np.pi), np.float32(0)))
HALF_PI = float(np.float32(np.pi / 2))
TWO_PI_PARTS = [6.28125, float(np.float32(2 * np.pi - 6.28125)),
                float(2 * np.pi - 6.28125 - float(np.float32(2 * np.pi - 6.28125)))]
ROUND = 12582912.0


class Store:
    pass


class Steps:

    def __init__(self, S, sem, per_turn=0):
        self.S, self.looped, self.sem, self.per_turn, self.n, self.marks = S, per_turn > 0, sem, per_turn, 0, {}

    def start(self, eng, turn=0):
        self.eng, self.base, self.n = eng, turn * self.per_turn, 0

    def done(self, ins):
        ins.then_inc(self.sem, 1)
        self.n += 1

    def wait(self):
        if self.looped:
            hold(self.S, self.eng, self.sem, self.base + self.n)
        else:
            self.eng.wait_ge(self.sem, self.n)

    def do(self, ins):
        self.done(ins)
        self.wait()

    def mark(self, name):
        self.marks[name] = self.n

    def end(self):
        assert self.n == self.per_turn, f"{self.n} steps a turn"

    def after(self, eng, name, turn=0):
        if self.looped:
            hold(self.S, eng, self.sem, turn * self.per_turn + self.marks[name])
        else:
            eng.wait_ge(self.sem, self.marks[name])


def hold(S, eng, sem, value):
    eng.wait_ge(sem, value)
    eng.sem_inc(S.waits[eng.engine], 1)


def bc(ap, shape):
    return ap.to_broadcast(shape)


def col(ap):
    return ap.rearrange("(p o) -> p o", o=1)


def setup_stage(nc, S, A):
    with ExitStack() as ctx:
        sb = lambda n, s, d=F32: ctx.enter_context(nc.sbuf_tensor(n, s, d))
        sem = lambda n: ctx.enter_context(nc.semaphore(n))
        x_row = sb("x_row", [B, T], I32)
        w_in = sb("w_in", [D, D])
        emb_last = sb("emb_last", [3, D])
        emb_rest = sb("emb_rest", [128, 2, D])
        last_part = sb("last_part", [3, 3, D], BF16)
        last_rest = sb("last_rest", [3, 2, D])
        emb_low = sb("emb_low", [128, D])
        pp = sb("pp", [T, P])
        ang = sb("ang", [T, P + NW])
        turns = sb("turns", [T, P + NW])
        absa = sb("absa", [T, P + NW])
        sincos = sb("sincos", [T, 2, P + NW])
        pdup = sb("pdup", [T, 2, 2, P])
        seq_len = sb("seq_len", [B, 1])
        mask_row = sb("mask_row", [B, T])
        idx_row = sb("idx_row", [B, T])
        neg_row = sb("neg_row", [B, T])
        idx_bf = sb("idx_bf", [B, T], BF16)
        rec_row = sb("rec_row", [128, 128])
        triS_f = sb("triS_f", [128, 128])
        xT_i = sb("xT_i", [T, B], I32)

        early_in = sem("early_in")
        idx_out = sem("idx_out")
        idx_back = sem("idx_back")
        masks_made = sem("masks_made")
        dve_done = sem("setup_dve_done")
        act_done = sem("setup_act_done")
        pe_done = sem("setup_pe_done")
        pool_done = sem("setup_pool_done")

        early = [(x_row[:, :], A["x"]), (S.x_bc[:, :].rearrange("p (b t) -> p b t", b=B), A["x"].partition_broadcast(128)),
                 (S.emb[:, :], A["emb"][0:T, :]),
                 (emb_last[:, :], A["emb"][T, :].partition_broadcast(3)), (w_in[:, :], A["w_in"]),
                 (pp[:, :], A["phases"][0:T, :]), (ang[:, P:P + NW], A["deltas"].partition_broadcast(T)),
                 (ang[:, 0:P], A["phases"][0:T, :]), (S.b_oah[:, :], A["b_oah"].partition_broadcast(128))]
        n_early = 16 * len(early)

        block = ctx.enter_context(nc.Block())

        at = {}

        @block.vector
        def _(dve):
            st = Steps(S, dve_done)
            st.start(dve)
            V, do = nc.vector, st.do

            for t in (S.w1c[D:128, 0:D], S.w1p[0:P, D:128], S.w1p[P:2 * P, :], S.w1p[2 * P:128, :], S.sg_w1[D:128, :], S.wx[D:128, :], S.ppT[P:2 * P, :],
                      S.ppT[2 * P:128, :], S.pcsT[D:128, :], S.w2c[0:D, ST:GT], S.w2c[D:128, 0:ST]):
                st.done(V.memset(t, 0.0))
            st.done(V.memset(S.qkT[D:128, :, :, :], 0.0))
            st.done(V.memset(S.w1_1[D:128, :, :], 0.0))
            st.done(V.memset(S.ones_bf[:, :], 1.0))
            st.done(V.memset(S.eps[:, :], EPS))
            st.done(V.memset(S.half_pi[:, :], HALF_PI))
            for r in range(2):
                st.done(V.memset(S.hn[:, r, :, D:D + 1], 1.0))
            dve.wait_ge(early_in, n_early)
            dve.wait_ge(masks_made, 2)
            do(V.tensor_scalar(mask_row[:, :], x_row[:, :], 0.0, None, ALU.not_equal))
            do(V.reduce_sum(seq_len[:, :], mask_row[:, :], AX.X))
            do(V.tensor_scalar(idx_row[:, :], S.iota_free[0:B, :], -1.0, seq_len[:, 0:1], ALU.mult, ALU.add))
            do(V.tensor_tensor(idx_row[:, :], idx_row[:, :], mask_row[:, :], ALU.mult))
            do(V.tensor_scalar(neg_row[:, :], idx_row[:, :], 0.0, float(NPOS), ALU.is_lt, ALU.mult))
            do(V.tensor_tensor(idx_bf[:, :], idx_row[:, :], neg_row[:, :], ALU.add))
            at['idx'] = st.n
            for k in range(4):
                st.done(V.transpose(xT_i[32 * k:32 * k + 32, :], x_row[:, 32 * k:32 * k + 32]))
            st.wait()
            st.done(V.tensor_copy(S.xT[:, :], xT_i[:, :]))
            do(V.tensor_scalar(S.maskT[:, :], xT_i[:, :], 0.0, None, ALU.not_equal))
            do(V.tensor_copy(S.emb3[:, 0, :], S.emb[:, :]))
            do(V.tensor_tensor(emb_rest[:, 0, :], S.emb[:, :], S.emb3[:, 0, :], ALU.subtract))
            do(V.tensor_copy(S.emb3[:, 1, :], emb_rest[:, 0, :]))
            do(V.tensor_tensor(emb_rest[:, 1, :], emb_rest[:, 0, :], S.emb3[:, 1, :], ALU.subtract))
            do(V.tensor_copy(S.emb3[:, 2, :], emb_rest[:, 1, :]))
            do(V.tensor_copy(last_part[:, 0, :], emb_last[:, :]))
            do(V.tensor_tensor(last_rest[:, 0, :], emb_last[:, :], last_part[:, 0, :], ALU.subtract))
            do(V.tensor_copy(last_part[:, 1, :], last_rest[:, 0, :]))
            do(V.tensor_tensor(last_rest[:, 1, :], last_rest[:, 0, :], last_part[:, 1, :], ALU.subtract))
            do(V.tensor_copy(last_part[:, 2, :], last_rest[:, 1, :]))
            do(V.tensor_scalar(emb_low[0:3, :], last_part[:, 0, :], S.ident[0:3, 0:1], None, ALU.mult))
            for k in (1, 2):
                do(V.scalar_tensor_tensor(emb_low[0:3, :], last_part[:, k, :], S.ident[0:3, k:k + 1],
                                          emb_low[0:3, :], ALU.mult, ALU.add))
            do(V.tensor_copy(S.emb_last3[:, :], emb_low[0:3, :]))
            do(V.tensor_scalar(S.triS[:, :], triS_f[:, :], -1.0, None, ALU.add))
            do(V.tensor_scalar(rec_row[:, :], S.iota_free[:, :], 1.0, None, ALU.add))
            do(V.reciprocal(rec_row[:, :], rec_row[:, :]))
            do(V.tensor_tensor(S.cmean[:, :], rec_row[:, :], S.triC[:, :], ALU.mult))
            do(V.tensor_tensor(S.nhd2[:, :], ang[:, P:P + NW], ang[:, P:P + NW], ALU.mult))
            do(V.tensor_scalar(S.nhd2[:, :], S.nhd2[:, :], -0.5, None, ALU.mult))
            do(V.tensor_scalar(ang[:, P:P + NW], ang[:, P:P + NW], 0.1, None, ALU.mult))
            do(V.tensor_scalar(turns[:, :], ang[:, :], float(1 / (2 * np.pi)), ROUND, ALU.mult, ALU.add))
            do(V.tensor_scalar(turns[:, :], turns[:, :], -ROUND, None, ALU.add))
            for c in TWO_PI_PARTS:
                do(V.scalar_tensor_tensor(ang[:, :], turns[:, :], -c, ang[:, :], ALU.mult, ALU.add))
            do(V.tensor_scalar(ang[:, :], ang[:, :], PI_BELOW, -PI_BELOW, ALU.min, ALU.max))
            at['angle'] = st.n
            dve.wait_ge(act_done, 3)
            st.done(V.tensor_copy(S.pcs[:, :, :], sincos[:, :, 0:P]))
            st.done(V.tensor_copy(S.dcs[:, :, :], sincos[:, :, P:P + NW]))
            for k in range(2):
                st.done(V.tensor_copy(pdup[:, k, :, :], sincos[:, :, 0:P]))
            at['pdup'] = st.n
            dve.wait_ge(pe_done, 1)
            st.done(V.tensor_copy(S.w_inT[:, :], S.ps[0][0:D, 0:D]))
            st.done(V.tensor_copy(S.pcsT[0:D, :], S.ps[0][0:D, 256:384]))
            st.done(V.tensor_copy(S.ppT[0:P, :], S.ps[0][0:P, 384:512]))

        @block.sync
        def _(sp):
            for dst, src in early:
                sp.dma_start(dst, src, allow_slow_non_contiguous=True).then_inc(early_in, 16)
            sp.wait_ge(dve_done, at['idx'])
            sp.dma_start(A["idx_scratch"], idx_bf[:, :]).then_inc(idx_out, 16)
            sp.wait_ge(idx_out, 16)
            sp.dma_start(S.idx_bc[:, :].rearrange("p (b t) -> p b t", b=B),
                         A["idx_scratch"].partition_broadcast(128)).then_inc(idx_back, 16)
            sp.wait_ge(idx_back, 16)

        @block.gpsimd
        def _(pool):
            nc.gpsimd.memset(S.ident[:, :], 0.0)
            nc.gpsimd.memset(S.triG[:, :], 1.0)
            nc.gpsimd.memset(S.triC[:, :], 1.0)
            nc.gpsimd.memset(triS_f[:, :], 1.0)
            nc.gpsimd.iota(S.iota_free[:, :], [[1, 128]], base=0, channel_multiplier=0, allow_small_or_imprecise_dtypes=True)
            nc.gpsimd.iota(S.iota_part[:, :], [[0, 1]], base=0, channel_multiplier=1,
                           allow_small_or_imprecise_dtypes=True).then_inc(masks_made, 1)
            nc.gpsimd.memset(S.zeros[:, :], 0.0)
            pool.wait_ge(masks_made, 1)
            sel = nc.gpsimd.affine_select
            sel(out=S.ident[:, :], in_=S.ident[:, :], compare_op=ALU.not_equal, fill=1.0, base=0,
                pattern=[[-1, 128]], channel_multiplier=1)
            sel(out=S.triG[:, :], in_=S.triG[:, :], compare_op=ALU.is_ge, fill=0.0, base=0,
                pattern=[[-1, 128]], channel_multiplier=1)
            sel(out=S.triC[:, :], in_=S.triC[:, :], compare_op=ALU.is_ge, fill=0.0, base=0,
                pattern=[[1, 128]], channel_multiplier=-1)
            sel(out=triS_f[:, :], in_=triS_f[:, :], compare_op=ALU.is_gt, fill=0.0, base=0,
                pattern=[[1, 128]], channel_multiplier=-1).then_inc(masks_made, 1)

        @block.scalar
        def _(act):
            act.wait_ge(dve_done, at['angle'])
            nc.scalar.activation(sincos[:, 1, :], ang[:, :], ACT.Sin).then_inc(act_done, 1)
            nc.scalar.activation(absa[:, :], ang[:, :], ACT.Abs).then_inc(act_done, 1)
            act.wait_ge(act_done, 2)
            nc.scalar.activation(sincos[:, 0, :], absa[:, :], ACT.Sin, bias=S.half_pi[:, 0:1], scale=-1.0).then_inc(act_done, 1)

        @block.tensor
        def _(pe):
            M = nc.tensor.matmul
            pe.wait_ge(early_in, n_early)
            pe.wait_ge(masks_made, 2)
            pe.wait_ge(dve_done, at['pdup'])
            idn = S.ident
            nc.tensor.transpose(S.ps[0][0:D, 0:D], w_in[:, :], idn[0:D, 0:D])
            nc.tensor.transpose(S.ps[0][:, 256:384], pdup[:, :, :, :].rearrange("p a b c -> p (a b c)"), idn[:, :])
            nc.tensor.transpose(S.ps[0][0:P, 384:512], pp[:, :], idn[:, :]).then_inc(pe_done, 1)


def weights_to_load(S, A, sb):
    L = Store()
    L.kce_w = sb("kce_w", [D, D])
    L.ksk_low = sb("ksk_low", [D, D])
    L.kce_b = sb("kce_b", [D, 1])
    L.ksk_b1 = sb("ksk_b1", [128, 1])
    L.ln_g = sb("ln_g", [128, 1])
    L.ln_b = sb("ln_b", [D, 1])
    L.out_w = sb("out_w", [128, D])
    L.out_b = sb("out_b", [128, D])
    L.wq = sb("wq", [D, GH, D])
    L.wk = sb("wk", [D, GH, D])
    L.wo = sb("wo", [D, GH, D])
    pairs = [(S.w1c[0:D, 0:D], A["hop_w1"][0:D, :]), (S.w1p[0:P, 0:D], A["hop_w1"][D:D + P, :]),
             (S.w1c[0:D, D:2 * D], A["ksk_w1"][0:D, :]), (L.ksk_low[:, :], A["ksk_w1"][D:2 * D, :]),
             (L.kce_w[:, :], A["kce_w"]), (L.kce_b[:, :], col(A["kce_b"])), (L.ksk_b1[D:128, :], col(A["ksk_b1"])),
             (S.b1c[0:D, :], col(A["hop_b1"])), (S.w2c[0:D, 0:ST], A["hop_w2"]), (S.w2c[D:128, ST:GT], A["ksk_w2"]),
             (S.sg_w1[0:D, :], A["sg_w1"]), (S.sg_b1[:, :], col(A["sg_b1"])), (S.sg_w2[:, :], A["sg_w2"]),
             (S.wx[0:D, 0:P], A["cpe_w"]), (S.wx[0:D, P:P + D], A["mc_w"]), (S.wx[0:D, P + D:P + 2 * D], A["ve_w"]),
             (S.proj_b[:, AO:ST], A["hop_b2"].partition_broadcast(128)), (S.proj_b[:, ST:GT], A["ksk_b2"].partition_broadcast(128)),
             (S.proj_b[:, GT:KY], A["sg_b2"].partition_broadcast(128)), (S.proj_b[:, KY:CT], A["cpe_b"].partition_broadcast(128)),
             (S.proj_b[:, CT:VL], A["mc_b"].partition_broadcast(128)), (S.proj_b[:, VL:NPROJ], A["ve_b"].partition_broadcast(128)),
             (L.ln_g[0:D, :], col(A["ln_g"])), (L.ln_g[D:128, :], col(A["ln_g"])), (L.ln_b[:, :], col(A["ln_b"])),
             (L.out_w[0:D, :], A["out_w"]), (L.out_w[D:128, :], A["out_w"]), (L.out_b[:, :], A["out_b"].partition_broadcast(128)),
             (S.wr0[:, :], A["wr0"]), (S.br0[:, :], A["br0"].partition_broadcast(128)),
             (L.wq[:, :, :], A["wq"].rearrange("h d e -> d h e")), (L.wk[:, :, :], A["wk"].rearrange("h d e -> d h e")),
             (L.wo[:, :, :], A["wo"].rearrange("o (h e) -> o h e", e=D)),
             (S.gamma[:, :], col(A["gamma"])), (S.beta[:, :], col(A["beta"])), (S.wr1[:, :], A["wr1"]),
             (S.br1[:, :], A["br1"].partition_broadcast(128)),
             (S.w1_1[0:D, :, :], A["w1_1"].rearrange("e d h -> d e h")), (S.w2_1[:, :, :], A["w2_1"].rearrange("e h d -> h e d")),
             (S.b1_1[:, :], A["b1_1"].rearrange("e h -> h e")), (S.b2_1[:, :], A["b2_1"])]
    return L, pairs


def product_stage(nc, S, L):
    with ExitStack() as ctx:
        sb = lambda n, s, d=F32: ctx.enter_context(nc.sbuf_tensor(n, s, d))
        sem = lambda n: ctx.enter_context(nc.semaphore(n))
        kce_wT = sb("kce_wT", [D, D])
        ln_bb = sb("ln_bb", [D, 128])
        wqT = sb("wqT", [128, NPAR, D])
        wkT = sb("wkT", [128, NPAR, D])
        woT = sb("woT", [128, NPAR, D])
        dve_done = sem("product_dve_done")
        pe_done = sem("product_pe_done")
        rooted = sem("token_rooted")

        block = ctx.enter_context(nc.Block())

        at = {}

        @block.vector
        def _(dve):
            st = Steps(S, dve_done)
            st.start(dve)
            V = nc.vector

            st.done(V.tensor_scalar(S.out_w2[:, :], L.out_w[:, :], L.ln_g[:, 0:1], None, ALU.mult))
            st.done(V.tensor_copy(ln_bb[:, :], bc(L.ln_b[:, 0:1], [D, 128])))
            at['lnbb'] = st.n
            dve.wait_ge(rooted, 1)
            V.reciprocal(S.rstd[:, :], S.rstd[:, :])
            dve.wait_ge(pe_done, 1)
            st.done(V.tensor_copy(kce_wT[:, :], S.ps[0][0:D, 128:128 + D]))
            for n, dst in enumerate((wqT, wkT, woT)):
                st.done(V.tensor_copy(dst[:, :, :], S.ps[1 + n][:, 0:NPAR * D].rearrange("p (n d) -> p n d", d=D)))
            at['wT'] = st.n
            dve.wait_ge(pe_done, 2)
            st.done(V.tensor_copy(S.w1c[D:128, D:128], S.ps[0][D:128, 0:D]))
            st.done(V.tensor_tensor(S.b1c[D:128, :], S.ps[0][D:128, 64:65], L.ksk_b1[D:128, :], ALU.add))
            st.done(V.tensor_tensor(S.out_row[:, :], S.ps[7][:, 0:D], L.out_b[:, :], ALU.add))
            for par in range(2):
                st.done(V.tensor_copy(S.qkT[0:D, :, par, :], S.ps[1 + par][0:D, 0:NPAR * D].rearrange("p (n d) -> p n d", d=D)))
            for half in range(2):
                st.done(V.tensor_copy(S.wv[64 * half:64 * half + 64, :, :],
                                      S.ps[3 + half][64 * half:64 * half + 64, 0:NPAR * D].rearrange("p (n d) -> p n d", d=D)))

        @block.scalar
        def _(act):
            nc.scalar.activation(S.rstd[:, :], S.var[:, :], ACT.Sqrt, bias=S.eps[:, 0:1]).then_inc(rooted, 1)

        @block.tensor
        def _(pe):
            M = nc.tensor.matmul
            pe.wait_ge(dve_done, at['lnbb'])
            idn = S.ident
            nc.tensor.transpose(S.ps[0][0:D, 128:128 + D], L.kce_w[:, :], idn[0:D, 0:D])
            for n, src in enumerate((L.wq, L.wk, L.wo)):
                for k in range(NPAR):
                    last = nc.tensor.transpose(S.ps[1 + n][:, D * k:D * k + D],
                                               src[:, 2 * k:2 * k + 2, :].rearrange("p a b -> p (a b)"), idn[0:D, 0:D])
            last.then_inc(pe_done, 1)
            pe.wait_ge(dve_done, at['wT'])
            M(S.ps[0][D:128, 0:D], kce_wT[:, :], L.ksk_low[:, :], start=True, stop=True)
            M(S.ps[0][D:128, 64:65], L.ksk_low[:, :], L.kce_b[:, :], start=True, stop=True)
            M(S.ps[7][:, 0:D], ln_bb[:, :], L.out_w[0:D, :], start=True, stop=True)
            for par in range(2):
                rows = slice(64 * par, 64 * par + 64)
                for k in range(NPAR):
                    M(S.ps[1 + par][0:D, D * k:D * k + D], wkT[rows, k, :], wqT[rows, k, :], start=True, stop=True)
                    last = M(S.ps[3 + par][rows, D * k:D * k + D], wkT[rows, k, :], woT[rows, k, :], start=True, stop=True)
            last.then_inc(pe_done, 1)


def all_chunks(eng, chunk):
    for c in range(2):
        chunk(c, c, c, True)
    with eng.Fori(1, NCH // 2 - 1) as i:
        for r in range(2):
            chunk(i * 2 + r, r, 2, True)
    for r in range(2):
        chunk(NCH - 2 + r, r, 2, r == 0)


def has_second(c):
    return not isinstance(c, int) or c + 2 < NCH


def measure_h(nc, S, st, c, stats, mv):
    V = nc.vector
    for k in range(CH):
        st.done(V.bn_stats(stats[:, k, :], S.h[:, bass.ds(c * CH + k, 1), :].rearrange("p a d -> p (a d)")))
    st.wait()
    for k in range(CH):
        st.done(V.bn_aggr(mv[:, k, :], stats[:, k, :]))
    st.wait()
    tiles = bass.ds(c * CH, CH)
    st.done(V.tensor_copy(S.mean[:, tiles], mv[:, :, 0]))
    st.do(V.tensor_copy(S.var[:, tiles], mv[:, :, 1]))


def normalise(nc, S, st, dst, tiles):
    V = nc.vector
    st.do(V.tensor_tensor(dst, S.h[:, tiles, :], bc(S.mean[:, tiles].unsqueeze(2), [128, CH, D]), ALU.subtract))
    st.do(V.tensor_tensor(dst, dst, bc(S.rstd[:, tiles].unsqueeze(2), [128, CH, D]), ALU.mult))


def token_stage(nc, S, slot_x, pairs):
    with ExitStack() as ctx:
        sb = lambda n, s, d=F32: ctx.enter_context(nc.sbuf_tensor(n, s, d))
        sem = lambda n: ctx.enter_context(nc.semaphore(n))
        onehot = sb("onehot", [128, 2, W], BF16)
        onehot_last = sb("onehot_last", [3, 2, W], BF16)
        differ = sb("differ", [128, CH, T], I32)
        graph = sb("graph", [128, 2, CH, T])
        pe_sb = sb("pe_sb", [D, 2, CH, T])
        pe_sq = sb("pe_sq", [D, 2, CH, T])
        pe_n = sb("pe_n", [D, CH, T])
        nrm = sb("nrm", [D, 2, CH])
        half = sb("half", [D, CH])
        wgt = sb("wgt", [128, CH])
        stats = sb("token_stats", [128, CH, 6])
        mv = sb("token_mv", [128, CH, 2])

        weights_in = sem("weights_in")
        zeroed = sem("rows_zeroed")
        filled = sem("half_filled")
        embedded = sem("embedded")
        squared = sem("squared")
        rooted = sem("rooted")
        projected = sem("projected")
        h_copied = sem("hn_copied")
        gathered = sem("gathered")
        hot_st = Steps(S, sem("one_hot_steps"), 2)
        graph_st = Steps(S, sem("graph_steps"), 2)
        norm_st = Steps(S, sem("norm_steps"), 4)
        fin_st = Steps(S, sem("token_steps"), 14)

        block = ctx.enter_context(nc.Block())

        @block.sync
        def _(sp):
            for dst, src in pairs:
                sp.dma_start(dst, src, allow_slow_non_contiguous=True).then_inc(weights_in, 16)
            for r in range(0, S.slots, 128 * 32):
                sp.dma_start(slot_x[r:r + 128 * 32, :].rearrange("(p n) d -> p n d", p=128),
                             S.zeros[:, :].rearrange("p (n d) -> p n d", d=D)).then_inc(zeroed, 16)
            sp.wait_ge(weights_in, 16 * len(pairs))
            sp.wait_ge(zeroed, 16 * (S.slots // 4096))

        @block.vector
        def _(dve):
            V = nc.vector

            def mark(c, r, reused):
                hot_st.start(dve, c)
                tok = bass.ds(c * W, W)
                if reused:
                    hold(S, dve, embedded, c - 1)
                hot_st.done(V.tensor_scalar(onehot[:, r, :], S.idx_bc[:, tok], S.iota_part[:, 0:1], None, ALU.is_equal))
                hot_st.done(V.tensor_scalar(onehot_last[:, r, :], S.idx_bc[0:3, tok], float(T), None, ALU.is_equal))
                hot_st.mark("one-hot")
                hot_st.end()

            def connect(c, r, reused):
                graph_st.start(dve, c)
                graph_st.do(V.tensor_tensor(differ[:, :, :], S.x_bc[:, bass.ds(c * W, W)].rearrange("p (b t) -> p b t", t=T),
                                            bc(S.xT[:, bass.ds(c * CH, CH)].unsqueeze(2), [128, CH, T]), ALU.bitwise_xor))
                if reused:
                    hold(S, dve, gathered, c - 1)
                graph_st.do(V.scalar_tensor_tensor(graph[:, r, :, :], differ[:, :, :], 0.0,
                                                   bc(S.triG[:, :].unsqueeze(1), [128, CH, T]), ALU.is_equal, ALU.mult))
                graph_st.mark("graph")
                graph_st.end()

            def sum_squares(c, r):
                norm_st.start(dve, c)
                hold(S, dve, squared, c * 2 + 2)
                norm_st.done(V.reduce_sum(nrm[:, r, :], pe_sq[:, r, :, :], AX.X))
                norm_st.mark("summed")

            def divide(c, r, reused):
                st = norm_st
                hold(S, dve, rooted, c + 1)
                st.do(V.tensor_scalar(nrm[:, r, :], nrm[:, r, :], 1e-12, None, ALU.max))
                st.do(V.reciprocal(nrm[:, r, :], nrm[:, r, :]))
                if reused:
                    hold(S, dve, projected, c)
                st.done(V.tensor_tensor(pe_n[:, :, :], pe_sb[:, r, :, :], bc(nrm[:, r, :].unsqueeze(2), [D, CH, T]), ALU.mult))
                st.mark("divided")
                st.end()

            def finish(c, r):
                st = fin_st
                st.start(dve, c)
                tiles = bass.ds(c * CH, CH)
                out = S.ps[4 + r][:, 0:CH * (D + 1)].rearrange("p (k d) -> p k d", d=D + 1)
                hc = S.h[:, tiles, :]
                hold(S, dve, gathered, c + 1)
                st.do(V.reciprocal(wgt[:, :], out[:, :, D]))
                st.do(V.tensor_tensor(wgt[:, :], wgt[:, :], S.maskT[:, tiles], ALU.mult))
                st.do(V.tensor_tensor(hc, out[:, :, 0:D], bc(wgt[:, :].unsqueeze(2), [128, CH, D]), ALU.mult))
                st.mark("taken")
                st.do(V.tensor_tensor(hc, hc, bc(S.b_oah[:, :].unsqueeze(1), [128, CH, D]), ALU.add))
                measure_h(nc, S, st, c, stats, mv)
                st.end()

            def chunk(c, r, before, after):
                if after:
                    mark(c + 1, 1 - r, before > 0)
                sum_squares(c, r)
                if after:
                    connect(c + 1, 1 - r, before > 0)
                divide(c, r, before > 0)
                if before:
                    finish(c - 1, 1 - r)

            mark(0, 0, False)
            connect(0, 0, False)
            all_chunks(dve, chunk)
            finish(NCH - 1, 1)

        @block.gpsimd
        def _(pool):
            G = nc.gpsimd
            G.memset(half[:, :], 0.5).then_inc(filled, 1)
            pool.wait_ge(filled, 1)

            def chunk(c, r, before, after):
                norm_st.after(pool, "summed", c)
                G.tensor_tensor(nrm[:, r, :], nrm[:, r, :], half[:, :], ALU.pow).then_inc(rooted, 1)

            all_chunks(pool, chunk)

        @block.tensor
        def _(pe):
            M = nc.tensor.matmul

            def embed(c, r, reused):
                hot_st.after(pe, "one-hot", c)
                if reused:
                    hold(S, pe, squared, c * 2 - 2)
                for k in range(3):
                    M(S.ps[r][0:D, :], S.emb3[:, k, :], onehot[:, r, :], start=(k == 0), stop=False)
                M(S.ps[r][0:D, :], S.emb_last3[:, :], onehot_last[:, r, :], start=False, stop=True).then_inc(embedded, 1)

            def chunk(c, r, before, after):
                if after:
                    embed(c + 1, 1 - r, before > 0)
                norm_st.after(pe, "divided", c)
                if before:
                    hold(S, pe, h_copied, c)
                for k in range(CH):
                    last = M(S.ps[2][:, D * k:D * k + D], pe_n[:, k, :], S.w_inT[:, :], start=True, stop=True)
                last.then_inc(projected, 1)
                hold(S, pe, h_copied, c + 1)
                graph_st.after(pe, "graph", c)
                if before == 2:
                    fin_st.after(pe, "taken", c - 2)
                for k in range(CH):
                    last = M(S.ps[4 + r][:, (D + 1) * k:(D + 1) * (k + 1)], graph[:, r, k, :], S.hn[:, r, k, :],
                             start=True, stop=True)
                last.then_inc(gathered, 1)

            embed(0, 0, False)
            all_chunks(pe, chunk)

        @block.scalar
        def _(act):
            N = nc.scalar.activation

            def copy(c, r, reused):
                hold(S, act, embedded, c + 1)
                if reused:
                    norm_st.after(act, "divided", c - 2)
                src = S.ps[r][0:D, :].rearrange("p (k t) -> p k t", t=T)
                N(pe_sb[:, r, :, :], src, ACT.Copy).then_inc(squared, 1)
                N(pe_sq[:, r, :, :], src, ACT.Square).then_inc(squared, 1)

            def chunk(c, r, before, after):
                if after:
                    copy(c + 1, 1 - r, before > 0)
                hold(S, act, projected, c + 1)
                if before == 2:
                    hold(S, act, gathered, c - 1)
                N(S.hn[:, r, :, 0:D], S.ps[2][:, 0:CH * D].rearrange("p (k d) -> p k d", d=D), ACT.Copy).then_inc(h_copied, 1)

            copy(0, 0, False)
            all_chunks(act, chunk)


def project_stage(nc, S, A):
    with ExitStack() as ctx:
        sb = lambda n, s, d=F32: ctx.enter_context(nc.sbuf_tensor(n, s, d))
        sem = lambda n: ctx.enter_context(nc.semaphore(n))
        xr = sb("xr", [128, 2, CH, D])
        xx = sb("xx", [128, 2, W])
        g1 = sb("g1", [128, W])
        g2 = sb("g2", [D // 2, W])

        turned = sem("x_turned")
        xx_copied = sem("xx_copied")
        hidden = sem("hidden")
        gelued = sem("gelued")
        out_ready = sem("proj_ready")
        proj_added = sem("proj_added")
        added = sem("residual_added")
        x_st = Steps(S, sem("project_steps"), 2)

        block = ctx.enter_context(nc.Block())

        @block.vector
        def _(dve):
            V = nc.vector

            def normed(c, r, reused):
                x_st.start(dve, c)
                if reused:
                    hold(S, dve, turned, c - 1)
                    hold(S, dve, added, c - 1)
                normalise(nc, S, x_st, xr[:, r, :, :], bass.ds(c * CH, CH))
                x_st.mark("x")
                x_st.end()

            def chunk(c, r, before, after):
                hold(S, dve, out_ready, c + 1)
                V.tensor_tensor(S.proj[:, bass.ds(c * CH, CH), :], S.bank[:, 4:8, 0:NPROJ],
                                bc(S.proj_b[:, :].unsqueeze(1), [128, CH, NPROJ]), ALU.add).then_inc(proj_added, 1)
                if has_second(c):
                    normed(c + 2, r, True)

            for c in range(2):
                normed(c, c, False)
            all_chunks(dve, chunk)

        @block.gpsimd
        def _(pool):
            def chunk(c, r, before, after):
                tiles = bass.ds(c * CH, CH)
                x_st.after(pool, "x", c)
                nc.gpsimd.tensor_tensor(S.h[:, tiles, :], S.h[:, tiles, :], xr[:, r, :, :], ALU.add).then_inc(added, 1)

            all_chunks(pool, chunk)

        @block.tensor
        def _(pe):
            M = nc.tensor.matmul

            def turn_x(c, r):
                x_st.after(pe, "x", c)
                for k in range(CH):
                    t = slice(T * k, T * k + T)
                    nc.tensor.transpose(S.ps[0][0:D, t], xr[:, r, k, :], S.ident[:, :])
                    last = M(S.ps[0][D:128, t], xr[:, r, k, :], S.cmean[:, :], start=True, stop=True)
                last.then_inc(turned, 1)

            def chunk(c, r, before, after):
                hold(S, pe, xx_copied, c + 1)
                M(S.ps[2][:, :], S.w1c[:, :], xx[:, r, :], start=True, stop=False)
                M(S.ps[2][:, :].rearrange("p (k t) -> p k t", t=T), S.w1p[:, :], bc(S.ppT[:, :].unsqueeze(1), [128, CH, T]),
                  start=False, stop=True)
                M(S.ps[1][0:D // 2, :], S.sg_w1[:, :], xx[:, r, :], start=True, stop=True).then_inc(hidden, 1)
                if after:
                    turn_x(c + 1, 1 - r)
                if before:
                    hold(S, pe, proj_added, c)
                for k in range(CH):
                    M(S.ps[4 + k][:, KY:NPROJ], xx[:, r, T * k:T * k + T], S.wx[:, :], start=True, stop=True)
                hold(S, pe, gelued, c * 2 + 1)
                for k in range(CH):
                    M(S.ps[4 + k][:, 0:GT], g1[:, T * k:T * k + T], S.w2c[:, :], start=True, stop=True)
                hold(S, pe, gelued, c * 2 + 2)
                for k in range(CH):
                    last = M(S.ps[4 + k][:, GT:KY], g2[:, T * k:T * k + T], S.sg_w2[:, :], start=True, stop=True)
                last.then_inc(out_ready, 1)

            turn_x(0, 0)
            all_chunks(pe, chunk)

        @block.scalar
        def _(act):
            N = nc.scalar.activation

            def copy_x(c, r):
                hold(S, act, turned, c + 1)
                N(xx[:, r, :], S.ps[0][:, :], ACT.Copy).then_inc(xx_copied, 1)

            def chunk(c, r, before, after):
                hold(S, act, hidden, c + 1)
                N(g1[:, :], S.ps[2][:, :], ACT.Gelu, bias=S.b1c[:, 0:1]).then_inc(gelued, 1)
                N(g2[:, :], S.ps[1][0:D // 2, :], ACT.Gelu, bias=S.sg_b1[:, 0:1]).then_inc(gelued, 1)
                if after:
                    copy_x(c + 1, 1 - r)

            copy_x(0, 0)
            all_chunks(act, chunk)


def phase_stage(nc, S, A):
    NQ = (NH + 1) * P
    NA = NQ + P
    with ExitStack() as ctx:
        sb = lambda n, s, d=F32: ctx.enter_context(nc.sbuf_tensor(n, s, d))
        sem = lambda n: ctx.enter_context(nc.semaphore(n))
        cosn = sb("cosn", [128, B, NA])
        sinn = sb("sinn", [128, B, NQ])
        width = sb("width", [128, B, NH])
        gate = sb("gate", [128, B])
        wexp = sb("wexp", [128, B * NH, NW])
        wprod = sb("wprod", [128, 2, B * NH, NW])
        wsum = sb("wsum", [128, B * NH])
        along = sb("along", [128, 2, B * NH])
        kscale = sb("kscale", [128, B])
        power = sb("gate_power", [128, B])
        t_c = sb("t_c", [128, 2, 2 * CH, NH * P])
        t_s = [sb(f"t_s{k}", [128, 2, 2 * CH, NH * P]) for k in range(2)]
        r_c = sb("r_c", [128, 2, 2 * CH, P])
        r_s = sb("r_s", [128, 2, 2 * CH, P])

        tanhs = sem("tanhs")
        exped = sem("exped")
        filled = sem("power_filled")
        rooted = sem("gate_rooted")
        summed = sem("gates_summed")
        trig = sem("trig")
        sized = sem("sized")
        pre = Steps(S, sem("weights_steps"))
        gated = sem("gated")
        st = Steps(S, sem("phase_steps"), 13)
        ps = Steps(S, sem("phase_pool_steps"), 4)
        sines = sem("sines_summed")

        block = ctx.enter_context(nc.Block())

        def combine(eng, st, t, hop, t4, al, first, second, op):
            st.done(eng.tensor_tensor(t4(t, 0), hop(first[0]), al(first[1]), ALU.mult))
            st.do(eng.tensor_tensor(t4(t, 1), hop(second[0]), al(second[1]), ALU.mult))
            st.do(eng.tensor_tensor(t[:, 0, :, :], t[:, 0, :, :], t[:, 1, :, :], op))
            st.do(eng.tensor_tensor(t[:, 0, :, 0:2 * P], t[:, 0, :, 0:2 * P], t[:, 0, :, 2 * P:4 * P], ALU.add))
            return eng.tensor_tensor(t[:, 0, :, 0:P], t[:, 0, :, 0:P], t[:, 0, :, P:2 * P], ALU.add)

        @block.vector
        def _(dve):
            V = nc.vector
            pre.start(dve)
            do = pre.do
            dve.wait_ge(tanhs, 2)
            do(V.tensor_scalar(gate[:, :], gate[:, :], 0.5, 0.5, ALU.mult, ALU.add))
            pre.mark("gate")
            do(V.tensor_scalar(width[:, :, :], width[:, :, :], 1.1, None, ALU.add))
            do(V.tensor_tensor(width[:, :, :], width[:, :, :], width[:, :, :], ALU.mult))
            do(V.tensor_scalar(width[:, :, :], width[:, :, :], 1e-6, None, ALU.add))
            wv = width[:, :, :].rearrange("p b h -> p (b h)")
            do(V.reciprocal(wv, wv))
            do(V.tensor_tensor(wexp[:, :, :], bc(wv.unsqueeze(2), [128, B * NH, NW]),
                               bc(S.nhd2[:, :].unsqueeze(1), [128, B * NH, NW]), ALU.mult))
            pre.mark("exponents")
            dve.wait_ge(summed, 1)
            do(V.tensor_scalar(kscale[:, :], S.ps[0][:, 0:B], 1.0, float(P), ALU.max, ALU.mult))
            pre.mark("gate sum")
            dve.wait_ge(exped, 1)
            do(V.reduce_sum(wsum[:, :], wexp[:, :, :], AX.X))
            do(V.tensor_scalar(wsum[:, :], wsum[:, :], 1e-6, None, ALU.add))
            do(V.reciprocal(wsum[:, :], wsum[:, :]))
            do(V.tensor_scalar(wsum[:, :], wsum[:, :], 1.0 / (NH * P ** 0.5), None, ALU.mult))
            for k in range(2):
                pre.done(V.tensor_tensor(wprod[:, k, :, :], wexp[:, :, :], bc(S.dcs[:, k, :].unsqueeze(1), [128, B * NH, NW]),
                                         ALU.mult))
            pre.wait()
            for k in range(2):
                pre.done(V.reduce_sum(along[:, k, :], wprod[:, k, :, :], AX.X))
            pre.wait()
            for k in range(2):
                pre.done(V.tensor_tensor(along[:, k, :], along[:, k, :], wsum[:, :], ALU.mult))
            pre.wait()
            dve.wait_ge(rooted, 1)
            pre.mark("weights")
            def turn(i, ts):
                st.start(dve, i)
                two = bass.ds(i * (2 * CH), 2 * CH)
                hop = lambda t: t[:, two, 0:NH * P].rearrange("p b (h f) -> p b h f", f=P)
                t4 = lambda t, k: t[:, k, :, :].rearrange("p b (h f) -> p b h f", f=P)
                al = lambda k: bc(along[:, k, :].rearrange("p (b h) -> p b h", h=NH)[:, two, :].unsqueeze(3),
                                  [128, 2 * CH, NH, P])
                hold(S, dve, trig, i * 4 + 4)
                st.do(combine(nc.vector, st, t_c, hop, t4, al, (cosn, 0), (sinn, 1), ALU.subtract))
                hold(S, dve, sines, i + 1)
                pc = bc(S.pcs[:, 0, :].unsqueeze(1), [128, 2 * CH, P])
                pn = bc(S.pcs[:, 1, :].unsqueeze(1), [128, 2 * CH, P])
                st.done(V.tensor_tensor(r_c[:, 0, :, :], t_c[:, 0, :, 0:P], pc, ALU.mult))
                st.done(V.tensor_tensor(r_c[:, 1, :, :], ts[:, 0, :, 0:P], pn, ALU.mult))
                st.done(V.tensor_tensor(r_s[:, 0, :, :], t_c[:, 0, :, 0:P], pn, ALU.mult))
                st.do(V.tensor_tensor(r_s[:, 1, :, :], ts[:, 0, :, 0:P], pc, ALU.mult))
                st.mark("turned")
                st.done(V.tensor_tensor(S.q_pos[:, two, 0:P], r_c[:, 0, :, :], r_c[:, 1, :, :], ALU.subtract))
                st.done(V.tensor_tensor(S.q_pos[:, two, P:2 * P], r_s[:, 0, :, :], r_s[:, 1, :, :], ALU.add))
                ks = bc(kscale[:, two].unsqueeze(2), [128, 2 * CH, P])
                ky = slice(NH * P, NQ)
                st.done(V.tensor_tensor(S.q_kv[:, two, 0:P], cosn[:, two, ky], ks, ALU.mult))
                st.done(V.tensor_tensor(S.q_kv[:, two, P:2 * P], sinn[:, two, ky], ks, ALU.mult))
                st.wait()
                st.end()

            with dve.Fori(0, NCH // 4) as j:
                for k in range(2):
                    turn(j * 2 + k, t_s[k])

        @block.gpsimd
        def _(pool):
            G = nc.gpsimd
            G.memset(power[:, :], -0.5).then_inc(filled, 1)
            pool.wait_ge(filled, 1)
            pre.after(pool, "gate sum")
            G.tensor_tensor(kscale[:, :], kscale[:, :], power[:, :], ALU.pow).then_inc(rooted, 1)
            pre.after(pool, "gate")
            G.tensor_tensor(S.gv[:, :, :], S.proj[:, :, VL:NPROJ], bc(gate[:, :].unsqueeze(2), [128, B, D]),
                            ALU.mult).then_inc(gated, 1)
            pre.after(pool, "weights")

            def turn(i, ts):
                ps.start(pool, i)
                two = bass.ds(i * (2 * CH), 2 * CH)
                hop = lambda t: t[:, two, 0:NH * P].rearrange("p b (h f) -> p b h f", f=P)
                t4 = lambda t, k: t[:, k, :, :].rearrange("p b (h f) -> p b h f", f=P)
                al = lambda k: bc(along[:, k, :].rearrange("p (b h) -> p b h", h=NH)[:, two, :].unsqueeze(3),
                                  [128, 2 * CH, NH, P])
                hold(S, pool, trig, i * 4 + 4)
                combine(nc.gpsimd, ps, ts, hop, t4, al, (cosn, 1), (sinn, 0), ALU.add).then_inc(sines, 1)
                ps.end()

            with pool.Fori(0, NCH // 4) as j:
                for k in range(2):
                    turn(j * 2 + k, t_s[k])
                st.after(pool, "turned", j * 2 + 1)

        @block.tensor
        def _(pe):
            pre.after(pe, "gate")
            nc.tensor.matmul(S.ps[0][:, 0:B], S.triC[:, :], gate[:, :], start=True, stop=True).then_inc(summed, 1)

        @block.scalar
        def _(act):
            N = nc.scalar.activation
            N(width[:, :, :], S.proj[:, :, AO:ST].rearrange("p b (h f) -> p b h f", f=HP)[:, :, :, P], ACT.Tanh,
              scale=0.5).then_inc(tanhs, 1)
            N(gate[:, :], S.proj[:, :, GT], ACT.Tanh, scale=0.5).then_inc(tanhs, 1)
            N(cosn[:, :, 0:NH * P].rearrange("p b (h f) -> p b h f", f=P),
              S.proj[:, :, AO:ST].rearrange("p b (h f) -> p b h f", f=HP)[:, :, :, 0:P], ACT.Tanh)
            N(cosn[:, :, NH * P:NQ], S.proj[:, :, KY:CT], ACT.Tanh)
            N(cosn[:, :, NQ:NA], S.proj[:, :, ST:GT], ACT.Tanh).then_inc(tanhs, 1)
            pre.after(act, "exponents")
            N(wexp[:, :, :], wexp[:, :, :], ACT.Exp).then_inc(exped, 1)
            act.wait_ge(tanhs, 3)
            with act.Fori(0, NCH // 2) as i:
                two = bass.ds(i * (2 * CH), 2 * CH)
                N(sinn[:, two, :], cosn[:, two, 0:NQ], ACT.Sin, scale=PI_BELOW).then_inc(trig, 1)
                N(S.k_kv[:, two, P:2 * P], cosn[:, two, NQ:NA], ACT.Sin, scale=PI_BELOW).then_inc(trig, 1)
                hold(S, act, trig, i * 4 + 2)
                N(cosn[:, two, :], cosn[:, two, :], ACT.Abs).then_inc(sized, 1)
                hold(S, act, sized, i + 1)
                N(cosn[:, two, 0:NQ], cosn[:, two, 0:NQ], ACT.Sin, scale=-PI_BELOW, bias=S.half_pi[:, 0:1]).then_inc(trig, 1)
                N(S.k_kv[:, two, 0:P], cosn[:, two, NQ:NA], ACT.Sin, scale=-PI_BELOW, bias=S.half_pi[:, 0:1]).then_inc(trig, 1)


def memory_stage(nc, S, A):
    with ExitStack() as ctx:
        sb = lambda n, s, d=F32: ctx.enter_context(nc.sbuf_tensor(n, s, d))
        sem = lambda n: ctx.enter_context(nc.semaphore(n))
        rows = sb("qk_rows", [128, 2, 2, CH, 2 * P + D])
        qkT = sb("qk_turned", [128, 2, W])
        masked = sb("masked", [128, 2, CH, T])
        comb = sb("comb", [128, CH, D])
        combT = sb("combT", [128, CH // 2, T])
        stats = sb("comb_stats", [128, CH, 6])
        mv = sb("comb_mv", [128, CH, 2])
        dev = sb("comb_dev", [128, CH])
        power = sb("comb_power", [128, CH])
        stats_f = sb("h_stats", [128, CH, 6])
        mv_f = sb("h_mv", [128, CH, 2])

        padded = sem("rows_padded")
        copied = sem("rows_copied")
        turned = sem("qk_turned")
        evacuated = sem("qkT_copied")
        scored = sem("scored")
        masks_done = sem("scores_masked")
        retrieved = sem("retrieved")
        rooted = sem("comb_rooted")
        comb_turned = sem("comb_turned")
        combT_copied = sem("combT_copied")
        out_ready = sem("out_ready")
        biased = sem("h_biased")
        norm_st = Steps(S, sem("normalise_steps"), 11)
        fin_st = Steps(S, sem("add_out_steps"), 12)

        block = ctx.enter_context(nc.Block())

        @block.vector
        def _(dve):
            V = nc.vector

            def measure(c):
                st = norm_st
                st.start(dve, c)
                hold(S, dve, retrieved, c + 1)
                for t in range(CH):
                    st.done(V.bn_stats(stats[:, t, :], S.ps[4][:, D * t:D * t + D]))
                st.wait()
                for t in range(CH):
                    st.done(V.bn_aggr(mv[:, t, :], stats[:, t, :]))
                st.wait()
                st.do(V.tensor_scalar(dev[:, :], mv[:, :, 1], EPS, None, ALU.add))
                st.mark("variance")

            def scale(c):
                st = norm_st
                hold(S, dve, rooted, c + 1)
                st.do(V.tensor_tensor(comb[:, :, :], S.ps[4][:, 0:CH * D].rearrange("p (k d) -> p k d", d=D),
                                      bc(mv[:, :, 0].unsqueeze(2), [128, CH, D]), ALU.subtract))
                st.do(V.tensor_tensor(comb[:, :, :], comb[:, :, :], bc(dev[:, :].unsqueeze(2), [128, CH, D]), ALU.mult))
                st.mark("comb")
                st.end()

            def mask(c):
                hold(S, dve, scored, c + 1)
                for m in range(2):
                    V.tensor_tensor(masked[:, m, :, :], S.ps[2 + m][:, :].rearrange("p (n t) -> p n t", t=T),
                                    bc(S.triC[:, :].unsqueeze(1), [128, CH, T]), ALU.mult).then_inc(masks_done, 1)

            def finish(c):
                st = fin_st
                st.start(dve, c)
                hold(S, dve, out_ready, c + 1)
                hold(S, dve, biased, c + 1)
                hv = S.h[:, :, :].rearrange("p (n j a) d -> p n a j d", j=CH // 2, a=2)
                for a in range(2):
                    hh = hv[:, bass.ds(c, 1), a, :, :].rearrange("p n j d -> p (n j) d")
                    st.done(V.tensor_tensor(hh, hh, S.ps[6 + a][:, 0:CH // 2 * D].rearrange("p (j d) -> p j d", d=D), ALU.add))
                st.mark("added")
                st.wait()
                measure_h(nc, S, st, c, stats_f, mv_f)
                st.end()

            def chunk(c, r, before, after):
                if before:
                    measure(c - 1)
                    scale(c - 1)
                mask(c)
                if before == 2:
                    finish(c - 2)

            all_chunks(dve, chunk)
            measure(NCH - 1)
            finish(NCH - 2)
            scale(NCH - 1)
            finish(NCH - 1)

        @block.gpsimd
        def _(pool):
            G = nc.gpsimd
            for r in range(2):
                G.memset(rows[:, r, 1, :, 0:2 * P], 0.0).then_inc(padded, 1)
            G.memset(power[:, :], -0.5).then_inc(padded, 1)
            pool.wait_ge(padded, 3)

            def fill(c, r, reused):
                if reused:
                    hold(S, pool, turned, c - 1)
                tiles = bass.ds(c * CH, CH)
                G.tensor_copy(rows[:, r, 0, :, 0:2 * P], S.q_pos[:, tiles, :]).then_inc(copied, 1)
                G.tensor_copy(rows[:, r, 0, :, 2 * P:2 * P + D], S.q_kv[:, tiles, :]).then_inc(copied, 1)
                G.tensor_copy(rows[:, r, 1, :, 2 * P:2 * P + D], S.k_kv[:, tiles, :]).then_inc(copied, 1)

            def root(c):
                norm_st.after(pool, "variance", c)
                G.tensor_tensor(dev[:, :], dev[:, :], power[:, :], ALU.pow).then_inc(rooted, 1)

            def chunk(c, r, before, after):
                if before:
                    root(c - 1)
                if has_second(c):
                    fill(c + 2, r, True)
                tiles = bass.ds(c * CH, CH)
                G.tensor_tensor(S.h[:, tiles, :], S.h[:, tiles, :], bc(S.out_row[:, :].unsqueeze(1), [128, CH, D]),
                                ALU.add).then_inc(biased, 1)

            for c in range(2):
                fill(c, c, False)
            all_chunks(pool, chunk)
            root(NCH - 1)

        @block.tensor
        def _(pe):
            M = nc.tensor.matmul

            def turn_rows(c, r):
                hold(S, pe, copied, c * 3 + 3)
                for m in range(2):
                    for k in range(CH):
                        last = nc.tensor.transpose(S.ps[m][:, T * k:T * k + T], rows[:, r, m, k, :], S.ident[:, :])
                last.then_inc(turned, 1)

            def score(c):
                hold(S, pe, evacuated, c * 2 + 2)
                M(S.ps[2][:, :], S.pcsT[:, :], qkT[:, 0, :], start=True, stop=True)
                for k in range(CH):
                    t = slice(T * k, T * k + T)
                    last = M(S.ps[3][:, t], qkT[:, 1, t], qkT[:, 0, t], start=True, stop=True)
                last.then_inc(scored, 1)

            def retrieve(c):
                hold(S, pe, masks_done, c * 2 + 2)
                for k in range(CH):
                    tile = bass.ds(c * CH + k, 1)
                    M(S.ps[4][:, D * k:D * k + D], masked[:, 0, k, :],
                      S.proj[:, tile, CT:VL].rearrange("p a d -> p (a d)"), start=True, stop=False)
                    last = M(S.ps[4][:, D * k:D * k + D], masked[:, 1, k, :],
                             S.gv[:, tile, :].rearrange("p a d -> p (a d)"), start=False, stop=True)
                last.then_inc(retrieved, 1)

            def turn_comb(c):
                norm_st.after(pe, "comb", c)
                for j in range(CH // 2):
                    last = nc.tensor.transpose(S.ps[5][:, T * j:T * j + T],
                                               comb[:, 2 * j:2 * j + 2, :].rearrange("p b d -> p (b d)"), S.ident[:, :])
                last.then_inc(comb_turned, 1)

            def project(c, reused):
                hold(S, pe, combT_copied, c + 1)
                if reused:
                    fin_st.after(pe, "added", c - 1)
                for a in range(2):
                    half = slice(64 * a, 64 * a + 64)
                    for j in range(CH // 2):
                        last = M(S.ps[6 + a][:, D * j:D * j + D], combT[half, j, :], S.out_w2[half, :], start=True, stop=True)
                last.then_inc(out_ready, 1)

            def chunk(c, r, before, after):
                score(c)
                if after:
                    turn_rows(c + 1, 1 - r)
                if before:
                    turn_comb(c - 1)
                retrieve(c)
                if before:
                    project(c - 1, before == 2)

            turn_rows(0, 0)
            all_chunks(pe, chunk)
            turn_comb(NCH - 1)
            project(NCH - 1, True)

        @block.scalar
        def _(act):
            N = nc.scalar.activation

            def copy_rows(c):
                hold(S, act, turned, c + 1)
                for m in range(2):
                    N(qkT[:, m, :], S.ps[m][:, :], ACT.Copy).then_inc(evacuated, 1)

            def copy_comb(c):
                hold(S, act, comb_turned, c + 1)
                N(combT[:, :, :].rearrange("p j t -> p (j t)"), S.ps[5][:, 0:CH // 2 * T], ACT.Copy).then_inc(combT_copied, 1)

            def chunk(c, r, before, after):
                if after:
                    copy_rows(c + 1)
                if before:
                    copy_comb(c - 1)

            copy_rows(0)
            all_chunks(act, chunk)
            copy_comb(NCH - 1)


def root_stage(nc, S, name):
    with ExitStack() as ctx:
        rooted = ctx.enter_context(nc.semaphore(name))
        block = ctx.enter_context(nc.Block())

        @block.scalar
        def _(act):
            nc.scalar.activation(S.rstd[:, :], S.var[:, :], ACT.Sqrt, bias=S.eps[:, 0:1]).then_inc(rooted, 1)

        @block.vector
        def _(dve):
            dve.wait_ge(rooted, 1)
            nc.vector.reciprocal(S.rstd[:, :], S.rstd[:, :])


def route_stage(nc, S, A):
    NQ = 4
    QB = B // NQ
    with ExitStack() as ctx:
        sb = lambda n, s, d=F32: ctx.enter_context(nc.sbuf_tensor(n, s, d))
        sem = lambda n: ctx.enter_context(nc.semaphore(n))
        xr = sb("xr0", [128, 2, CH, D])
        xT = sb("xT0", [D, 2, W])
        logits = sb("logits", [128, CH, E0])
        top = sb("top", [128, CH, 8])
        top_i = sb("top_i", [128, CH, 8], U32)
        top_f = sb("top_f", [128, CH, 2])
        hot = sb("hot", [128, 2, B, E0], BF16)
        both = sb("both", [128, B, E0], BF16)
        before = sb("before", [128, E0, B])
        carry = sb("carry", [128, E0, B])
        slot_m = sb("slot_m", [128, B, E0])
        picked = sb("picked", [128, 2, B, E0])
        n_tiles = sb("n_tiles", [128, E0])
        ends = sb("ends", [128, E0])
        base = sb("base", [128, E0])
        slot_f = sb("slot_f", [128, 2, B])
        past = sb("past", [128, E0])
        first_slot = sb("first_slot", [128, 1])
        owner = sb("owner", [128, 1])
        comb = sb("comb0", [128, 2, CH, E0])
        comb2 = sb("comb20", [128, 2, CH, E0])
        combT = sb("combT0", [E0, 2, W])

        turned = sem("x_turned0")
        xT_copied = sem("xT_copied0")
        scored = sem("router_scored")
        rooted = sem("h_rooted")
        kept = sem("x_kept")
        x_st = Steps(S, sem("route_x_steps"), 2)
        st = Steps(S, sem("route_steps"), 14)
        sl = Steps(S, sem("slot_steps"))
        counted = sem("counted")
        exped = sem("gate_exped")
        owner_turned = sem("owner_turned")
        scattered = [sem(f"scattered{k}") for k in range(2)]
        cb = Steps(S, sem("b2_steps"), 8)
        c_turned = sem("comb0_turned")
        c_copied = sem("comb0_copied")
        b2_ready = sem("b2_ready")

        block = ctx.enter_context(nc.Block())

        @block.sync
        def _(sp):
            sp.dma_start(S.w1_0[0:D, :, :], A["w1_0"].rearrange("e d h -> d e h")).then_inc(S.experts_in, 16)
            sp.dma_start(S.w1_0[D:D + 1, :, :].rearrange("p e h -> p (e h)"), A["b1_0"].rearrange("(o e) h -> o (e h)", o=1)
                         ).then_inc(S.experts_in, 16)
            sp.dma_start(S.w2_0[:, :, :], A["w2_0"].rearrange("e h d -> h e d")).then_inc(S.experts_in, 16)
            sp.dma_start(S.b2_0[:, :], A["b2_0"]).then_inc(S.experts_in, 16)

        @block.vector
        def _(dve):
            V = nc.vector

            def normed(c, r, reused):
                x_st.start(dve, c)
                if reused:
                    hold(S, dve, turned, c - 1)
                    hold(S, dve, kept, c - 1)
                normalise(nc, S, x_st, xr[:, r, :, :], bass.ds(c * CH, CH))
                x_st.mark("x")
                x_st.end()

            def chunk(c, r, before, after):
                if before and after:
                    normed(c + 1, 1 - r, True)
                st.start(dve, c)
                tiles = bass.ds(c * CH, CH)
                hold(S, dve, scored, c + 1)
                st.do(V.tensor_tensor(logits[:, :, :], S.ps[2 + r][:, 0:CH * E0].rearrange("p (k e) -> p k e", e=E0),
                                      bc(S.br0[:, :].unsqueeze(1), [128, CH, E0]), ALU.add))
                st.mark("logits")
                for k in range(CH):
                    st.done(V.max(top[:, k, :], logits[:, k, :]))
                st.wait()
                for k in range(CH):
                    st.done(V.max_index(top_i[:, k, :], top[:, k, :], logits[:, k, :]))
                st.done(V.tensor_tensor(S.gates[:, 1, tiles], top[:, :, 1], top[:, :, 0], ALU.subtract))
                st.wait()
                st.do(V.tensor_copy(top_f[:, :, :], top_i[:, :, 0:2]))
                for j in range(2):
                    st.done(V.tensor_tensor(hot[:, j, tiles, :], bc(S.iota_free[:, 0:E0].unsqueeze(1), [128, CH, E0]),
                                            bc(top_f[:, :, j:j + 1], [128, CH, E0]), ALU.is_equal))
                st.wait()
                st.do(V.tensor_tensor(both[:, tiles, :], hot[:, 0, tiles, :], hot[:, 1, tiles, :], ALU.add))
                st.end()

            sl.start(dve)
            do = sl.do
            do(V.memset(carry[:, :, :], 1.0))
            do(V.memset(carry[:, :, 0:1], 0.0))
            dve.wait_ge(rooted, 1)
            do(V.reciprocal(S.rstd[:, :], S.rstd[:, :]))
            for c in range(2):
                normed(c, c, False)
            all_chunks(dve, chunk)
            hold(S, dve, kept, NCH)
            do(V.memset(first_slot[:, :], 128.0))
            sl.mark("routed")
            dve.wait_ge(exped, 1)
            do(V.tensor_scalar(S.gates[:, 0, :], S.gates[:, 1, :], 1.0, None, ALU.add))
            do(V.reciprocal(S.gates[:, 0, :], S.gates[:, 0, :]))
            do(V.tensor_tensor(S.gates[:, 1, :], S.gates[:, 1, :], S.gates[:, 0, :], ALU.mult))
            dve.wait_ge(counted, 1)
            do(V.tensor_tensor_scan(before[:, :, :].rearrange("p e b -> p (e b)"), carry[:, :, :].rearrange("p e b -> p (e b)"),
                                    S.bank[:, 4:8, :].rearrange("p n f -> p (n f)"), 0.0, ALU.mult, ALU.add))
            do(V.tensor_scalar(n_tiles[:, :], before[:, :, B - 1], 1.0 / 128, 63.5 / 128, ALU.mult, ALU.add))
            do(V.tensor_scalar(n_tiles[:, :], n_tiles[:, :], ROUND, None, ALU.add))
            do(V.tensor_scalar(n_tiles[:, :], n_tiles[:, :], -ROUND, 128.0, ALU.add, ALU.mult))
            do(V.tensor_tensor_scan(ends[:, :], bc(carry[:, 0, 1:2], [128, E0]),
                                    n_tiles[:, :], 0.0, ALU.mult, ALU.add))
            do(V.tensor_tensor(base[:, :], ends[:, :], n_tiles[:, :], ALU.subtract))
            dve.wait_ge(counted, 2)
            for n in range(NQ):
                q = slice(QB * n, QB * n + QB)
                do(V.tensor_tensor(before[:, :, q], before[:, :, q], bc(base[:, :].unsqueeze(2), [128, E0, QB]), ALU.add))
                do(V.tensor_tensor(slot_m[:, q, :], S.ps[n][:, :].rearrange("p (b e) -> p b e", e=E0),
                                   before[:, :, q].rearrange("p e b -> p b e"), ALU.add))
                for c in range(2):
                    sl.done(V.tensor_tensor(picked[:, c, q, :], hot[:, c, q, :], slot_m[:, q, :], ALU.mult))
                sl.wait()
                for c in range(2):
                    sl.done(V.reduce_sum(slot_f[:, c, q], picked[:, c, q, :], AX.X))
                sl.wait()
                do(V.tensor_copy(S.slot_u[:, :, q], slot_f[:, :, q]))
                sl.mark(("slots", n))
            do(V.tensor_tensor(first_slot[:, :], S.iota_part[:, :], first_slot[:, :], ALU.mult))
            do(V.tensor_scalar(past[:, :], ends[:, :], first_slot[:, 0:1], None, ALU.is_le))
            do(V.reduce_sum(owner[:, :], past[:, :], AX.X))
            do(V.tensor_scalar(owner[:, :], owner[:, :], float(E0 - 1), None, ALU.min))
            sl.mark("owner")
            dve.wait_ge(owner_turned, 1)
            do(V.tensor_copy(S.owner_row[:, :], S.ps[0][0:1, 0:128]))
            sl.mark("owner row")
            with dve.Fori(0, NCH // 2) as i:
                cb.start(dve, i)
                for r in range(2):
                    tiles = bass.ds(i * (2 * CH) + r * CH, CH)
                    cb.done(V.tensor_tensor(comb[:, r, :, :], hot[:, 0, tiles, :],
                                            bc(S.gates[:, 0, tiles].unsqueeze(2), [128, CH, E0]), ALU.mult))
                    cb.do(V.tensor_tensor(comb2[:, r, :, :], hot[:, 1, tiles, :],
                                          bc(S.gates[:, 1, tiles].unsqueeze(2), [128, CH, E0]), ALU.mult))
                    cb.do(V.tensor_tensor(comb[:, r, :, :], comb[:, r, :, :], comb2[:, r, :, :], ALU.add))
                    cb.mark(("comb", r))
                for r in range(2):
                    tiles = bass.ds(i * (2 * CH) + r * CH, CH)
                    hold(S, dve, b2_ready, i * 2 + r + 1)
                    cb.do(V.tensor_tensor(S.h[:, tiles, :], S.h[:, tiles, :],
                                          S.ps[4 + r][:, 0:CH * D].rearrange("p (k d) -> p k d", d=D), ALU.add))
                cb.end()

        @block.gpsimd
        def _(pool):
            def keep(c, r, before, after):
                x_st.after(pool, "x", c)
                nc.gpsimd.tensor_copy(S.xn[:, bass.ds(c * CH, CH), :], xr[:, r, :, :]).then_inc(kept, 1)

            all_chunks(pool, keep)
            pool.wait_ge(kept, NCH)
            for b in range(B):
                if b % QB == 0:
                    sl.after(pool, ("slots", b // QB))
                for c in range(2):
                    nc.gpsimd.indirect_dma_start(A["slot_x"], bass.IndirectOffsetOnAxis(ap=S.slot_u[:, c, b:b + 1], axis=0),
                                                 S.xn[:, b, :], None).then_inc(scattered[c], 16)
            for c in range(2):
                pool.wait_ge(scattered[c], 16 * B)

        @block.tensor
        def _(pe):
            M = nc.tensor.matmul

            def router(c, r, reused):
                x_st.after(pe, "x", c)
                for k in range(CH):
                    last = nc.tensor.transpose(S.ps[r][0:D, T * k:T * k + T], xr[:, r, k, :], S.ident[:, :])
                last.then_inc(turned, 1)
                hold(S, pe, xT_copied, c + 1)
                if reused:
                    st.after(pe, "logits", c - 2)
                for k in range(CH):
                    last = M(S.ps[2 + r][:, E0 * k:E0 * k + E0], xT[:, r, T * k:T * k + T], S.wr0[:, :], start=True, stop=True)
                last.then_inc(scored, 1)

            def chunk(c, r, before, after):
                if after:
                    router(c + 1, 1 - r, before > 0)

            router(0, 0, False)
            all_chunks(pe, chunk)
            sl.after(pe, "routed")
            for n in range(4):
                last = M(S.ps[4 + n][:, :].rearrange("p (e b) -> p e b", b=B), S.ones_bf[:, :],
                         both[:, :, E0 // 4 * n:E0 // 4 * (n + 1)].rearrange("p b e -> p e b"), start=True, stop=True)
            last.then_inc(counted, 1)
            for n in range(4):
                last = M(S.ps[n][:, :], S.triS[:, :], both[:, 8 * n:8 * n + 8, :].rearrange("p b e -> p (b e)"),
                         start=True, stop=True)
            last.then_inc(counted, 1)
            sl.after(pe, "owner")
            nc.tensor.transpose(S.ps[0][0:1, 0:128], owner[:, :], S.ident[:, :]).then_inc(owner_turned, 1)
            sl.after(pe, "owner row")
            pe.wait_ge(S.experts_in, 64)
            with pe.Fori(0, NCH // 2) as i:
                for r in range(2):
                    cb.after(pe, ("comb", r), i)
                    for k in range(CH):
                        last = nc.tensor.transpose(S.ps[r][0:E0, T * k:T * k + T], comb[:, r, k, :], S.ident[:, :])
                    last.then_inc(c_turned, 1)
                for r in range(2):
                    hold(S, pe, c_copied, i * 2 + r + 1)
                    for k in range(CH):
                        last = M(S.ps[4 + r][:, D * k:D * k + D], combT[:, r, T * k:T * k + T], S.b2_0[:, :], start=True, stop=True)
                    last.then_inc(b2_ready, 1)

        @block.scalar
        def _(act):
            N = nc.scalar.activation
            N(S.rstd[:, :], S.var[:, :], ACT.Sqrt, bias=S.eps[:, 0:1]).then_inc(rooted, 1)

            def chunk(c, r, before, after):
                hold(S, act, turned, c + 1)
                N(xT[:, r, :], S.ps[r][0:D, :], ACT.Copy).then_inc(xT_copied, 1)

            all_chunks(act, chunk)
            sl.after(act, "routed")
            N(S.gates[:, 1, :], S.gates[:, 1, :], ACT.Exp).then_inc(exped, 1)
            with act.Fori(0, NCH // 2) as i:
                for r in range(2):
                    hold(S, act, c_turned, i * 2 + r + 1)
                    N(combT[:, r, :], S.ps[r][0:E0, :], ACT.Copy).then_inc(c_copied, 1)


def experts_stage(nc, S, A):
    NG = S.slots // W
    with ExitStack() as ctx:
        sb = lambda n, s, d=F32: ctx.enter_context(nc.sbuf_tensor(n, s, d))
        sem = lambda n: ctx.enter_context(nc.semaphore(n))
        xs = sb("xs", [128, 2, CH, D])
        xsT = sb("xsT", [128, 2, W])
        w1e = sb("w1e", [128, 2, CH, HID])
        w2e = sb("w2e", [HID, 2, CH, D])
        hidT = sb("hidT", [HID, 2, CH, 128])
        ys = sb("ys", [128, 2, CH, D])

        loaded = [sem(f"slots_loaded{r}") for r in range(2)]
        stored = [sem(f"slots_stored{r}") for r in range(2)]
        turned = sem("slots_turned")
        padded = sem("padded")
        xsT_copied = sem("xsT_copied")
        w1_copied = sem("w1_copied")
        w2_copied = sem("w2_copied")
        h_ready = sem("h_ready")
        relued = sem("relued")
        y_ready = sem("y_ready")
        y_copied = sem("y_copied")

        rows_in = A["slot_x"].rearrange("(g k p) d -> g p k d", k=CH, p=128)
        rows_out = A["slot_y"].rearrange("(g k p) d -> g p k d", k=CH, p=128)
        owners = lambda eng, g, n: nc.values_load_multi_w_load_instructions(
            S.owner_row[0:1, bass.ds(g * CH, n)], engines=(eng.engine,), min_val=0, max_val=E0 - 1)[1]
        block = ctx.enter_context(nc.Block())

        @block.sync
        def _(sp):
            for r in range(2):
                sp.dma_start(xs[:, r, :, :], rows_in[r]).then_inc(loaded[r], 16)
            with sp.Fori(0, NG // 2 - 1) as i:
                for r in range(2):
                    hold(S, sp, turned, i * 2 + r + 1)
                    sp.dma_start(xs[:, r, :, :], rows_in[bass.ds(i * 2 + r + 2, 1)].rearrange("g p k d -> (g p) k d")
                                 ).then_inc(loaded[r], 16)

        @block.tensor
        def _(pe):
            M = nc.tensor.matmul

            def turn_rows(i):
                for r in range(2):
                    hold(S, pe, loaded[r], i * 16 + 16)
                    for k in range(CH):
                        last = nc.tensor.transpose(S.ps[r][0:D, T * k:T * k + T], xs[:, r, k, :], S.ident[:, :])
                    last.then_inc(turned, 1)

            def turn(i, more):
                for r in range(2):
                    hold(S, pe, xsT_copied, i * 2 + r + 1)
                    for k in range(CH):
                        if k == 0:
                            hold(S, pe, w1_copied, (i * 2 + r) * CH + CH)
                        last = M(S.ps[2 + r][:, T * k:T * k + T], w1e[:, r, k, :], xsT[:, r, T * k:T * k + T],
                                 start=True, stop=True)
                    last.then_inc(h_ready, 1)
                if more:
                    turn_rows(i + 1)
                for r in range(2):
                    hold(S, pe, relued, i * 2 + r + 1)
                    hold(S, pe, w2_copied, (i * 2 + r) * CH + CH)
                    hold(S, pe, y_copied, i * 2 + r + 1)
                    for k in range(CH):
                        last = M(S.ps[4 + r][:, D * k:D * k + D], hidT[:, r, k, :], w2e[:, r, k, :], start=True, stop=True)
                    last.then_inc(y_ready, 1)

            pe.wait_ge(padded, 3)
            turn_rows(0)
            with pe.Fori(0, NG // 2 - 1) as i:
                turn(i, True)
            turn(NG // 2 - 1, False)

        @block.scalar
        def _(act):
            N = nc.scalar.activation

            def copy_rows(i):
                for r in range(2):
                    hold(S, act, turned, i * 2 + r + 1)
                    N(xsT[0:D, r, :], S.ps[r][0:D, :], ACT.Copy).then_inc(xsT_copied, 1)

            def turn(i, more):
                if more:
                    copy_rows(i + 1)
                for r in range(2):
                    hold(S, act, y_ready, i * 2 + r + 1)
                    hold(S, act, stored[r], i * 16 + 16)
                    N(ys[:, r, :, :], S.ps[4 + r][:, 0:CH * D].rearrange("p (k d) -> p k d", d=D), ACT.Copy).then_inc(y_copied, 1)
                    hold(S, act, y_copied, i * 2 + r + 3)
                    act.dma_start(rows_out[bass.ds(i * 2 + r, 1)].rearrange("g p k d -> (g p) k d"), ys[:, r, :, :]
                                  ).then_inc(stored[r], 16)

            act.sem_inc(y_copied, 2)
            for r in range(2):
                act.sem_inc(stored[r], 16)
            copy_rows(0)
            with act.Fori(0, NG // 2 - 1) as i:
                turn(i, True)
            turn(NG // 2 - 1, False)
            for r in range(2):
                act.wait_ge(stored[r], 16 * (NG // 2) + 16)

        @block.vector
        def _(dve):
            V = nc.vector

            def copy_w2(experts, r):
                for k in range(CH):
                    V.tensor_copy(w2e[:, r, k, :], S.w2_0[:, bass.ds(experts[r * CH + k], 1), :].rearrange("p a d -> p (a d)")
                                  ).then_inc(w2_copied, 1)

            def turn(i, more):
                for r in range(2):
                    hold(S, dve, h_ready, i * 2 + r + 1)
                    V.tensor_scalar(hidT[:, r, :, :].rearrange("p k t -> p (k t)"), S.ps[2 + r][:, :], 0.0, None,
                                    ALU.max).then_inc(relued, 1)
                if more:
                    experts = owners(dve, i * 2 + 2, 2 * CH)
                    for r in range(2):
                        hold(S, dve, y_ready, i * 2 + r + 1)
                        copy_w2(experts, r)

            V.memset(w1e[D:128, :, :, :], 0.0).then_inc(padded, 1)
            V.memset(xsT[D:128, :, :], 0.0).then_inc(padded, 1)
            dve.wait_ge(padded, 2)
            V.memset(xsT[D:D + 1, :, :], 1.0).then_inc(padded, 1)
            dve.wait_ge(S.experts_in, 64)
            experts = owners(dve, 0, 2 * CH)
            for r in range(2):
                copy_w2(experts, r)
            with dve.Fori(0, NG // 2 - 1) as i:
                turn(i, True)
            turn(NG // 2 - 1, False)

        @block.gpsimd
        def _(pool):
            def copy_w1(experts, r):
                for k in range(CH):
                    nc.gpsimd.tensor_copy(w1e[0:D + 1, r, k, :], S.w1_0[:, bass.ds(experts[r * CH + k], 1), :].rearrange("p a h -> p (a h)")
                                          ).then_inc(w1_copied, 1)

            pool.wait_ge(padded, 3)
            pool.wait_ge(S.experts_in, 64)
            experts = owners(pool, 0, 2 * CH)
            for r in range(2):
                copy_w1(experts, r)
            with pool.Fori(0, NG // 2 - 1) as i:
                experts = owners(pool, i * 2 + 2, 2 * CH)
                for r in range(2):
                    hold(S, pool, h_ready, i * 2 + r + 1)
                    copy_w1(experts, r)


def grouped_stage(nc, S, A):
    NU = 2
    UH = NU * NPAR
    with ExitStack() as ctx:
        sb = lambda n, s, d=F32: ctx.enter_context(nc.sbuf_tensor(n, s, d))
        sem = lambda n: ctx.enter_context(nc.semaphore(n))
        yg = sb("yg", [128, 2, B, D])
        stats = sb("stats3", [128, CH, 6])
        mv = sb("mv3", [128, CH, 2])
        dev = sb("dev3", [128, CH])
        power = sb("power", [128, CH])
        stats_f = sb("stats4", [128, CH, 6])
        mv_f = sb("mv4", [128, CH, 2])
        xd = sb("xd", [128, 2, CH, 2, D])
        xv = sb("xv", [128, 2, CH, D])
        x3T = sb("x3T", [128, 2, 2, W])
        yk = sb("yk", [128, 2, NPAR, W])
        mx = sb("mx", [128, 2, 2, UH])
        ex = sb("ex", [128, 2, 2, UH, GC])
        sums = sb("sums", [128, 2, 2, UH])
        pT = sb("pT", [128, 2, 2, UH, GC])
        rs = sb("rs", [128, 2, UH, T])
        oT = sb("oT", [128, 2, T])

        zeroed = sem("x3T_zeroed")
        gathered = sem("gathered_y")
        ready = sem("chunk_gathered")
        rooted = sem("x3_rooted")
        doubled = sem("x3_doubled")
        kept = sem("x3_kept")
        turned = sem("x3_turned")
        x3T_copied = sem("x3T_copied")
        y_ready = sem("yk_ready")
        y_copied = sem("yk_copied")
        scored = sem("group_scored")
        shifted = sem("shifted")
        exped = sem("group_exped")
        weighed = sem("weighed")
        mixed = sem("mixed")
        rs_copied = sem("rs_copied")
        projected = sem("group_projected")
        o_copied = sem("oT_copied")
        final = sem("group_final")
        first_banks = [0, 4, 5, 6, 7]
        soft = Steps(S, sem("soften_steps"), 1)
        weigh_st = Steps(S, sem("weigh_steps"), 3)
        prep_st = Steps(S, sem("add_steps"), 13)
        x_st = Steps(S, sem("prepare_steps"), 2)
        fin_st = Steps(S, sem("finish_steps"), 11)

        block = ctx.enter_context(nc.Block())

        @block.vector
        def _(dve):
            V = nc.vector
            s = S.bank[:, 2:4, 0:UH * GC].rearrange("p a (u k) -> p a u k", k=GC)

            def soften(n, p):
                soft.start(dve, n)
                hold(S, dve, scored, n + 1)
                soft.do(V.reduce_max(mx[:, p, :, :], s, AX.X))
                V.tensor_tensor(ex[:, p, :, :, :], s, bc(mx[:, p, :, :].unsqueeze(3), [128, 2, UH, GC]),
                                ALU.subtract).then_inc(shifted, 1)
                soft.end()

            def weigh(n, p):
                weigh_st.start(dve, n)
                do = weigh_st.do
                hold(S, dve, exped, n + 1)
                do(V.reduce_sum(sums[:, p, :, :], ex[:, p, :, :, :], AX.X))
                do(V.reciprocal(sums[:, p, :, :], sums[:, p, :, :]))
                do(V.tensor_tensor(ex[:, p, :, :, :], ex[:, p, :, :, :],
                                   bc(sums[:, p, :, :].unsqueeze(3), [128, 2, UH, GC]), ALU.mult))
                V.transpose(pT[:, p, :, :, :].rearrange("p a u k -> p (a u k)"),
                            ex[:, p, :, :, :].rearrange("p a u k -> p (a u k)")).then_inc(weighed, 1)
                weigh_st.end()

            def add_experts(c):
                st = prep_st
                st.start(dve, c)
                tiles = bass.ds(c * CH, CH)
                hold(S, dve, ready, c + 1)
                for j in range(2):
                    st.done(V.tensor_tensor(yg[:, j, tiles, :], yg[:, j, tiles, :],
                                            bc(S.gates[:, j, tiles].unsqueeze(2), [128, CH, D]), ALU.mult))
                st.wait()
                for j in range(2):
                    st.do(V.tensor_tensor(S.h[:, tiles, :], S.h[:, tiles, :], yg[:, j, tiles, :], ALU.add))
                for k in range(CH):
                    st.done(V.bn_stats(stats[:, k, :], S.h[:, bass.ds(c * CH + k, 1), :].rearrange("p a d -> p (a d)")))
                st.wait()
                for k in range(CH):
                    st.done(V.bn_aggr(mv[:, k, :], stats[:, k, :]))
                st.wait()
                st.do(V.tensor_scalar(dev[:, :], mv[:, :, 1], EPS, None, ALU.add))
                st.mark("variance")
                st.end()

            def prepare(c, r, reused):
                st = x_st
                st.start(dve, c)
                tiles = bass.ds(c * CH, CH)
                hold(S, dve, rooted, c + 1)
                if reused:
                    hold(S, dve, turned, c - 1)
                    hold(S, dve, kept, c - 1)
                st.do(V.tensor_tensor(xd[:, r, :, 0, :], S.h[:, tiles, :], bc(mv[:, :, 0].unsqueeze(2), [128, CH, D]),
                                      ALU.subtract))
                st.do(V.tensor_tensor(xd[:, r, :, 0, :], xd[:, r, :, 0, :], bc(dev[:, :].unsqueeze(2), [128, CH, D]),
                                      ALU.mult))
                st.mark("x")
                st.end()

            def finish(c):
                st = fin_st
                st.start(dve, c)
                tiles = bass.ds(c * CH, CH)
                hold(S, dve, final, c + 1)
                st.do(V.tensor_tensor(S.h[:, tiles, :], S.h[:, tiles, :],
                                      S.ps[0][:, 0:CH * D].rearrange("p (k d) -> p k d", d=D), ALU.add))
                st.mark("added")
                measure_h(nc, S, st, c, stats_f, mv_f)
                st.end()

            def chunk(c, r, before, after):
                soften(c * 2 + 1, 1)
                weigh(c * 2 + 1, 1)
                if has_second(c):
                    add_experts(c + 2)
                if after:
                    soften(c * 2 + 2, 0)
                if has_second(c):
                    prepare(c + 2, r, True)
                if after:
                    weigh(c * 2 + 2, 0)
                if before:
                    finish(c - 1)

            V.memset(x3T[D:128, 0, :, :], 0.0).then_inc(zeroed, 1)
            V.memset(x3T[0:D, 1, :, :], 0.0).then_inc(zeroed, 1)
            V.memset(power[:, :], -0.5).then_inc(zeroed, 1)
            add_experts(0)
            prepare(0, 0, False)
            soften(0, 0)
            weigh(0, 0)
            add_experts(1)
            prepare(1, 1, False)
            all_chunks(dve, chunk)
            finish(NCH - 1)

        @block.gpsimd
        def _(pool):
            def gather(c):
                for b in range(c * CH, (c + 1) * CH):
                    for j in range(2):
                        nc.gpsimd.indirect_dma_start(yg[:, j, b, :], None, A["slot_y"],
                                                     bass.IndirectOffsetOnAxis(ap=S.slot_u[:, j, b:b + 1], axis=0)
                                                     ).then_inc(gathered, 16)
                pool.wait_ge(gathered, 16 * 2 * CH * (c + 1))
                pool.sem_inc(ready, 1)

            def root(c):
                prep_st.after(pool, "variance", c)
                nc.gpsimd.tensor_tensor(dev[:, :], dev[:, :], power[:, :], ALU.pow).then_inc(rooted, 1)

            gather(0)
            pool.wait_ge(zeroed, 3)
            root(0)
            gather(1)
            root(1)
            gather(2)
            for c in range(2, NCH):
                if c + 1 < NCH:
                    gather(c + 1)
                root(c)

        @block.tensor
        def _(pe):
            M = nc.tensor.matmul
            keys_copied = lambda c, n: hold(S, pe, y_copied, c * NPAR + n)

            def turn_x(c, r, finished):
                hold(S, pe, doubled, c + 1)
                if finished:
                    fin_st.after(pe, "added", c - 3)
                for k in range(CH):
                    last = nc.tensor.transpose(S.ps[0][:, T * k:T * k + T], xd[:, r, k, :, :].rearrange("p a d -> p (a d)"),
                                               S.ident[:, :])
                last.then_inc(turned, 1)

            def keys(c, r, k, bank=0):
                if k == 0:
                    hold(S, pe, x3T_copied, c * 2 + 2)
                elif bank == 0:
                    keys_copied(c, k)
                M(S.ps[bank][:, :], S.qkT[:, k, :, :].rearrange("p a d -> p (a d)"), x3T[:, 0, r, :],
                  start=True, stop=True).then_inc(y_ready, 1)

            def score(n, r, p, first=False):
                if not first:
                    hold(S, pe, shifted, n)
                for a in range(2):
                    for u in range(NU):
                        at = T * (NU * p + u)
                        for g in range(GG):
                            v = (g + 1) % GG
                            last = M(S.ps[2 + a][GC * v:GC * v + GC, NPAR * GC * u:NPAR * GC * (u + 1)].rearrange(
                                        "p (h k) -> p h k", k=GC),
                                     x3T[:, a, r, at + GC * g:at + GC * g + GC],
                                     yk[:, r, :, at + GC * v:at + GC * v + GC], start=True, stop=True)
                last.then_inc(scored, 1)

            def mix(n, c, r, p, part, parts, before):
                if part == 0:
                    hold(S, pe, weighed, n + 1)
                    hold(S, pe, kept, c + 1)
                    if before:
                        hold(S, pe, rs_copied, n)
                products = [(u, g, a) for u in range(NU) for g in range(GG) for a in range(2)]
                for u, g, a in products[len(products) * part // parts:len(products) * (part + 1) // parts]:
                    v = (g + 1) % GG
                    last = M(S.ps[4 + g][64 * a:64 * a + 64, NPAR * GC * u:NPAR * GC * (u + 1)],
                             xv[GC * v:GC * v + GC, r, NU * p + u, :],
                             pT[GC * v:GC * v + GC, p, a, NPAR * u:NPAR * (u + 1), :].rearrange("p h q -> p (h q)"),
                             start=True, stop=True)
                if part == parts - 1:
                    last.then_inc(mixed, 1)

            def project(n, p, reused):
                hold(S, pe, rs_copied, n + 1)
                if reused:
                    hold(S, pe, o_copied, n)
                for k in range(NPAR):
                    for u in range(NU):
                        last = M(S.ps[1][64 * u:64 * u + 64, T * p:T * p + T], S.wv[:, k, :], rs[:, p, NPAR * u + k, :],
                                 start=(k == 0), stop=(k == NPAR - 1))
                last.then_inc(projected, 1)

            def turn_out(c, after):
                hold(S, pe, o_copied, c * 2 + 2)
                if after:
                    keys_copied(c + 2, NPAR)
                else:
                    fin_st.after(pe, "added", c - 1)
                for p in range(2):
                    last = nc.tensor.transpose(S.ps[0][:, T * p:T * p + T], oT[:, p, :], S.ident[:, :])
                last.then_inc(final, 1)

            def chunk(c, r, before, after):
                n = c * 2
                score(n + 1, r, 1)
                if after:
                    turn_x(c + 1, 1 - r, before == 2)
                if before:
                    project(n - 1, 1, True)
                for k in range(NPAR):
                    if after:
                        keys(c + 1, 1 - r, k)
                    mix(n, c, r, 0, k, NPAR, before)
                if after:
                    keys_copied(c + 1, NPAR)
                    score(n + 2, 1 - r, 0)
                if before:
                    turn_out(c - 1, after)
                project(n, 0, before)
                mix(n + 1, c, r, 1, 0, 1, True)

            pe.wait_ge(zeroed, 2)
            turn_x(0, 0, False)
            for k in range(NPAR):
                keys(0, 0, k, first_banks[k])
            keys_copied(0, NPAR)
            score(0, 0, 0, True)
            all_chunks(pe, chunk)
            project(2 * NCH - 1, 1, True)
            turn_out(NCH - 1, False)

        @block.scalar
        def _(act):
            N = nc.scalar.activation

            def double(c, r):
                x_st.after(act, "x", c)
                N(xd[:, r, :, 1, :], xd[:, r, :, 0, :], ACT.Copy).then_inc(doubled, 1)

            def keep(c, r, before):
                if before:
                    hold(S, act, mixed, c * 2 - 2)
                N(xv[:, r, :, :], xd[:, r, :, 0, :], ACT.Copy).then_inc(kept, 1)

            def copy_x(c, r):
                hold(S, act, turned, c + 1)
                for a in range(2):
                    half = slice(64 * a, 64 * a + 64)
                    N(x3T[half, a, r, :], S.ps[0][half, :], ACT.Copy).then_inc(x3T_copied, 1)

            def copy_keys(c, r, banks=NPAR * [0]):
                for k in range(NPAR):
                    hold(S, act, y_ready, c * NPAR + k + 1)
                    N(yk[:, r, k, :], S.ps[banks[k]][:, :], ACT.Copy).then_inc(y_copied, 1)

            def exponential(n, p):
                hold(S, act, shifted, n + 1)
                e = ex[:, p, :, :, :].rearrange("p a u k -> p (a u k)")
                N(e, e, ACT.Exp).then_inc(exped, 1)

            def copy_mixed(n, p):
                hold(S, act, mixed, n + 1)
                N(rs[:, p, :, :].rearrange("p u (g q) -> p g u q", q=GC),
                  S.bank[:, 4:8, 0:UH * GC].rearrange("p g (u q) -> p g u q", q=GC), ACT.Copy).then_inc(rs_copied, 1)

            def copy_out(n, p):
                hold(S, act, projected, n + 1)
                N(oT[:, p, :], S.ps[1][:, T * p:T * p + T], ACT.Copy).then_inc(o_copied, 1)

            def chunk(c, r, before, after):
                n = c * 2
                if after:
                    copy_x(c + 1, 1 - r)
                exponential(n + 1, 1)
                if before:
                    copy_out(n - 1, 1)
                if after:
                    copy_keys(c + 1, 1 - r)
                    keep(c + 1, 1 - r, before)
                copy_mixed(n, 0)
                if after:
                    exponential(n + 2, 0)
                copy_out(n, 0)
                copy_mixed(n + 1, 1)
                if has_second(c):
                    double(c + 2, r)

            act.wait_ge(zeroed, 2)
            double(0, 0)
            keep(0, 0, False)
            copy_x(0, 0)
            copy_keys(0, 0, first_banks)
            exponential(0, 0)
            double(1, 1)
            all_chunks(act, chunk)
            copy_out(2 * NCH - 1, 1)


def second_experts_stage(nc, S, A, out):
    with ExitStack() as ctx:
        sb = lambda n, s, d=F32: ctx.enter_context(nc.sbuf_tensor(n, s, d))
        sem = lambda n: ctx.enter_context(nc.semaphore(n))
        r2 = sb("r2", [128, B])
        xr = sb("x4", [128, 2, CH, D])
        xT = sb("x4T", [128, 2, W])
        logits = sb("logits1", [128, CH, E1])
        top = sb("top1", [128, CH, 8])
        top_i = sb("top_i1", [128, CH, 8], U32)
        top_f = sb("top_f1", [128, CH, 2])
        gates = sb("gates1", [128, 2, CH])
        hot = sb("hot1", [128, 2, CH, E1])
        share = sb("share", [128, 2, CH, E1])
        shareT = sb("shareT", [E1, W])
        hid = sb("hid1", [HID, 4, W])
        acc = sb("acc", [128, 2, CH, D])

        zeroed = sem("x4T_zeroed")
        scaled = sem("r2_rooted")
        turned = sem("x4_turned")
        x_copied = sem("x4T_copied")
        scored = sem("router1_scored")
        tanhed = sem("gates1_tanhed")
        share_turned = sem("share_turned")
        shareT_copied = sem("shareT_copied")
        b2_ready = sem("b2_ready1")
        hidden = sem("hidden1")
        gelued = sem("gelued1")
        y_ready = sem("y1_ready")
        sent = [sem(f"sent{r}") for r in range(2)]
        pre = Steps(S, sem("r2_steps"))
        x_st = Steps(S, sem("x4_steps"), 2)
        top_st = Steps(S, sem("router1_steps"), 13)
        share_st = Steps(S, sem("share_steps"), 5)
        add_st = Steps(S, sem("expert1_steps"), 1 + E1 * CH)

        block = ctx.enter_context(nc.Block())

        @block.vector
        def _(dve):
            V = nc.vector

            def normed(c, r, reused):
                x_st.start(dve, c)
                tiles = bass.ds(c * CH, CH)
                if reused:
                    hold(S, dve, turned, c - 1)
                x_st.do(V.tensor_tensor(xr[:, r, :, :], S.h[:, tiles, :], bc(S.mean[:, tiles].unsqueeze(2), [128, CH, D]),
                                        ALU.subtract))
                x_st.do(V.tensor_tensor(xr[:, r, :, :], xr[:, r, :, :], bc(r2[:, tiles].unsqueeze(2), [128, CH, D]), ALU.mult))
                x_st.mark("x")
                x_st.end()

            def choose(c):
                st = top_st
                st.start(dve, c)
                hold(S, dve, scored, c + 1)
                st.do(V.tensor_tensor(logits[:, :, :], S.ps[3][:, 0:CH * E1].rearrange("p (k e) -> p k e", e=E1),
                                      bc(S.br1[:, :].unsqueeze(1), [128, CH, E1]), ALU.add))
                for k in range(CH):
                    st.done(V.max(top[:, k, :], logits[:, k, :]))
                st.wait()
                for k in range(CH):
                    st.done(V.max_index(top_i[:, k, :], top[:, k, :], logits[:, k, :]))
                st.done(V.tensor_tensor(gates[:, 1, :], top[:, :, 1], top[:, :, 0], ALU.subtract))
                st.mark("difference")
                st.wait()
                st.do(V.tensor_copy(top_f[:, :, :], top_i[:, :, 0:2]))
                for j in range(2):
                    st.done(V.tensor_tensor(hot[:, j, :, :], bc(S.iota_free[:, 0:E1].unsqueeze(1), [128, CH, E1]),
                                            bc(top_f[:, :, j:j + 1], [128, CH, E1]), ALU.is_equal))
                st.wait()
                st.end()

            def weigh(c, r, reused):
                st = share_st
                st.start(dve, c)
                hold(S, dve, tanhed, c + 1)
                if reused:
                    hold(S, dve, share_turned, c - 1)
                st.done(V.tensor_scalar(gates[:, 0, :], gates[:, 1, :], -0.5, 0.5, ALU.mult, ALU.add))
                st.do(V.tensor_scalar(gates[:, 1, :], gates[:, 1, :], 0.5, 0.5, ALU.mult, ALU.add))
                for j in range(2):
                    st.done(V.tensor_tensor(hot[:, j, :, :], hot[:, j, :, :], bc(gates[:, j, :].unsqueeze(2), [128, CH, E1]),
                                            ALU.mult))
                st.wait()
                st.do(V.tensor_tensor(share[:, r, :, :], hot[:, 0, :, :], hot[:, 1, :, :], ALU.add))
                st.mark("share")
                st.end()

            def add(c, r, e):
                hold(S, dve, y_ready, c * E1 + e + 1)
                add_st.wait()
                for k in range(CH):
                    add_st.done(V.scalar_tensor_tensor(acc[:, r, k, :], S.ps[4 + e % 4][:, D * k:D * k + D],
                                                       share[:, r, k, e:e + 1], acc[:, r, k, :], ALU.mult, ALU.add))
                add_st.mark(("added", e))

            def chunk(c, r, before, after):
                add_st.start(dve, c)
                hold(S, dve, b2_ready, c + 1)
                if before == 2:
                    hold(S, dve, sent[r], (c - r) * 8)
                tiles = bass.ds(c * CH, CH)
                add_st.done(V.tensor_tensor(acc[:, r, :, :], S.h[:, tiles, :],
                                            S.ps[3][:, 128:128 + CH * D].rearrange("p (k d) -> p k d", d=D), ALU.add))
                add_st.mark("started")
                for e in range(E1):
                    add(c, r, e)
                    if after and e == 1:
                        choose(c + 1)
                    if after and e == 3:
                        weigh(c + 1, 1 - r, before)
                    if has_second(c) and e == 5:
                        normed(c + 2, r, True)
                add_st.end()

            pre.start(dve)
            pre.do(V.tensor_scalar(r2[:, :], S.var[:, :], 1.0 + EPS, EPS * EPS, ALU.mult, ALU.add))
            pre.mark("variance")
            dve.wait_ge(scaled, 1)
            pre.do(V.reciprocal(r2[:, :], r2[:, :]))
            for c in range(2):
                normed(c, c, False)
            choose(0)
            weigh(0, 0, False)
            all_chunks(dve, chunk)

        @block.gpsimd
        def _(pool):
            nc.gpsimd.memset(xT[D:128, :, :], 0.0).then_inc(zeroed, 1)

        @block.tensor
        def _(pe):
            M = nc.tensor.matmul

            def turn_x(c, r):
                x_st.after(pe, "x", c)
                for k in range(CH):
                    last = nc.tensor.transpose(S.ps[2][0:D, T * k:T * k + T], xr[:, r, k, :], S.ident[:, :])
                last.then_inc(turned, 1)

            def router(c, r, started):
                hold(S, pe, x_copied, c + 1)
                if started:
                    add_st.after(pe, "started", c - 1)
                for k in range(CH):
                    last = M(S.ps[3][:, E1 * k:E1 * k + E1], xT[0:D, r, T * k:T * k + T], S.wr1[:, :], start=True, stop=True)
                last.then_inc(scored, 1)

            def turn_share(c, r):
                share_st.after(pe, "share", c)
                for k in range(CH):
                    last = nc.tensor.transpose(S.ps[2][0:E1, T * k:T * k + T], share[:, r, k, :], S.ident[:, :])
                last.then_inc(share_turned, 1)

            def biases(c):
                hold(S, pe, shareT_copied, c + 1)
                for k in range(CH):
                    last = M(S.ps[3][:, 128 + D * k:128 + D * k + D], shareT[:, T * k:T * k + T], S.b2_1[:, :], start=True, stop=True)
                last.then_inc(b2_ready, 1)

            def up(c, r, e, reused):
                if reused:
                    hold(S, pe, gelued, c * E1 + e - 1)
                M(S.ps[e % 2][:, :], S.w1_1[:, e, :], xT[:, r, :], start=True, stop=True).then_inc(hidden, 1)

            def down(c, r, e, before):
                hold(S, pe, gelued, c * E1 + e + 1)
                if e >= 4:
                    add_st.after(pe, ("added", e - 4), c)
                elif before:
                    add_st.after(pe, ("added", e + 4), c - 1)
                for k in range(CH):
                    last = M(S.ps[4 + e % 4][:, D * k:D * k + D], hid[:, e % 4, T * k:T * k + T], S.w2_1[:, e, :],
                             start=True, stop=True)
                last.then_inc(y_ready, 1)

            def chunk(c, r, before, after):
                for e in range(2):
                    up(c, r, e, before)
                if before and after:
                    turn_x(c + 1, 1 - r)
                for e in range(E1):
                    if e + 2 < E1:
                        up(c, r, e + 2, True)
                    down(c, r, e, before)
                    if not before and e == 1:
                        turn_share(c, r)
                        biases(c)
                        turn_x(c + 1, 1 - r)
                    if after and e == (1 if before else 3):
                        router(c + 1, 1 - r, True)
                    if after and e == 5:
                        turn_share(c + 1, 1 - r)
                if after:
                    biases(c + 1)

            pe.wait_ge(zeroed, 1)
            turn_x(0, 0)
            router(0, 0, False)
            all_chunks(pe, chunk)

        @block.scalar
        def _(act):
            N = nc.scalar.activation

            def copy_x(c, r):
                hold(S, act, turned, c + 1)
                N(xT[0:D, r, :], S.ps[2][0:D, :], ACT.Identity, scale=S.gamma[:, 0:1], bias=S.beta[:, 0:1]).then_inc(x_copied, 1)

            def gate(c):
                top_st.after(act, "difference", c)
                N(gates[:, 1, :], gates[:, 1, :], ACT.Tanh, scale=0.5).then_inc(tanhed, 1)

            def copy_share(c):
                hold(S, act, share_turned, c + 1)
                N(shareT[:, :], S.ps[2][0:E1, :], ACT.Copy).then_inc(shareT_copied, 1)

            def chunk(c, r, before, after):
                for e in range(E1):
                    hold(S, act, hidden, c * E1 + e + 1)
                    if before or e >= 4:
                        hold(S, act, y_ready, c * E1 + e - 3)
                    N(hid[:, e % 4, :], S.ps[e % 2][:, :], ACT.Gelu, bias=S.b1_1[:, e:e + 1]).then_inc(gelued, 1)
                    if not before and e == 1:
                        gate(c)
                        copy_share(c)
                    if after and e == (1 if before else 2):
                        copy_x(c + 1, 1 - r)
                    if after and e == 5:
                        gate(c + 1)
                if after:
                    copy_share(c + 1)

            pre.after(act, "variance")
            N(r2[:, :], r2[:, :], ACT.Sqrt).then_inc(scaled, 1)
            copy_x(0, 0)
            all_chunks(act, chunk)

        @block.sync
        def _(sp):
            rows = out.rearrange("(c k) p d -> c p k d", k=CH)
            with sp.Fori(0, NCH // 2) as i:
                for r in range(2):
                    add_st.after(sp, ("added", E1 - 1), i * 2 + r)
                    sp.dma_start(rows[bass.ds(i * 2 + r, 1)].rearrange("c p k d -> (c p) k d"), acc[:, r, :, :]).then_inc(sent[r], 16)
            for r in range(2):
                sp.wait_ge(sent[r], 16 * (NCH // 2))


def build(nc, A, out):
    A["idx_scratch"] = nc.dram_tensor("idx_scratch", [B, T], BF16).ap()
    S = Store()
    S.slots = 2 * B * T + E0 * 128
    A["slot_y"] = nc.dram_tensor("slot_y", [S.slots, D], F32).ap()
    A["slot_x"] = nc.dram_tensor("slot_x", [S.slots, D], F32).ap()
    with ExitStack() as ctx:
        sb = lambda n, s, d=F32: ctx.enter_context(nc.sbuf_tensor(n, s, d))
        S.bank = ctx.enter_context(nc.psum_tensor("banks", [128, 8, 512], F32))
        S.ps = [S.bank[:, k, :] for k in range(8)]
        S.ident = sb("ident", [128, 128])
        S.triC = sb("triC", [128, 128])
        S.triS = sb("triS", [128, 128], BF16)
        S.cmean = sb("cmean", [128, 128])
        S.iota_free = sb("iota_free", [128, 128])
        S.iota_part = sb("iota_part", [128, 1])
        S.ones_bf = sb("ones_bf", [128, 128], BF16)
        S.eps = sb("eps", [128, 1])
        S.half_pi = sb("half_pi", [128, 1])
        S.xT = sb("xT", [T, B], I32)
        S.maskT = sb("maskT", [T, B])
        S.w1c = sb("w1c", [128, 128])
        S.w1p = sb("w1p", [128, 128])
        S.b1c = sb("b1c", [128, 1])
        S.w2c = sb("w2c", [128, GT])
        S.sg_w1 = sb("sg_w1", [128, D // 2])
        S.sg_b1 = sb("sg_b1", [D // 2, 1])
        S.sg_w2 = sb("sg_w2", [D // 2, 1])
        S.wx = sb("wx", [128, P + 2 * D])
        S.proj_b = sb("proj_b", [128, NPROJ])
        S.pcs = sb("pcs", [T, 2, P])
        S.pcsT = sb("pcsT", [128, T])
        S.ppT = sb("ppT", [128, T])
        S.dcs = sb("dcs", [T, 2, NW])
        S.nhd2 = sb("nhd2", [T, NW])
        S.out_w2 = sb("out_w2", [128, D])
        S.out_row = sb("out_row", [128, D])
        S.wr0 = sb("wr0", [D, E0])
        S.br0 = sb("br0", [128, E0])
        S.qkT = sb("qkT", [128, NPAR, 2, D])
        S.wv = sb("wv", [128, NPAR, D])
        S.gamma = sb("gamma", [D, 1])
        S.beta = sb("beta", [D, 1])
        S.wr1 = sb("wr1", [D, E1])
        S.br1 = sb("br1", [128, E1])
        S.w1_1 = sb("w1_1", [128, E1, HID])
        S.w2_1 = sb("w2_1", [HID, E1, D])
        S.b1_1 = sb("b1_1", [HID, E1])
        S.b2_1 = sb("b2_1", [E1, D])
        S.h = sb("h", [128, B, D])
        S.mean = sb("mean", [128, B])
        S.var = sb("var", [128, B])
        S.rstd = sb("rstd", [128, B])
        S.waits = {e.engine: ctx.enter_context(nc.semaphore(f"waits_{n}")) for n, e in enumerate(
            (nc.tensor, nc.vector, nc.scalar, nc.gpsimd, nc.sync))}
        with ExitStack() as tok:
            tb = lambda n, s, d=F32: tok.enter_context(nc.sbuf_tensor(n, s, d))
            S.b_oah = tb("b_oah", [128, D])
            S.zeros = tb("zeros", [128, 32 * D])
            S.x_bc = tb("x_bc", [128, B * T], I32)
            S.idx_bc = tb("idx_bc", [128, B * T], BF16)
            S.triG = tb("triG", [128, 128])
            S.emb = tb("emb", [T, D])
            S.emb3 = tb("emb3", [T, 3, D], BF16)
            S.emb_last3 = tb("emb_last3", [3, D], BF16)
            S.w_inT = tb("w_inT", [D, D])
            S.hn = tb("hn", [128, 2, CH, D + 1])
            setup_stage(nc, S, A)
            L, pairs = weights_to_load(S, A, tb)
            token_stage(nc, S, A["slot_x"], pairs)
            product_stage(nc, S, L)
        with ExitStack() as mem:
            mb = lambda n, s, d=F32: mem.enter_context(nc.sbuf_tensor(n, s, d))
            S.proj = mb("proj", [128, B, NPROJ])
            project_stage(nc, S, A)
            S.q_pos = mb("q_pos", [128, B, 2 * P])
            S.q_kv = mb("q_kv", [128, B, 2 * P])
            S.k_kv = mb("k_kv", [128, B, 2 * P])
            S.gv = mb("gv", [128, B, D])
            phase_stage(nc, S, A)
            memory_stage(nc, S, A)
        with ExitStack() as moe:
            eb = lambda n, s, d=F32: moe.enter_context(nc.sbuf_tensor(n, s, d))
            S.gates = eb("gates", [128, 2, B])
            S.slot_u = eb("slot_u", [128, 2, B], U32)
            with ExitStack() as experts:
                wb = lambda n, s, d=F32: experts.enter_context(nc.sbuf_tensor(n, s, d))
                S.xn = wb("xn", [128, B, D])
                S.w1_0 = wb("w1_0", [D + 1, E0, HID])
                S.w2_0 = wb("w2_0", [HID, E0, D])
                S.b2_0 = wb("b2_0", [E0, D])
                S.experts_in = experts.enter_context(nc.semaphore("experts_in"))
                S.owner_row = wb("owner_row", [1, 128], I32)
                route_stage(nc, S, A)
                experts_stage(nc, S, A)
            grouped_stage(nc, S, A)
        second_experts_stage(nc, S, A, out)


INPUTS = {
    "x": "x", "L0_tok_emb_table": "emb", "L0_tok_W_in": "w_in", "L0_tok_b_oah": "b_oah",
    "L0_attn_pos_phases": "phases", "L0_attn_window_deltas": "deltas", "L0_attn_mc_w": "mc_w", "L0_attn_mc_b": "mc_b",
    "L0_attn_hop_w1": "hop_w1", "L0_attn_hop_b1": "hop_b1", "L0_attn_hop_w2": "hop_w2", "L0_attn_hop_b2": "hop_b2",
    "L0_attn_cpe_w": "cpe_w", "L0_attn_cpe_b": "cpe_b", "L0_attn_ve_w": "ve_w", "L0_attn_ve_b": "ve_b",
    "L0_attn_kce_w": "kce_w", "L0_attn_kce_b": "kce_b", "L0_attn_ksk_w1": "ksk_w1", "L0_attn_ksk_b1": "ksk_b1",
    "L0_attn_ksk_w2": "ksk_w2", "L0_attn_ksk_b2": "ksk_b2", "L0_attn_sg_w1": "sg_w1", "L0_attn_sg_b1": "sg_b1",
    "L0_attn_sg_w2": "sg_w2", "L0_attn_sg_b2": "sg_b2", "L0_attn_ln_g": "ln_g", "L0_attn_ln_b": "ln_b",
    "L0_attn_out_w": "out_w", "L0_attn_out_b": "out_b", "L0_ffn_Wr": "wr0", "L0_ffn_br": "br0",
    "L0_ffn_W1": "w1_0", "L0_ffn_b1": "b1_0", "L0_ffn_W2": "w2_0", "L0_ffn_b2": "b2_0",
    "L1_attn_Wq": "wq", "L1_attn_Wk": "wk", "L1_attn_Wo": "wo", "L1_ffn_gamma": "gamma", "L1_ffn_beta": "beta",
    "L1_ffn_Wr": "wr1", "L1_ffn_br": "br1", "L1_ffn_W1": "w1_1", "L1_ffn_b1": "b1_1", "L1_ffn_W2": "w2_1",
    "L1_ffn_b2": "b2_1",
}


def kernel(**inputs):
    import concourse.bacc as _bacc
    from concourse.bass_utils import run_bass_kernel_spmd as _run

    nc = _bacc.Bacc("TRN2", target_bir_lowering=False, num_devices=1)
    arrays, aps = {}, {}
    for name, short in INPUTS.items():
        a = np.ascontiguousarray(inputs[name])
        arrays[f"in_{short}"] = a
        aps[short] = nc.dram_tensor(f"in_{short}", a.shape, mybir.dt.from_np(a.dtype), kind="ExternalInput").ap()
    out = nc.dram_tensor("out_h", (B, T, D), F32, kind="ExternalOutput").ap()
    build(nc, aps, out)
    r = _run(nc, [arrays], core_ids=[0])
    return r.results[0]["out_h"]
```
